# Optimizing a Trainium2 kernel written in Bass

```python
import numpy as np
import jax
import jax.numpy as jnp

def _softmax(x, axis=-1):
    return jax.nn.softmax(x, axis=axis)

def _gelu(x):
    return jax.nn.gelu(x, approximate=True)

def _silu(x):
    return jax.nn.silu(x)

def _sigmoid(x):
    return jax.nn.sigmoid(x)

def _layernorm(x, axis=-1, eps=1e-05):
    m = jnp.mean(x, axis=axis, keepdims=True)
    v = jnp.var(x, axis=axis, keepdims=True)
    return (x - m) / jnp.sqrt(v + eps)

def _scatter_add(tgt, idx, src, axis=0):
    return tgt.at[idx].add(src)

def _segment_sum(src, seg, n):
    return jax.ops.segment_sum(src, seg, n)
kernel_name = 'mk_vit_tower_postln_d1_tok_img512_r4_fdce16'

def setup_inputs(seed: int=0):
    np.random.seed(seed)
    _w = jnp.asarray

    def _rec_inputs():
        import jax
        import jax.numpy as jnp
        _rk = jax.random.key(seed)
        x = 7.57192e-06 + 1.00007 * jax.random.normal(jax.random.fold_in(_rk, 1), (128, 3, 224, 224), jnp.float32)
        return x
    x = _rec_inputs()

    def _L0_tok_setup():
        import jax, jax.numpy as jnp
        import numpy as np
        D_MODEL = 128
        N_HEADS = 8
        D_HEAD = D_MODEL // N_HEADS
        D_FF = 344
        PATCH = 16
        IMG = 224
        N_PATCHES = (IMG // PATCH) ** 2
        T = N_PATCHES + 1
        B = 64
        EPS = 1e-06

        def rmsnorm(x, w):
            xf = x.astype(jnp.float32)
            norm = jax.lax.rsqrt(jnp.mean(xf * xf, axis=-1, keepdims=True) + EPS)
            return (xf * norm).astype(x.dtype) * w

        def _patch_embed(images, conv_w, conv_b, cls_token, pos_emb):
            y = jax.lax.conv_general_dilated(images, conv_w, window_strides=(PATCH, PATCH), padding='VALID', dimension_numbers=('NCHW', 'OIHW', 'NCHW'))
            y = y + conv_b[None, :, None, None]
            patches = y.reshape(y.shape[0], D_MODEL, -1).transpose(0, 2, 1)
            cls = jnp.broadcast_to(cls_token, (images.shape[0], 1, D_MODEL))
            return jnp.concatenate([cls, patches], axis=1) + pos_emb

        def _block(x, ln1w, wqkv, wo, ln2w, wg, wu, wd):
            Bx, Tx, C = x.shape
            h = rmsnorm(x, ln1w)
            qkv = (h @ wqkv.T).reshape(Bx, Tx, 3, N_HEADS, D_HEAD)
            q, k, v = jnp.moveaxis(qkv, 2, 0)
            scale = 1.0 / float(np.sqrt(D_HEAD))
            attn = jnp.einsum('bthd,bshd->bhts', q, k) * scale
            attn = jax.nn.softmax(attn, axis=-1)
            out = jnp.einsum('bhts,bshd->bthd', attn, v).reshape(Bx, Tx, C)
            x = x + out @ wo.T
            h2 = rmsnorm(x, ln2w)
            ff = jax.nn.silu(h2 @ wg.T) * (h2 @ wu.T) @ wd.T
            return x + ff
        key = jax.random.key(seed)
        ks = jax.random.split(key, 16)
        std = 0.02
        d = {'images': jax.random.normal(ks[0], (B, 3, IMG, IMG), dtype=jnp.float32), 'conv_w': jax.random.normal(ks[1], (D_MODEL, 3, PATCH, PATCH), dtype=jnp.float32) * std, 'conv_b': jnp.zeros((D_MODEL,), dtype=jnp.float32), 'cls_token': jax.random.normal(ks[2], (1, 1, D_MODEL), dtype=jnp.float32) * std, 'pos_emb': jax.random.normal(ks[3], (1, T, D_MODEL), dtype=jnp.float32) * std, 'ln_f': jnp.ones((D_MODEL,), dtype=jnp.float32)}
        ki = 4
        for i in range(2):
            d[f'ln1_{i}'] = jnp.ones((D_MODEL,), dtype=jnp.float32)
            d[f'qkv_{i}'] = jax.random.normal(ks[ki + 0], (3 * D_MODEL, D_MODEL), dtype=jnp.float32) * std
            d[f'wo_{i}'] = jax.random.normal(ks[ki + 1], (D_MODEL, D_MODEL), dtype=jnp.float32) * std
            d[f'ln2_{i}'] = jnp.ones((D_MODEL,), dtype=jnp.float32)
            d[f'gate_{i}'] = jax.random.normal(ks[ki + 2], (D_FF, D_MODEL), dtype=jnp.float32) * std
            d[f'up_{i}'] = jax.random.normal(ks[ki + 3], (D_FF, D_MODEL), dtype=jnp.float32) * std
            d[f'down_{i}'] = jax.random.normal(ks[ki + 4], (D_MODEL, D_FF), dtype=jnp.float32) * std
            ki += 5
        return d
    _L0_tok_all = _L0_tok_setup()
    _L0_tok_in = {k: v for k, v in _L0_tok_all.items() if k in ('conv_w', 'conv_b', 'cls_token', 'pos_emb', 'ln_f', 'ln1_0', 'qkv_0', 'wo_0', 'ln2_0', 'gate_0', 'up_0', 'down_0', 'ln1_1', 'qkv_1', 'wo_1', 'ln2_1', 'gate_1', 'up_1', 'down_1')}
    del _L0_tok_all

    def _L0_attn_setup():
        import jax, jax.numpy as jnp
        import numpy as np
        DM = 128
        DI = 128
        N = 16
        K = 4
        R = 32
        B_, L_ = (4, 256)

        def _block_params(keys, sfx):

            def rn(k, shape, s=0.02):
                return jax.random.normal(k, shape, jnp.float32) * s
            A = jnp.tile(jnp.arange(1, N + 1, dtype=jnp.float32), (DI, 1))
            return {f'W_in_{sfx}': rn(keys[0], (DM, 2 * DI)), f'W_conv_{sfx}': rn(keys[1], (DI, K), 0.1), f'b_conv_{sfx}': jnp.zeros((DI,), jnp.float32), f'W_xproj_{sfx}': rn(keys[2], (DI, R + 2 * N)), f'W_dt_{sfx}': rn(keys[3], (R, DI), 0.1), f'b_dt_{sfx}': rn(keys[4], (DI,), 0.1), f'A_log_{sfx}': jnp.log(A), f'D_{sfx}': jnp.ones((DI,), jnp.float32), f'W_out_{sfx}': rn(keys[5], (DI, DM))}

        def _mamba(x, W_in, W_conv, b_conv, W_xproj, W_dt, b_dt, A_log, D, W_out):
            B, L, _ = x.shape
            xz = x @ W_in
            xc, z = jnp.split(xz, 2, axis=-1)
            xp = jnp.pad(xc, ((0, 0), (K - 1, 0), (0, 0)))
            xconv = sum((xp[:, k:k + L, :] * W_conv[:, k] for k in range(K))) + b_conv
            xs = jax.nn.silu(xconv)
            dbc = xs @ W_xproj
            dt_in, Bm, Cm = (dbc[..., :R], dbc[..., R:R + N], dbc[..., R + N:])
            dt = jax.nn.softplus(dt_in @ W_dt + b_dt)
            A = -jnp.exp(A_log)
            dA = jnp.exp(dt[..., None] * A)
            dBx = dt[..., None] * Bm[:, :, None, :] * xs[..., None]

            def comb(e1, e2):
                a1, b1 = e1
                a2, b2 = e2
                return (a1 * a2, a2 * b1 + b2)
            _, h = jax.lax.associative_scan(comb, (dA, dBx), axis=1)
            y = jnp.einsum('blds,bls->bld', h, Cm) + D * xs
            y = y * jax.nn.silu(z)
            return y @ W_out
        key = jax.random.key(seed)
        ks = jax.random.split(key, 13)
        inp = {'x': jax.random.normal(ks[0], (B_, L_, DM), jnp.float32)}
        inp.update(_block_params(ks[1:7], 'f'))
        inp.update(_block_params(ks[7:13], 'b'))
        return inp
    _L0_attn_all = _L0_attn_setup()
    _L0_attn_in = {k: v for k, v in _L0_attn_all.items() if k in ('W_in_f', 'W_conv_f', 'b_conv_f', 'W_xproj_f', 'W_dt_f', 'b_dt_f', 'A_log_f', 'D_f', 'W_out_f', 'W_in_b', 'W_conv_b', 'b_conv_b', 'W_xproj_b', 'W_dt_b', 'b_dt_b', 'A_log_b', 'D_b', 'W_out_b')}
    del _L0_attn_all

    def _L0_ffn_setup():
        import jax, jax.numpy as jnp
        import numpy as np
        DIM = 128
        MOE_DIM = 64
        E = 64
        G = 8
        TOPK_G = 4
        K = 8
        SCALE = 2.5
        CAP = 256

        def _gate(x2, gate_w, gate_b):
            T = x2.shape[0]
            scores = jax.nn.sigmoid(x2 @ gate_w.T)
            s = (scores + gate_b).reshape(T, G, E // G)
            group_scores = jax.lax.top_k(s, 2)[0].sum(-1)
            top_groups = jax.lax.top_k(group_scores, TOPK_G)[1]
            gmask = jnp.zeros((T, G), bool).at[jnp.arange(T)[:, None], top_groups].set(True)
            s = jnp.where(gmask[..., None], s, -jnp.inf).reshape(T, E)
            idx = jax.lax.top_k(s, K)[1]
            w = jnp.take_along_axis(scores, idx, axis=1)
            w = w / w.sum(-1, keepdims=True) * SCALE
            return (w, idx)

        def _moe_forward(x, gate_w, gate_b, w1, w3, w2):
            shape = x.shape
            x2 = x.reshape(-1, DIM)
            T = x2.shape[0]
            w, idx = _gate(x2, gate_w, gate_b)
            flat_e = idx.reshape(-1)
            oh = (flat_e[:, None] == jnp.arange(E)[None, :]).astype(jnp.int32)
            pos = (jnp.cumsum(oh, axis=0) * oh).sum(-1) - 1
            x_rep = jnp.repeat(x2, K, axis=0)
            xb = jnp.zeros((E, CAP, DIM), x2.dtype).at[flat_e, pos].set(x_rep, mode='drop')
            h = jax.nn.silu(jnp.einsum('ecd,edm->ecm', xb, w1)) * jnp.einsum('ecd,edm->ecm', xb, w3)
            yb = jnp.einsum('ecm,emd->ecd', h, w2)
            y = yb.at[flat_e, pos].get(mode='fill', fill_value=0.0) * w.reshape(-1)[:, None]
            return y.reshape(T, K, DIM).sum(1).reshape(shape)
        key = jax.random.key(seed)
        ks = jax.random.split(key, 6)
        x = jax.random.normal(ks[0], (4, 128, DIM), jnp.float32)
        gate_w = jax.random.normal(ks[1], (E, DIM), jnp.float32) / np.sqrt(DIM).astype(np.float32)
        gate_b = jax.random.normal(ks[2], (E,), jnp.float32) * 0.01
        w1 = jax.random.normal(ks[3], (E, DIM, MOE_DIM), jnp.float32) / np.sqrt(DIM).astype(np.float32)
        w3 = jax.random.normal(ks[4], (E, DIM, MOE_DIM), jnp.float32) / np.sqrt(DIM).astype(np.float32)
        w2 = jax.random.normal(ks[5], (E, MOE_DIM, DIM), jnp.float32) / np.sqrt(MOE_DIM).astype(np.float32)
        return {'x': x, 'gate_w': gate_w, 'gate_b': gate_b, 'w1': w1, 'w3': w3, 'w2': w2}
    _L0_ffn_all = _L0_ffn_setup()
    _L0_ffn_in = {k: v for k, v in _L0_ffn_all.items() if k in ('gate_w', 'gate_b', 'w1', 'w3', 'w2')}
    del _L0_ffn_all
    return {'x': x, 'L0_tok_conv_w': _L0_tok_in['conv_w'], 'L0_tok_conv_b': _L0_tok_in['conv_b'], 'L0_tok_cls_token': _L0_tok_in['cls_token'], 'L0_tok_pos_emb': _L0_tok_in['pos_emb'], 'L0_tok_ln_f': _L0_tok_in['ln_f'], 'L0_tok_ln1_0': _L0_tok_in['ln1_0'], 'L0_tok_qkv_0': _L0_tok_in['qkv_0'], 'L0_tok_wo_0': _L0_tok_in['wo_0'], 'L0_tok_ln2_0': _L0_tok_in['ln2_0'], 'L0_tok_gate_0': _L0_tok_in['gate_0'], 'L0_tok_up_0': _L0_tok_in['up_0'], 'L0_tok_down_0': _L0_tok_in['down_0'], 'L0_tok_ln1_1': _L0_tok_in['ln1_1'], 'L0_tok_qkv_1': _L0_tok_in['qkv_1'], 'L0_tok_wo_1': _L0_tok_in['wo_1'], 'L0_tok_ln2_1': _L0_tok_in['ln2_1'], 'L0_tok_gate_1': _L0_tok_in['gate_1'], 'L0_tok_up_1': _L0_tok_in['up_1'], 'L0_tok_down_1': _L0_tok_in['down_1'], 'L0_attn_W_in_f': _L0_attn_in['W_in_f'], 'L0_attn_W_conv_f': _L0_attn_in['W_conv_f'], 'L0_attn_b_conv_f': _L0_attn_in['b_conv_f'], 'L0_attn_W_xproj_f': _L0_attn_in['W_xproj_f'], 'L0_attn_W_dt_f': _L0_attn_in['W_dt_f'], 'L0_attn_b_dt_f': _L0_attn_in['b_dt_f'], 'L0_attn_A_log_f': _L0_attn_in['A_log_f'], 'L0_attn_D_f': _L0_attn_in['D_f'], 'L0_attn_W_out_f': _L0_attn_in['W_out_f'], 'L0_attn_W_in_b': _L0_attn_in['W_in_b'], 'L0_attn_W_conv_b': _L0_attn_in['W_conv_b'], 'L0_attn_b_conv_b': _L0_attn_in['b_conv_b'], 'L0_attn_W_xproj_b': _L0_attn_in['W_xproj_b'], 'L0_attn_W_dt_b': _L0_attn_in['W_dt_b'], 'L0_attn_b_dt_b': _L0_attn_in['b_dt_b'], 'L0_attn_A_log_b': _L0_attn_in['A_log_b'], 'L0_attn_D_b': _L0_attn_in['D_b'], 'L0_attn_W_out_b': _L0_attn_in['W_out_b'], 'L0_ffn_gate_w': _L0_ffn_in['gate_w'], 'L0_ffn_gate_b': _L0_ffn_in['gate_b'], 'L0_ffn_w1': _L0_ffn_in['w1'], 'L0_ffn_w3': _L0_ffn_in['w3'], 'L0_ffn_w2': _L0_ffn_in['w2']}

def reference(x, L0_tok_conv_w, L0_tok_conv_b, L0_tok_cls_token, L0_tok_pos_emb, L0_tok_ln_f, L0_tok_ln1_0, L0_tok_qkv_0, L0_tok_wo_0, L0_tok_ln2_0, L0_tok_gate_0, L0_tok_up_0, L0_tok_down_0, L0_tok_ln1_1, L0_tok_qkv_1, L0_tok_wo_1, L0_tok_ln2_1, L0_tok_gate_1, L0_tok_up_1, L0_tok_down_1, L0_attn_W_in_f, L0_attn_W_conv_f, L0_attn_b_conv_f, L0_attn_W_xproj_f, L0_attn_W_dt_f, L0_attn_b_dt_f, L0_attn_A_log_f, L0_attn_D_f, L0_attn_W_out_f, L0_attn_W_in_b, L0_attn_W_conv_b, L0_attn_b_conv_b, L0_attn_W_xproj_b, L0_attn_W_dt_b, L0_attn_b_dt_b, L0_attn_A_log_b, L0_attn_D_b, L0_attn_W_out_b, L0_ffn_gate_w, L0_ffn_gate_b, L0_ffn_w1, L0_ffn_w3, L0_ffn_w2):
    import jax
    import jax.numpy as jnp

    def _L0_tok_ref(images, conv_w, conv_b, cls_token, pos_emb, ln_f, ln1_0, qkv_0, wo_0, ln2_0, gate_0, up_0, down_0, ln1_1, qkv_1, wo_1, ln2_1, gate_1, up_1, down_1):
        import jax, jax.numpy as jnp
        import numpy as np
        D_MODEL = 128
        N_HEADS = 8
        D_HEAD = D_MODEL // N_HEADS
        D_FF = 344
        PATCH = 16
        IMG = 224
        N_PATCHES = (IMG // PATCH) ** 2
        T = N_PATCHES + 1
        B = 64
        EPS = 1e-06

        def rmsnorm(x, w):
            xf = x.astype(jnp.float32)
            norm = jax.lax.rsqrt(jnp.mean(xf * xf, axis=-1, keepdims=True) + EPS)
            return (xf * norm).astype(x.dtype) * w

        def _patch_embed(images, conv_w, conv_b, cls_token, pos_emb):
            y = jax.lax.conv_general_dilated(images, conv_w, window_strides=(PATCH, PATCH), padding='VALID', dimension_numbers=('NCHW', 'OIHW', 'NCHW'))
            y = y + conv_b[None, :, None, None]
            patches = y.reshape(y.shape[0], D_MODEL, -1).transpose(0, 2, 1)
            cls = jnp.broadcast_to(cls_token, (images.shape[0], 1, D_MODEL))
            return jnp.concatenate([cls, patches], axis=1) + pos_emb

        def _block(x, ln1w, wqkv, wo, ln2w, wg, wu, wd):
            Bx, Tx, C = x.shape
            h = rmsnorm(x, ln1w)
            qkv = (h @ wqkv.T).reshape(Bx, Tx, 3, N_HEADS, D_HEAD)
            q, k, v = jnp.moveaxis(qkv, 2, 0)
            scale = 1.0 / float(np.sqrt(D_HEAD))
            attn = jnp.einsum('bthd,bshd->bhts', q, k) * scale
            attn = jax.nn.softmax(attn, axis=-1)
            out = jnp.einsum('bhts,bshd->bthd', attn, v).reshape(Bx, Tx, C)
            x = x + out @ wo.T
            h2 = rmsnorm(x, ln2w)
            ff = jax.nn.silu(h2 @ wg.T) * (h2 @ wu.T) @ wd.T
            return x + ff
        x = _patch_embed(images, conv_w, conv_b, cls_token, pos_emb)
        x = _block(x, ln1_0, qkv_0, wo_0, ln2_0, gate_0, up_0, down_0)
        x = _block(x, ln1_1, qkv_1, wo_1, ln2_1, gate_1, up_1, down_1)
        return rmsnorm(x, ln_f)

    def _L0_attn_ref(x, W_in_f, W_conv_f, b_conv_f, W_xproj_f, W_dt_f, b_dt_f, A_log_f, D_f, W_out_f, W_in_b, W_conv_b, b_conv_b, W_xproj_b, W_dt_b, b_dt_b, A_log_b, D_b, W_out_b):
        import jax, jax.numpy as jnp
        import numpy as np
        DM = 128
        DI = 128
        N = 16
        K = 4
        R = 32
        B_, L_ = (4, 256)

        def _block_params(keys, sfx):

            def rn(k, shape, s=0.02):
                return jax.random.normal(k, shape, jnp.float32) * s
            A = jnp.tile(jnp.arange(1, N + 1, dtype=jnp.float32), (DI, 1))
            return {f'W_in_{sfx}': rn(keys[0], (DM, 2 * DI)), f'W_conv_{sfx}': rn(keys[1], (DI, K), 0.1), f'b_conv_{sfx}': jnp.zeros((DI,), jnp.float32), f'W_xproj_{sfx}': rn(keys[2], (DI, R + 2 * N)), f'W_dt_{sfx}': rn(keys[3], (R, DI), 0.1), f'b_dt_{sfx}': rn(keys[4], (DI,), 0.1), f'A_log_{sfx}': jnp.log(A), f'D_{sfx}': jnp.ones((DI,), jnp.float32), f'W_out_{sfx}': rn(keys[5], (DI, DM))}

        def _mamba(x, W_in, W_conv, b_conv, W_xproj, W_dt, b_dt, A_log, D, W_out):
            B, L, _ = x.shape
            xz = x @ W_in
            xc, z = jnp.split(xz, 2, axis=-1)
            xp = jnp.pad(xc, ((0, 0), (K - 1, 0), (0, 0)))
            xconv = sum((xp[:, k:k + L, :] * W_conv[:, k] for k in range(K))) + b_conv
            xs = jax.nn.silu(xconv)
            dbc = xs @ W_xproj
            dt_in, Bm, Cm = (dbc[..., :R], dbc[..., R:R + N], dbc[..., R + N:])
            dt = jax.nn.softplus(dt_in @ W_dt + b_dt)
            A = -jnp.exp(A_log)
            dA = jnp.exp(dt[..., None] * A)
            dBx = dt[..., None] * Bm[:, :, None, :] * xs[..., None]

            def comb(e1, e2):
                a1, b1 = e1
                a2, b2 = e2
                return (a1 * a2, a2 * b1 + b2)
            _, h = jax.lax.associative_scan(comb, (dA, dBx), axis=1)
            y = jnp.einsum('blds,bls->bld', h, Cm) + D * xs
            y = y * jax.nn.silu(z)
            return y @ W_out
        out_f = _mamba(x, W_in_f, W_conv_f, b_conv_f, W_xproj_f, W_dt_f, b_dt_f, A_log_f, D_f, W_out_f)
        out_b = jnp.flip(_mamba(jnp.flip(x, 1), W_in_b, W_conv_b, b_conv_b, W_xproj_b, W_dt_b, b_dt_b, A_log_b, D_b, W_out_b), 1)
        return out_f + out_b

    def _L0_ffn_ref(x, gate_w, gate_b, w1, w3, w2):
        import jax, jax.numpy as jnp
        import numpy as np
        DIM = 128
        MOE_DIM = 64
        E = 64
        G = 8
        TOPK_G = 4
        K = 8
        SCALE = 2.5
        CAP = 256

        def _gate(x2, gate_w, gate_b):
            T = x2.shape[0]
            scores = jax.nn.sigmoid(x2 @ gate_w.T)
            s = (scores + gate_b).reshape(T, G, E // G)
            group_scores = jax.lax.top_k(s, 2)[0].sum(-1)
            top_groups = jax.lax.top_k(group_scores, TOPK_G)[1]
            gmask = jnp.zeros((T, G), bool).at[jnp.arange(T)[:, None], top_groups].set(True)
            s = jnp.where(gmask[..., None], s, -jnp.inf).reshape(T, E)
            idx = jax.lax.top_k(s, K)[1]
            w = jnp.take_along_axis(scores, idx, axis=1)
            w = w / w.sum(-1, keepdims=True) * SCALE
            return (w, idx)

        def _moe_forward(x, gate_w, gate_b, w1, w3, w2):
            shape = x.shape
            x2 = x.reshape(-1, DIM)
            T = x2.shape[0]
            w, idx = _gate(x2, gate_w, gate_b)
            flat_e = idx.reshape(-1)
            oh = (flat_e[:, None] == jnp.arange(E)[None, :]).astype(jnp.int32)
            pos = (jnp.cumsum(oh, axis=0) * oh).sum(-1) - 1
            x_rep = jnp.repeat(x2, K, axis=0)
            xb = jnp.zeros((E, CAP, DIM), x2.dtype).at[flat_e, pos].set(x_rep, mode='drop')
            h = jax.nn.silu(jnp.einsum('ecd,edm->ecm', xb, w1)) * jnp.einsum('ecd,edm->ecm', xb, w3)
            yb = jnp.einsum('ecm,emd->ecd', h, w2)
            y = yb.at[flat_e, pos].get(mode='fill', fill_value=0.0) * w.reshape(-1)[:, None]
            return y.reshape(T, K, DIM).sum(1).reshape(shape)
        return _moe_forward(x, gate_w, gate_b, w1, w3, w2)
    h = _L0_tok_ref(x, L0_tok_conv_w, L0_tok_conv_b, L0_tok_cls_token, L0_tok_pos_emb, L0_tok_ln_f, L0_tok_ln1_0, L0_tok_qkv_0, L0_tok_wo_0, L0_tok_ln2_0, L0_tok_gate_0, L0_tok_up_0, L0_tok_down_0, L0_tok_ln1_1, L0_tok_qkv_1, L0_tok_wo_1, L0_tok_ln2_1, L0_tok_gate_1, L0_tok_up_1, L0_tok_down_1)
    h = _layernorm(h + _L0_attn_ref(h, L0_attn_W_in_f, L0_attn_W_conv_f, L0_attn_b_conv_f, L0_attn_W_xproj_f, L0_attn_W_dt_f, L0_attn_b_dt_f, L0_attn_A_log_f, L0_attn_D_f, L0_attn_W_out_f, L0_attn_W_in_b, L0_attn_W_conv_b, L0_attn_b_conv_b, L0_attn_W_xproj_b, L0_attn_W_dt_b, L0_attn_b_dt_b, L0_attn_A_log_b, L0_attn_D_b, L0_attn_W_out_b), axis=-1)
    h = _layernorm(h + _L0_ffn_ref(h, L0_ffn_gate_w, L0_ffn_gate_b, L0_ffn_w1, L0_ffn_w3, L0_ffn_w2), axis=-1)
    return h

_drawn_inputs = setup_inputs


def setup_inputs(seed=0):
    import zlib

    import numpy as np

    out = dict(_drawn_inputs(seed))
    spreads = {'L0_tok_conv_b': (0.0, 0.1),
     'L0_tok_ln_f': (1.0, 0.2),
     'L0_tok_ln1_0': (1.0, 0.6),
     'L0_tok_ln2_0': (1.0, 0.6),
     'L0_tok_ln1_1': (1.0, 0.6),
     'L0_tok_ln2_1': (1.0, 0.6),
     'L0_attn_b_conv_f': (0.0, 0.8),
     'L0_attn_D_f': (1.0, 0.6),
     'L0_attn_b_conv_b': (0.0, 0.8),
     'L0_attn_D_b': (1.0, 0.6)}
    factors = {'L0_attn_W_in_f': 6.461,
     'L0_attn_W_conv_f': 8.0,
     'L0_attn_W_xproj_f': 8.0,
     'L0_attn_W_dt_f': 8.0,
     'L0_attn_b_dt_f': 8.0,
     'L0_attn_A_log_f': 8.0,
     'L0_attn_W_out_f': 7.184,
     'L0_attn_W_in_b': 7.104,
     'L0_attn_W_conv_b': 8.0,
     'L0_attn_W_xproj_b': 8.0,
     'L0_attn_W_dt_b': 8.0,
     'L0_attn_b_dt_b': 8.0,
     'L0_attn_A_log_b': 8.0,
     'L0_attn_W_out_b': 6.71}
    for name, (base, spread) in spreads.items():
        noise = np.random.default_rng([zlib.crc32(name.encode()), seed]).standard_normal(out[name].shape)
        drawn = base * np.exp(spread * noise) if base else spread * noise
        out[name] = jnp.asarray(drawn.astype(out[name].dtype))
    for name, factor in factors.items():
        out[name] = (out[name] * factor).astype(out[name].dtype)
    return out
```

```python
import concourse.bass as bass
from concourse import mybir
from contextlib import ExitStack

DVE_PER = 50
D = 128
B = 128
PATCH, IMG, CH = 16, 224, 3
NP = (IMG // PATCH) ** 2
T = NP + 1
G = 2
N = G * T
STEPS = B // G
KP = CH * PATCH * PATCH // 128
HEADS, HD = 8, 16
FF = 344
FC = 3
FW = -(-FF // FC)
NS = 16
DTR = 32
TAPS = 4
XW = T + TAPS - 1
E, GR, TOPG, TOPK, CAP, MD = 64, 8, 4, 8, 256, 64
ROUTE_SCALE = 2.5
CT = 99
NC4 = 4
PADN = NC4 * CT
ROW = D + E
TOK = B * T
SLOTS = E * CAP
QC = [(0, 128), (128, T - 128)]
NOSLOT = 1 << 20
LOG1P_SERIES = 2.0 ** -8
BIG = 1e30
EPS_RMS, EPS_LN = 1e-6, 1e-5

def _cols(widths):
    at, out = 0, {}
    for name, w in widths:
        out[name] = (at, w)
        at += w
    return out, at


W_COLS, W_N = _cols(
    [("conv", KP * D)]
    + [(f"{n}{l}", w) for l in range(2) for n, w in (
        ("qe", D), ("qo", D), ("ke", D), ("ko", D), ("v", D), ("woe", D), ("woo", D),
        ("gate", FC * FW), ("up", FC * FW), ("down", FC * D))]
    + [(f"{n}{d}", w) for d in "fb" for n, w in (
        ("win", 2 * D), ("xdt", DTR), ("xbc", 3 * 2 * NS), ("wdt", D), ("wout", D))]
    + [("route", E)])
V_COLS, V_N = _cols(
    [("convb", 1), ("cls", 1), ("pos", T), ("lnf", 1)]
    + [(f"{n}{l}", 1) for l in range(2) for n in ("ln1", "ln2")]
    + [(f"{n}{d}", w) for d in "fb" for n, w in (
        ("taps", TAPS), ("bconv", 1), ("bdt", 1), ("alog", NS), ("dskip", 1))])
C_COLS, C_N = _cols([("ident", D), ("negident", D), ("mean", D), ("dsel", D), ("before", D), ("ones", D),
                     ("slot1", E), ("valid", NC4), ("tok0", NC4), ("part1", 1), ("part2", 1),
                     ("kone", 1), ("groupbefore", GR * GR), ("unused", (SLOTS + 128) // 128)])


def vit_mamba_moe(nc, patches, weights, vectors, consts, bcsel_d, gate_b, w13, w2, out):
    f32, bf16, i32 = mybir.dt.float32, mybir.dt.bfloat16, mybir.dt.int32
    ACT = mybir.ActivationFunctionType
    ALU = mybir.AluOpType
    AX = mybir.AxisListType.X

    rows_d = nc.dram_tensor("rows_scratch", (TOK + 128, ROW), f32, kind="Internal").ap()
    sum_d = nc.dram_tensor("sum_scratch", (TOK + 128, D), f32, kind="Internal").ap()
    slot_d = nc.dram_tensor("slot_scratch", (SLOTS + 128, 1), i32, kind="Internal").ap()

    ctx = ExitStack()
    with ctx:
        def sb(name, shape, dt=f32):
            return ctx.enter_context(nc.sbuf_tensor(name, shape, dt))

        def sem(name):
            return ctx.enter_context(nc.semaphore(name))

        wts = sb("wts", [128, W_N])
        vec = sb("vec", [128, V_N])
        cst = sb("cst", [128, C_N])

        def w(name, a=0, b=None):
            at, n = W_COLS[name]
            return wts[:, at + a:at + (n if b is None else b)]

        def v(name, a=0, b=None):
            at, n = V_COLS[name]
            return vec[:, at + a:at + (n if b is None else b)]

        def c(name, a=0, b=None):
            at, n = C_COLS[name]
            return cst[:, at + a:at + (n if b is None else b)]

        bcsel = sb("bcsel_h", [96, 2 * NS, D], bf16)
        before_h = sb("before_h", [128, D], bf16)
        ones_h = sb("ones_h", [128, D], bf16)
        posb = sb("posb", [128, T])
        cls0 = sb("cls0", [128, 1])
        aneg = sb("aneg", [128, 2, NS])
        dskip = sb("dskip", [128, 2, D])
        gateb = sb("gateb", [128, E])
        epsr = sb("epsr", [128, 2])

        pat = sb("pat", [128, KP, G * NP])
        X = sb("X", [128, G, T])
        sq = sb("sq", [128, N])
        rs = sb("rs", [128, N])
        Hn = sb("Hn", [128, G, T])
        Q = sb("Q", [128, 2, G, T])
        K = sb("K", [128, 2, G, T])
        V = sb("V", [128, G * 2, HEADS, 32])
        M = sb("M", [128, 2, D])
        P = sb("P", [128, 2, 4, 2 * T])
        O = sb("O", [128, G, 2, T])
        R = sb("R", [128, G, 2 * T])
        EF = sb("EF", [128, FC, N])
        H = sb("H", [128, N])
        Hr = sb("Hr", [128, N])
        XC = sb("XC", [128, G, XW])
        XZ = sb("XZ", [128, 2, N])
        SG = sb("SG", [128, 2, N])
        dtin = sb("dtin", [DTR, N])
        hi = sb("hi", [96, N], bf16)
        res = sb("res", [96, N])
        mid = sb("mid", [96, N], bf16)
        bc = sb("bc", [96, N], bf16)
        dt_ = sb("dt_", [128, N])
        sp = sb("sp", [128, N])
        spl = sb("spl", [128, N])
        u = sb("u", [128, N])
        small = sb("small", [128, N], mybir.dt.uint32)
        dA = sb("dA", [128, NS, N])
        hs = sb("hs", [128, NS, N])
        YS = sb("YS", [128, 2, N])
        Z = sb("Z", [128, N])
        h2 = sb("h2", [128, PADN])
        HW = sb("HW", [CT, NC4, ROW])
        score = sb("score", [CT, NC4, E])
        t1 = sb("t1", [CT, NC4, E])
        ext = sb("ext", [CT, NC4 * GR, 12])
        pairs = sb("pairs", [CT, NC4 * GR, 4, 8])
        gs = sb("gs", [CT, NC4, GR])
        cmp1 = sb("cmp1", [CT, NC4, GR, GR])
        cmp2 = sb("cmp2", [CT, NC4, GR, GR])
        rank = sb("rank", [CT, NC4 * GR])
        masked = sb("masked", [CT, NC4, E])
        top8 = sb("top8", [CT, NC4, 8])
        rest = sb("rest", [CT, NC4, E])
        sel = sb("sel", [CT, NC4, E])
        selh = sb("selh", [CT, NC4, E], bf16)
        wsum = sb("wsum", [CT, NC4])
        winv = sb("winv", [CT, NC4])
        pos = sb("pos", [CT, NC4, E])
        base = sb("base", [CT, E])
        slotf = sb("slotf", [CT, NC4, 8])
        noslot = sb("noslot", [CT, NC4, 8])
        sloti = sb("sloti", [CT, NC4 * 8], i32)
        tokf = sb("tokf", [CT, NC4])
        toki = sb("toki", [CT, NC4], i32)
        trashi = sb("trashi", [128, (SLOTS + 128) // 128], i32)

        psS = ctx.enter_context(nc.psum_tensor("psS", [128, 4, 512], f32))
        psG = ctx.enter_context(nc.psum_tensor("psG", [128, 512], f32))
        psA = ctx.enter_context(nc.psum_tensor("psA", [128, 512], f32))
        psB = ctx.enter_context(nc.psum_tensor("psB", [128, 512], f32))
        psY = ctx.enter_context(nc.psum_tensor("psY", [128, 512], f32))
        AB = [psA, psB]

        names = ("loaded patches_loaded consts_ready act_step dve_step pool_ready x_ready sq_ready ms_done rs_ready "
                 "hn_ready q_done k_done v_done q_ready k_ready v_ready s_done max_done place_done qm_ready "
                 "st_done p_ready o_done o_ready den_done inv_ready on_ready wo_done g_done ge_ready ge1_ready "
                 "gsig_ready gs_ready u_done ff_ready down_done conv_done h_ready xz_done xc_ready xconv_ready "
                 "sge_ready sg1_ready sgr_ready xs_ready bc_done dtin_ready hi_ready res_ready mid_ready bcs_ready "
                 "dtp_done sp_ready dt_ready da_ready bb_done mul_done y_done ys_ready m_done z_ready "
                 "mean_done zc_ready sq2_ready var_done rs2_ready h2_ready lg_done ht_done ht_ready gl_ready "
                 "gm_ready score_ready hw_ready sel_ready pos_done slot_ready rows_stored sent_a sent_b init_stored "
                 "mload gathered xt_done xt_ready e13_done e_exp e_one e_sig e_act e2_done e_out added fin_loaded fin_ready fin_stored midx e_free slots_free trash_ready e_mul fin_mv fin_rs fin_step abs_ready pool_waited dve_waited spe_ready").split()
        S = {n: sem(n) for n in names}
        (loaded, patches_loaded, consts_ready, act_step, dve_step, pool_ready, x_ready, sq_ready, ms_done, rs_ready,
         hn_ready, q_done, k_done, v_done, q_ready, k_ready, v_ready, s_done, max_done, place_done, qm_ready,
         st_done, p_ready, o_done, o_ready, den_done, inv_ready, on_ready, wo_done, g_done, ge_ready, ge1_ready,
         gsig_ready, gs_ready, u_done, ff_ready, down_done, conv_done, h_ready, xz_done, xc_ready, xconv_ready,
         sge_ready, sg1_ready, sgr_ready, xs_ready, bc_done, dtin_ready, hi_ready, res_ready, mid_ready, bcs_ready,
         dtp_done, sp_ready, dt_ready, da_ready, bb_done, mul_done, y_done, ys_ready, m_done, z_ready,
         mean_done, zc_ready, sq2_ready, var_done, rs2_ready, h2_ready, lg_done, ht_done, ht_ready, gl_ready,
         gm_ready, score_ready, hw_ready, sel_ready, pos_done, slot_ready, rows_stored, sent_a, sent_b, init_stored,
         mload, gathered, xt_done, xt_ready, e13_done, e_exp, e_one, e_sig, e_act, e2_done, e_out, added, fin_loaded,
         fin_ready, fin_stored, midx, e_free, slots_free, trash_ready, e_mul, fin_mv, fin_rs, fin_step, abs_ready, pool_waited, dve_waited, spe_ready) = (S[n] for n in names)

        eidx = sb("eidx", [128, 2], i32)
        ex = dA[:, 0:1, 0:2 * ROW].rearrange("p a (c r) -> p (a c) r", c=2)
        exT = dA[:, 2, 0:CAP]
        ew = dA[:, 4, 0:3 * 128]
        ea = dA[0:MD, 6, 0:CAP]
        eo = dA[:, 8, 0:2 * D].rearrange("p (c r) -> p c r", c=2)
        FT = 8
        fin = hs[:, 0:3, :].rearrange("p a b -> p (a b)")[:, 0:FT * D].rearrange("p (t d) -> p t d", d=D)
        fst = hs[:, 8, 0:6 * FT].rearrange("p (t s) -> p t s", s=6)
        fmv = hs[:, 9, 0:2 * FT].rearrange("p (t s) -> p t s", s=2)
        frs = hs[:, 10, 0:FT]

        block = ctx.enter_context(nc.Block())

        LOADS = 6
        FINAL = [(t, min(FT, T - t)) for t in range(0, T, FT)]

        def store_rows(sp_, i):
            sp_.wait_ge(ht_ready, i + 1)
            sp_.wait_ge(hw_ready, i + 1)
            for lo, nch, n in ((0, NC4 - 1, CT), (NC4 - 1, 1, N - (NC4 - 1) * CT)):
                for dram, wid in ((rows_d, ROW), (sum_d, D)):
                    dst = dram[bass.ds(i * N + lo * CT, nch * n), :].rearrange("(c p) r -> p c r", p=n)
                    sp_.dma_start(dst, HW[0:n, lo:lo + nch, 0:wid]).then_inc(rows_stored, 16)

        @block.sync
        def _(sp_):
            sp_.dma_start(wts[:, :], weights).then_inc(loaded, 16)
            sp_.dma_start(vec[:, :], vectors).then_inc(loaded, 16)
            sp_.dma_start(cst[:, :], consts).then_inc(loaded, 16)
            sp_.dma_start(dA[0:96, :, :].rearrange("p a b -> p (a b)")[:, 0:2 * NS * D], bcsel_d).then_inc(loaded, 16)
            sp_.dma_start(gateb[:, :], gate_b.rearrange("(a e) -> a e", a=1).to_broadcast([128, E])).then_inc(loaded, 16)
            sp_.dma_start(pat[:, :, :], patches[0]).then_inc(patches_loaded, 16)
            sp_.wait_ge(pool_ready, 9)
            sp_.wait_ge(trash_ready, 1)
            sp_.dma_start(rows_d[TOK:TOK + 128, :], hs[:, 0, 0:ROW]).then_inc(rows_stored, 16)
            sp_.dma_start(sum_d[TOK:TOK + 128, :], hs[:, 0, 0:D]).then_inc(rows_stored, 16)
            sp_.dma_start(slot_d.rearrange("(p a) o -> p (a o)", p=128), trashi[:, :]).then_inc(init_stored, 16)
            with sp_.Fori(0, STEPS - 1) as i:
                sp_.wait_ge(conv_done, i + 1)
                sp_.dma_start(pat[:, :, :], patches[bass.ds(i + 1, 1)].rearrange("o p k n -> (o p) k n")).then_inc(patches_loaded, 16)
                store_rows(sp_, i)
            store_rows(sp_, STEPS - 1)
            with sp_.Fori(0, E) as e:
                sp_.wait_ge(e_free, e + 1)
                sp_.dma_start(eidx[:, :], slot_d[bass.ds(e * CAP, CAP), :].rearrange("(p c) o -> p (c o)", p=128)).then_inc(midx, 16)
                sp_.dma_start(ew[:, 0:D], w13[bass.ds(e, 1)].rearrange("o p n -> (o p) n")).then_inc(mload, 16)
                sp_.dma_start(ew[0:MD, D:2 * D], w2[bass.ds(e, 1)].rearrange("o p n -> (o p) n")).then_inc(mload, 16)
            sp_.wait_ge(e_free, E + 1)
            r3 = sum_d[0:TOK, :].rearrange("(p t) d -> p t d", p=B)
            for n, (t, m) in enumerate(FINAL):
                if n:
                    sp_.wait_ge(fin_stored, 16 * n)
                sp_.dma_start(fin[0:B, 0:m, :], r3[:, t:t + m, :]).then_inc(fin_loaded, 16)
                sp_.wait_ge(fin_ready, n + 1)
                sp_.dma_start(out[:, t:t + m, :], fin[0:B, 0:m, :]).then_inc(fin_stored, 16)
            sp_.wait_ge(fin_stored, 16 * len(FINAL))

        @block.gpsimd
        def _(pool):
            nc.gpsimd.memset(V[:, :, :, :], 0.0).then_inc(pool_ready, 1)
            pool.wait_ge(pool_ready, 1)
            nc.gpsimd.memset(V[:, :, :, HD:HD + 1], 1.0).then_inc(pool_ready, 1)
            nc.gpsimd.memset(M[:, :, :], 0.0).then_inc(pool_ready, 1)
            nc.gpsimd.memset(XC[:, :, :], 0.0).then_inc(pool_ready, 1)
            nc.gpsimd.memset(h2[:, :], 0.0).then_inc(pool_ready, 1)
            nc.gpsimd.memset(hs[:, 0, 0:ROW], 0.0).then_inc(pool_ready, 1)
            nc.gpsimd.memset(epsr[:, 0:1], EPS_RMS).then_inc(pool_ready, 1)
            nc.gpsimd.memset(epsr[:, 1:2], EPS_LN).then_inc(pool_ready, 1)
            nc.gpsimd.memset(base[:, :], 0.0).then_inc(pool_ready, 1)
            pool.wait_ge(init_stored, 16)
            pool.sem_inc(slots_free, 1)
            with pool.Fori(0, STEPS) as i:
                pool.wait_ge(slot_ready, i + 1)
                pool.sem_inc(pool_waited, 1)
                for j in range(NC4 * 8):
                    nc.gpsimd.indirect_dma_start(
                        out=slot_d[:, :], out_offset=bass.IndirectOffsetOnAxis(ap=sloti[:, j:j + 1], axis=0),
                        in_=toki[:, j // 8:j // 8 + 1], in_offset=None,
                        bounds_check=SLOTS - 1, oob_is_err=False).then_inc(sent_a if j % 2 else sent_b, 16)
                pool.wait_ge(sent_a, i * 256 + 256)
                pool.wait_ge(sent_b, i * 256 + 256)
                pool.sem_inc(slots_free, 1)
            pool.wait_ge(rows_stored, 32 + 64 * STEPS)
            pool.sem_inc(e_free, 1)
            with pool.Fori(0, E) as e:
                pool.wait_ge(midx, e * 16 + 16)
                pool.sem_inc(pool_waited, 1)
                for k in range(2):
                    nc.gpsimd.indirect_dma_start(
                        out=ex[:, k, :], out_offset=None, in_=rows_d[:, :],
                        in_offset=bass.IndirectOffsetOnAxis(ap=eidx[:, k:k + 1], axis=0)).then_inc(gathered, 16)
                pool.wait_ge(e_out, e + 1)
                pool.sem_inc(pool_waited, 1)
                for k in range(2):
                    nc.gpsimd.indirect_dma_start(
                        out=sum_d[:, :], out_offset=bass.IndirectOffsetOnAxis(ap=eidx[:, k:k + 1], axis=0),
                        in_=eo[:, k, :], in_offset=None, compute_op=ALU.add).then_inc(added, 16)
                    pool.wait_ge(added, e * 32 + 16 * (k + 1))
                    pool.sem_inc(pool_waited, 1)
                pool.sem_inc(e_free, 1)

        @block.scalar
        def _(act):
            act.preload_act_table_set("natural_log_exp_and_others")
            step = [0]

            def link(ins, i, per):
                step[0] += 1
                ins.then_inc(act_step, 1)
                act.wait_ge(act_step, i * per + step[0])

            act.wait_ge(loaded, 16 * 5)
            act.wait_ge(pool_ready, 9)
            link(nc.scalar.activation(bcsel[:, :, :], dA[0:96, :, :].rearrange("p a b -> p (a b)")[:, 0:2 * NS * D].rearrange("p (n d) -> p n d", d=D), ACT.Copy), 0, 0)
            link(nc.scalar.activation(before_h[:, :], c("before"), ACT.Copy), 0, 0)
            link(nc.scalar.activation(ones_h[:, :], c("ones"), ACT.Copy), 0, 0)
            for n, d in enumerate("fb"):
                link(nc.scalar.activation(aneg[:, n, :], v(f"alog{d}"), ACT.Exp), 0, 0)
            link(nc.scalar.activation(aneg[:, :, :], aneg[:, :, :], ACT.Copy, scale=-1.0), 0, 0)
            nc.scalar.activation(epsr[:, :], epsr[:, :], ACT.Copy).then_inc(consts_ready, 1)
            first = step[0]
            PER = 14

            def norm(i, m):
                act.wait_ge(x_ready, i * 5 + 2 + m)
                nc.scalar.activation(sq[:, :], X[:, :, :].rearrange("p g t -> p (g t)"), ACT.Square).then_inc(sq_ready, 1)
                act.wait_ge(ms_done, i * 5 + m + 1)
                link(nc.scalar.activation(rs[:, :], psG[:, 0:N], ACT.Ln, bias=epsr[:, 0:1]), i, PER)
                nc.scalar.activation(rs[:, :], rs[:, :], ACT.Exp, scale=-0.5).then_inc(rs_ready, 1)

            with act.Fori(0, STEPS) as i:
                step[0] = first
                for l in range(2):
                    norm(i, 2 * l)
                    act.wait_ge(q_done, i * 2 + l + 1)
                    nc.scalar.activation(Q[:, :, :, :].rearrange("p e g t -> p e (g t)"), psS[:, 0:2, 0:N], ACT.Identity).then_inc(q_ready, 1)
                    act.wait_ge(k_done, i * 2 + l + 1)
                    nc.scalar.activation(K[:, :, :, :].rearrange("p e g t -> p e (g t)"), psS[:, 2:4, 0:N], ACT.Identity, bias=c("kone")).then_inc(k_ready, 1)
                    for b in range(G):
                        for kc, (_, n) in enumerate(QC):
                            act.wait_ge(st_done, i * 8 + l * 4 + b * 2 + kc + 1)
                            nc.scalar.activation(P[0:n, kc, :, :], psS[0:n, :, 0:2 * T], ACT.Exp, scale=HD ** -0.5).then_inc(p_ready, 1)
                        act.wait_ge(o_done, i * 4 + l * 2 + b + 1)
                        nc.scalar.activation(O[:, b, :, :].rearrange("p e t -> p (e t)"), psG[:, 0:2 * T], ACT.Copy).then_inc(o_ready, 1)
                    act.wait_ge(den_done, i * 2 + l + 1)
                    link(nc.scalar.activation(R[:, :, :], psS[:, 0:2, 0:2 * T], ACT.Ln), i, PER)
                    nc.scalar.activation(R[:, :, :], R[:, :, :], ACT.Exp, scale=-1.0).then_inc(inv_ready, 1)
                    norm(i, 2 * l + 1)
                    act.wait_ge(g_done, i * 2 + l + 1)
                    nc.scalar.activation(EF[0:FW, :, :], psS[0:FW, 0:FC, 0:N], ACT.Exp, scale=-1.0).then_inc(ge_ready, 1)
                    act.wait_ge(ge1_ready, i * 2 + l + 1)
                    link(nc.scalar.activation(EF[0:FW, :, :], EF[0:FW, :, :], ACT.Ln), i, PER)
                    nc.scalar.activation(EF[0:FW, :, :], EF[0:FW, :, :], ACT.Exp, scale=-1.0).then_inc(gsig_ready, 1)
                norm(i, 4)
                for d in range(2):
                    k = i * 2 + d + 1
                    act.wait_ge(xz_done, k)
                    if d:
                        act.wait_ge(ys_ready, i * 2 + 1)
                    nc.scalar.activation(XC[:, :, TAPS - 1:XW], psA[:, 0:N].rearrange("p (g t) -> p g t", g=G), ACT.Copy)
                    nc.scalar.activation(XZ[:, 1, :], psB[:, 0:N], ACT.Copy).then_inc(xc_ready, 1)
                    act.wait_ge(xconv_ready, k)
                    nc.scalar.activation(SG[:, :, :], XZ[:, :, :], ACT.Exp, scale=-1.0).then_inc(sge_ready, 1)
                    act.wait_ge(sg1_ready, k)
                    link(nc.scalar.activation(SG[:, :, :], SG[:, :, :], ACT.Ln), i, PER)
                    nc.scalar.activation(SG[:, :, :], SG[:, :, :], ACT.Exp, scale=-1.0).then_inc(sgr_ready, 1)
                    act.wait_ge(bc_done, k)
                    nc.scalar.activation(dtin[:, :], psY[0:DTR, 0:N], ACT.Copy).then_inc(dtin_ready, 1)
                    nc.scalar.activation(hi[:, :], psA[0:96, 0:N], ACT.Copy).then_inc(hi_ready, 1)
                    act.wait_ge(res_ready, k)
                    nc.scalar.activation(mid[:, :], res[:, :], ACT.Copy).then_inc(mid_ready, 1)
                    act.wait_ge(dtp_done, k)
                    nc.scalar.activation(sp[:, :], psY[:, 0:N], ACT.Abs, bias=v("bdt" + "fb"[d])).then_inc(abs_ready, 1)
                    act.wait_ge(abs_ready, k)
                    nc.scalar.activation(sp[:, :], sp[:, :], ACT.Exp, scale=-1.0).then_inc(spe_ready, 1)
                    act.wait_ge(spe_ready, k)
                    nc.scalar.activation(spl[:, :], sp[:, :], ACT.Ln, bias=1.0).then_inc(sp_ready, 1)
                    act.wait_ge(dt_ready, k)
                    for n in range(NS):
                        last = nc.scalar.activation(dA[:, n, :], dt_[:, :], ACT.Exp, scale=aneg[:, d, n:n + 1])
                    last.then_inc(da_ready, 1)
                act.wait_ge(zc_ready, i + 1)
                nc.scalar.activation(sq[:, :], Z[:, :], ACT.Square).then_inc(sq2_ready, 1)
                act.wait_ge(var_done, i + 1)
                link(nc.scalar.activation(rs[:, :], psY[:, 0:N], ACT.Ln, bias=epsr[:, 1:2]), i, PER)
                nc.scalar.activation(rs[:, :], rs[:, :], ACT.Exp, scale=-0.5).then_inc(rs2_ready, 1)
                act.wait_ge(lg_done, i + 1)
                flat = t1[:, :, :].rearrange("p c e -> p (c e)")
                link(nc.scalar.activation(flat, psA[0:CT, 0:NC4 * E], ACT.Abs), i, PER)
                link(nc.scalar.activation(flat, flat, ACT.Exp, scale=-1.0), i, PER)
                nc.scalar.activation(flat, flat, ACT.Ln, bias=1.0).then_inc(gl_ready, 1)
                act.wait_ge(ht_done, i + 1)
                act.wait_ge(rows_stored, i * 64 + 32)
                nc.scalar.activation(HW[:, :, 0:D], psB[0:CT, 0:NC4 * D].rearrange("p (c d) -> p c d", c=NC4), ACT.Copy).then_inc(ht_ready, 1)
                act.wait_ge(gm_ready, i + 1)
                nc.scalar.activation(score[:, :, :], t1[:, :, :], ACT.Exp).then_inc(score_ready, 1)
                assert step[0] - first == PER, step[0] - first
            with act.Fori(0, E) as e:
                act.wait_ge(xt_done, e + 1)
                nc.scalar.activation(exT, psS[:, 0, 0:CAP], ACT.Copy).then_inc(xt_ready, 1)
                act.wait_ge(e13_done, e + 1)
                nc.scalar.activation(ea, psS[0:MD, 1, 0:CAP], ACT.Exp, scale=-1.0).then_inc(e_exp, 1)
                act.wait_ge(e_one, e + 1)
                step[0] = first + PER * (STEPS)
                step[0] += 1
                nc.scalar.activation(ea, ea, ACT.Ln).then_inc(act_step, 1)
                act.wait_ge(act_step, e + step[0])
                nc.scalar.activation(ea, ea, ACT.Exp, scale=-1.0).then_inc(e_sig, 1)
            last = first + PER * STEPS + E
            for n, (t, m) in enumerate(FINAL):
                act.wait_ge(fin_mv, n + 1)
                nc.scalar.activation(frs[0:B, 0:m], fmv[0:B, 0:m, 1], ACT.Ln, bias=epsr[0:B, 1:2]).then_inc(act_step, 1)
                act.wait_ge(act_step, last + n + 1)
                nc.scalar.activation(frs[0:B, 0:m], frs[0:B, 0:m], ACT.Exp, scale=-0.5).then_inc(fin_rs, 1)

        @block.vector
        def _(dve):
            step = [0]

            def link(ins, i, per):
                step[0] += 1
                ins.then_inc(dve_step, 1)
                dve.wait_ge(dve_step, i * per + step[0])

            dve.wait_ge(loaded, 16 * 5)
            for l in range(2):
                for n in ("qe", "qo", "ke", "ko", "v"):
                    link(nc.vector.tensor_scalar(w(f"{n}{l}"), w(f"{n}{l}"), v(f"ln1{l}"), None, ALU.mult), 0, 0)
                for n in ("gate", "up"):
                    link(nc.vector.tensor_scalar(w(f"{n}{l}"), w(f"{n}{l}"), v(f"ln2{l}"), None, ALU.mult), 0, 0)
            for n, d in enumerate("fb"):
                link(nc.vector.tensor_scalar(dskip[:, n, :], c("ident"), v(f"dskip{d}"), None, ALU.mult), 0, 0)
            link(nc.vector.tensor_scalar(posb[:, :], v("pos"), v("convb"), None, ALU.add), 0, 0)
            link(nc.vector.tensor_tensor(cls0[:, :], v("cls"), v("pos", 0, 1), ALU.add), 0, 0)
            link(nc.vector.tensor_copy(tokf[:, :], c("tok0")[0:CT, :]), 0, 0)
            dve.wait_ge(pool_ready, 9)
            nc.vector.tensor_copy(trashi[:, :], c("unused")).then_inc(trash_ready, 1)
            dve.wait_ge(consts_ready, 1)
            dve.wait_ge(rows_stored, 32)
            nc.vector.memset(sq[:, :], 0.0).then_inc(x_ready, 1)
            first = step[0]
            PER = DVE_PER

            def apply_norm(i, m):
                dve.wait_ge(rs_ready, i * 5 + m + 1)
                nc.vector.tensor_tensor(Hn[:, :, :].rearrange("p g t -> p (g t)"), X[:, :, :].rearrange("p g t -> p (g t)"), rs[:, :], ALU.mult).then_inc(hn_ready, 1)

            def add_to_x():
                nc.vector.tensor_tensor(X[:, :, :].rearrange("p g t -> p (g t)"), X[:, :, :].rearrange("p g t -> p (g t)"), psG[:, 0:N], ALU.add).then_inc(x_ready, 1)

            with dve.Fori(0, STEPS) as i:
                step[0] = first
                dve.wait_ge(conv_done, i + 1)
                link(nc.vector.tensor_tensor(X[:, :, 1:T], psG[:, 0:G * NP].rearrange("p (g t) -> p g t", g=G), posb[:, 1:T].unsqueeze(1).to_broadcast([128, G, NP]), ALU.add), i, PER)
                nc.vector.tensor_copy(X[:, :, 0:1], cls0[:, :].unsqueeze(1).to_broadcast([128, G, 1])).then_inc(x_ready, 1)
                for l in range(2):
                    apply_norm(i, 2 * l)
                    dve.wait_ge(v_done, i * 2 + l + 1)
                    Gv = psG[:, :].rearrange("p (g c h d) -> p g c h d", g=G, c=2, h=HEADS)
                    Vv = V[:, :, :, :].rearrange("p (g c) h d -> p g c h d", g=G)
                    for b in range(G):
                        for cc, (_, n) in enumerate(QC):
                            last = nc.vector.tensor_copy(Vv[0:n, b, cc, :, 0:HD], Gv[0:n, b, cc, :, :])
                    last.then_inc(v_ready, 1)
                    for b in range(G):
                        for qc, (_, n) in enumerate(QC):
                            dve.wait_ge(s_done, i * 8 + l * 4 + b * 2 + qc + 1)
                            nc.vector.tensor_reduce(M[0:n, :, :].rearrange("p e (j r) -> p j e r", r=32)[:, :, :, HD],
                                                    psS[0:n, :, 0:2 * T].rearrange("p j (e t) -> p j e t", e=2), axis=AX, op=ALU.max).then_inc(max_done, 1)
                        dve.wait_ge(place_done, i * 4 + l * 2 + b + 1)
                        nc.vector.tensor_tensor(Q[:, :, b, :], Q[:, :, b, :], psG[:, 0:2 * T].rearrange("p (e t) -> p e t", e=2), ALU.add).then_inc(qm_ready, 1)
                    dve.wait_ge(inv_ready, i * 2 + l + 1)
                    nc.vector.tensor_tensor(O[:, :, :, :].rearrange("p g e t -> p g (e t)"), O[:, :, :, :].rearrange("p g e t -> p g (e t)"), R[:, :, :], ALU.mult).then_inc(on_ready, 1)
                    dve.wait_ge(wo_done, i * 2 + l + 1)
                    add_to_x()
                    apply_norm(i, 2 * l + 1)
                    dve.wait_ge(ge_ready, i * 2 + l + 1)
                    nc.vector.tensor_scalar(EF[0:FW, :, :], EF[0:FW, :, :], 1e18, 1.0, ALU.min, ALU.add).then_inc(ge1_ready, 1)
                    dve.wait_ge(gsig_ready, i * 2 + l + 1)
                    nc.vector.tensor_tensor(EF[0:FW, :, :], EF[0:FW, :, :], psS[0:FW, 0:FC, 0:N], ALU.mult).then_inc(gs_ready, 1)
                    dve.wait_ge(u_done, i * 2 + l + 1)
                    nc.vector.tensor_tensor(EF[0:FW, :, :], EF[0:FW, :, :], psS[0:FW, 0:FC, 0:N], ALU.mult).then_inc(ff_ready, 1)
                    dve.wait_ge(down_done, i * 2 + l + 1)
                    add_to_x()
                dve.wait_ge(rs_ready, i * 5 + 5)
                link(nc.vector.scalar_tensor_tensor(out=H[:, :], in0=X[:, :, :].rearrange("p g t -> p (g t)"), scalar=v("lnf"), in1=rs[:, :], op0=ALU.mult, op1=ALU.mult), i, PER)
                nc.vector.tensor_copy(Hr[:, :], H[:, ::-1]).then_inc(h_ready, 1)
                for d in range(2):
                    k = i * 2 + d + 1
                    dve.wait_ge(xc_ready, k)
                    xconv = XZ[:, 0, :].rearrange("p (g t) -> p g t", g=G)
                    link(nc.vector.tensor_scalar(xconv, XC[:, :, 0:T], v("taps" + "fb"[d], 0, 1), v("bconv" + "fb"[d]), ALU.mult, ALU.add), i, PER)
                    for tap in range(1, TAPS):
                        ins = nc.vector.scalar_tensor_tensor(out=xconv, in0=XC[:, :, tap:tap + T], scalar=v("taps" + "fb"[d], tap, tap + 1), in1=xconv, op0=ALU.mult, op1=ALU.add)
                        if tap < TAPS - 1:
                            link(ins, i, PER)
                        else:
                            ins.then_inc(xconv_ready, 1)
                    dve.wait_ge(sge_ready, k)
                    nc.vector.tensor_scalar(SG[:, :, :], SG[:, :, :], 1e18, 1.0, ALU.min, ALU.add).then_inc(sg1_ready, 1)
                    dve.wait_ge(sgr_ready, k)
                    nc.vector.tensor_tensor(XZ[:, :, :], XZ[:, :, :], SG[:, :, :], ALU.mult).then_inc(xs_ready, 1)
                    dve.wait_ge(hi_ready, k)
                    nc.vector.scalar_tensor_tensor(out=res[:, :], in0=hi[:, :], scalar=c("part1")[0:96, :], in1=psA[0:96, 0:N], op0=ALU.mult, op1=ALU.add).then_inc(res_ready, 1)
                    dve.wait_ge(mid_ready, k)
                    nc.vector.scalar_tensor_tensor(out=bc[:, :], in0=mid[:, :], scalar=c("part2")[0:96, :], in1=res[:, :], op0=ALU.mult, op1=ALU.add).then_inc(bcs_ready, 1)
                    dve.wait_ge(abs_ready, k)
                    link(nc.vector.tensor_scalar(dt_[:, :], psY[:, 0:N], v("bdt" + "fb"[d]), 0.0, ALU.add, ALU.max), i, PER)
                    dve.wait_ge(spe_ready, k)
                    nc.vector.tensor_scalar(small[:, :], sp[:, :], LOG1P_SERIES, None, ALU.is_lt)
                    link(nc.vector.tensor_scalar(u[:, :], sp[:, :], 1 / 3, -0.5, ALU.mult, ALU.add), i, PER)
                    link(nc.vector.tensor_tensor(u[:, :], u[:, :], sp[:, :], ALU.mult), i, PER)
                    dve.wait_ge(sp_ready, k)
                    link(nc.vector.scalar_tensor_tensor(out=u[:, :], in0=u[:, :], scalar=1.0, in1=sp[:, :], op0=ALU.add, op1=ALU.mult), i, PER)
                    dve.sem_inc(dve_waited, 1)
                    link(nc.vector.copy_predicated(spl[:, :], small[:, :], u[:, :]), i, PER)
                    nc.vector.tensor_tensor(dt_[:, :], dt_[:, :], spl[:, :], ALU.add).then_inc(dt_ready, 1)
                    dve.wait_ge(dt_ready, k)
                    link(nc.vector.tensor_tensor(u[:, :], dt_[:, :], XZ[:, 0, :], ALU.mult), i, PER)
                    for n in range(NS):
                        dve.wait_ge(bb_done, i * 4 * NS + d * 2 * NS + n + 1)
                        nc.vector.tensor_tensor(hs[:, n, :], u[:, :], AB[n % 2][:, 0:N], ALU.mult).then_inc(mul_done, 1)
                    dve.wait_ge(mul_done, i * 4 * NS + d * 2 * NS + NS)
                    dve.wait_ge(da_ready, k)
                    link(nc.vector.memset(dA[:, :, :].rearrange("p n (g t) -> p (n g) t", g=G)[:, :, 0:1], 0.0), i, PER)
                    hflat = hs[:, :, :].rearrange("p n t -> p (n t)")
                    link(nc.vector.tensor_tensor_scan(hflat, dA[:, :, :].rearrange("p n t -> p (n t)"), hflat, 0.0, ALU.mult, ALU.add), i, PER)
                    for n in range(NS):
                        dve.wait_ge(bb_done, i * 4 * NS + d * 2 * NS + NS + n + 1)
                        nc.vector.tensor_tensor(dA[:, n, :], hs[:, n, :], AB[n % 2][:, 0:N], ALU.mult).then_inc(mul_done, 1)
                    dve.wait_ge(y_done, k)
                    nc.vector.tensor_tensor(YS[:, d, ::-1] if d else YS[:, d, :], psY[:, 0:N], XZ[:, 1, :], ALU.mult).then_inc(ys_ready, 1)
                dve.wait_ge(m_done, i + 1)
                nc.vector.tensor_tensor(Z[:, :], H[:, :], psA[:, 0:N], ALU.add).then_inc(z_ready, 1)
                dve.wait_ge(mean_done, i + 1)
                nc.vector.tensor_tensor(Z[:, :], Z[:, :], psY[:, 0:N], ALU.subtract).then_inc(zc_ready, 1)
                dve.wait_ge(rs2_ready, i + 1)
                nc.vector.tensor_tensor(h2[:, 0:N], Z[:, :], rs[:, :], ALU.mult).then_inc(h2_ready, 1)
                dve.wait_ge(gl_ready, i + 1)
                nc.vector.scalar_tensor_tensor(out=t1[:, :, :].rearrange("p c e -> p (c e)"), in0=psA[0:CT, 0:NC4 * E], scalar=0.0, in1=t1[:, :, :].rearrange("p c e -> p (c e)"), op0=ALU.min, op1=ALU.subtract).then_inc(gm_ready, 1)
                dve.wait_ge(score_ready, i + 1)
                sg8 = score[:, :, :].rearrange("p c (g k) -> p (c g) k", k=8)
                link(nc.vector.tensor_tensor(ext[:, :, 0:8].rearrange("p (c g) k -> p c g k", c=NC4), score[:, :, :].rearrange("p c (g k) -> p c g k", k=8), gateb[0:CT, :].rearrange("p (g k) -> p g k", k=8).unsqueeze(1).to_broadcast([CT, NC4, GR, 8]), ALU.add), i, PER)
                link(nc.vector.tensor_copy(ext[:, :, 8:12], ext[:, :, 0:4]), i, PER)
                for s in range(1, 5):
                    last = nc.vector.tensor_tensor(pairs[:, :, s - 1, :], ext[:, :, 0:8], ext[:, :, s:s + 8], ALU.add)
                link(last, i, PER)
                link(nc.vector.tensor_reduce(gs[:, :, :].rearrange("p c g -> p (c g)"), pairs[:, :, :, :].rearrange("p m s k -> p m (s k)"), axis=AX, op=ALU.max), i, PER)
                them = gs[:, :, :].unsqueeze(2).to_broadcast([CT, NC4, GR, GR])
                mine = gs[:, :, :].unsqueeze(3).to_broadcast([CT, NC4, GR, GR])
                link(nc.vector.tensor_tensor(cmp1[:, :, :, :], them, mine, ALU.is_gt), i, PER)
                link(nc.vector.tensor_tensor(cmp2[:, :, :, :], them, mine, ALU.is_equal), i, PER)
                fore = c("groupbefore")[0:CT, :].unsqueeze(1).to_broadcast([CT, NC4, GR * GR])
                c1, c2 = (x[:, :, :, :].rearrange("p c g h -> p c (g h)") for x in (cmp1, cmp2))
                link(nc.vector.tensor_tensor(c2, c2, fore, ALU.mult), i, PER)
                link(nc.vector.tensor_tensor(c1, c1, c2, ALU.add), i, PER)
                link(nc.vector.tensor_reduce(rank[:, :], cmp1[:, :, :, :].rearrange("p c g h -> p (c g) h"), axis=AX, op=ALU.add), i, PER)
                link(nc.vector.tensor_scalar(rank[:, :], rank[:, :], float(TOPG), -BIG, ALU.is_ge, ALU.mult), i, PER)
                m8 = masked[:, :, :].rearrange("p c (g k) -> p (c g) k", k=8)
                link(nc.vector.tensor_tensor(m8, ext[:, :, 0:8], rank[:, :].unsqueeze(2).to_broadcast([CT, NC4 * GR, 8]), ALU.add), i, PER)
                dve.sem_inc(dve_waited, 1)
                for q in range(NC4):
                    last = nc.vector.max(top8[:, q, :], masked[:, q, :])
                link(last, i, PER)
                dve.sem_inc(dve_waited, 1)
                for q in range(NC4):
                    last = nc.vector.match_replace(out=rest[:, q, :], in_to_replace=top8[:, q, :], in_values=masked[:, q, :], imm_value=-3e38)
                link(last, i, PER)
                link(nc.vector.tensor_tensor(sel[:, :, :], rest[:, :, :], masked[:, :, :], ALU.not_equal), i, PER)
                link(nc.vector.tensor_tensor(score[:, :, :], score[:, :, :], sel[:, :, :], ALU.mult), i, PER)
                link(nc.vector.tensor_reduce(wsum[:, :], score[:, :, :], axis=AX, op=ALU.add), i, PER)
                link(nc.vector.reciprocal(winv[:, :], wsum[:, :]), i, PER)
                link(nc.vector.tensor_tensor(sel[:, :, :], sel[:, :, :], c("valid")[0:CT, :].unsqueeze(2).to_broadcast([CT, NC4, E]), ALU.mult), i, PER)
                nc.vector.tensor_copy(selh[:, :, :], sel[:, :, :]).then_inc(sel_ready, 1)
                dve.wait_ge(rows_stored, i * 64 + 32)
                nc.vector.scalar_tensor_tensor(out=HW[:, :, D:ROW], in0=score[:, :, :], scalar=ROUTE_SCALE, in1=winv[:, :].unsqueeze(2).to_broadcast([CT, NC4, E]), op0=ALU.mult, op1=ALU.mult).then_inc(hw_ready, 1)
                dve.wait_ge(pos_done, i + 1)
                link(nc.vector.tensor_tensor(pos[:, :, :], psA[0:CT, 0:NC4 * E].rearrange("p (c e) -> p c e", c=NC4), base[:, :].unsqueeze(1).to_broadcast([CT, NC4, E]), ALU.add), i, PER)
                link(nc.vector.tensor_tensor(base[:, :], base[:, :], psA[0:CT, NC4 * E:NC4 * E + E], ALU.add), i, PER)
                link(nc.vector.scalar_tensor_tensor(out=sel[:, :, :], in0=pos[:, :, :], scalar=float(CAP), in1=sel[:, :, :], op0=ALU.is_lt, op1=ALU.mult), i, PER)
                link(nc.vector.tensor_tensor(pos[:, :, :], pos[:, :, :], c("slot1")[0:CT, :].unsqueeze(1).to_broadcast([CT, NC4, E]), ALU.add), i, PER)
                link(nc.vector.tensor_tensor(pos[:, :, :], pos[:, :, :], sel[:, :, :], ALU.mult), i, PER)
                dve.sem_inc(dve_waited, 1)
                for q in range(NC4):
                    last = nc.vector.max(slotf[:, q, :], pos[:, q, :])
                link(last, i, PER)
                link(nc.vector.tensor_scalar(noslot[:, :, :], slotf[:, :, :], 0.0, float(NOSLOT), ALU.is_equal, ALU.mult), i, PER)
                dve.wait_ge(slots_free, i + 1)
                nc.vector.scalar_tensor_tensor(out=sloti[:, :], in0=slotf[:, :, :].rearrange("p c k -> p (c k)"), scalar=-1.0, in1=noslot[:, :, :].rearrange("p c k -> p (c k)"), op0=ALU.add, op1=ALU.add)
                link(nc.vector.tensor_copy(toki[:, :], tokf[:, :]), i, PER)
                nc.vector.tensor_scalar(tokf[:, :], tokf[:, :], float(N), None, ALU.add).then_inc(slot_ready, 1)
                dve.wait_ge(slot_ready, i + 1)
                if step[0] - first != PER:
                    raise AssertionError(f"DVE_PER {step[0] - first}")
            with dve.Fori(0, E) as e:
                dve.wait_ge(e_exp, e + 1)
                nc.vector.tensor_scalar(ea, ea, 1e18, 1.0, ALU.min, ALU.add).then_inc(e_one, 1)
                dve.wait_ge(e_sig, e + 1)
                nc.vector.tensor_tensor(ea, ea, psS[0:MD, 1, 0:CAP], ALU.mult).then_inc(e_mul, 1)
                dve.wait_ge(e_mul, e + 1)
                nc.vector.tensor_tensor(ea, ea, psS[0:MD, 2, 0:CAP], ALU.mult).then_inc(e_act, 1)
                dve.wait_ge(e2_done, e + 1)
                for k in range(2):
                    ins = nc.vector.tensor_scalar(eo[:, k, :], psS[:, 3, k * D:(k + 1) * D], ex[:, k, bass.ds(e + D, 1)], None, ALU.mult)
                ins.then_inc(e_out, 1)
            for n, (t, m) in enumerate(FINAL):
                dve.wait_ge(fin_loaded, 16 * (n + 1))
                for q in range(m):
                    last = nc.vector.bn_stats(fst[0:B, q, :], fin[0:B, q, :])
                last.then_inc(fin_step, 1)
                dve.wait_ge(fin_step, n * 2 + 1)
                for q in range(m):
                    last = nc.vector.bn_aggr(fmv[0:B, q, :], fst[0:B, q, :])
                last.then_inc(fin_mv, 1)
                dve.wait_ge(fin_rs, n + 1)
                nc.vector.tensor_tensor(fin[0:B, 0:m, :], fin[0:B, 0:m, :], fmv[0:B, 0:m, 0:1].to_broadcast([B, m, D]), ALU.subtract).then_inc(fin_step, 1)
                dve.wait_ge(fin_step, n * 2 + 2)
                nc.vector.tensor_tensor(fin[0:B, 0:m, :], fin[0:B, 0:m, :], frs[0:B, 0:m].unsqueeze(2).to_broadcast([B, m, D]), ALU.mult).then_inc(fin_ready, 1)

        @block.tensor
        def _(pe):
            mm = nc.tensor.matmul

            def norm(i, m):
                pe.wait_ge(sq_ready, i * 5 + m + 1)
                mm(psG[:, 0:N], c("mean"), sq[:, :], start=True, stop=True).then_inc(ms_done, 1)

            with pe.Fori(0, STEPS) as i:
                pe.wait_ge(x_ready, i * 5 + 1)
                pe.wait_ge(patches_loaded, i * 16 + 16)
                for k in range(KP):
                    last = mm(psG[:, 0:G * NP], w("conv", k * D, (k + 1) * D), pat[:, k, :], start=k == 0, stop=k == KP - 1)
                last.then_inc(conv_done, 1)
                for l in range(2):
                    norm(i, 2 * l)
                    pe.wait_ge(hn_ready, i * 4 + 2 * l + 1)
                    hn = Hn[:, :, :].rearrange("p g t -> p (g t)")
                    for s, n in enumerate(("qe", "qo", "ke", "ko")):
                        last = mm(psS[:, s, 0:N], w(f"{n}{l}"), hn, start=True, stop=True)
                        if s % 2:
                            last.then_inc((q_done, k_done)[s // 2], 1)
                    for b in range(G):
                        for cc, (t0, n) in enumerate(QC):
                            last = mm(psG[0:n, (2 * b + cc) * D:(2 * b + cc + 1) * D], Hn[:, b, t0:t0 + n], w(f"v{l}"), start=True, stop=True)
                    last.then_inc(v_done, 1)
                    pe.wait_ge(q_ready, i * 2 + l + 1)
                    pe.wait_ge(k_ready, i * 2 + l + 1)
                    for b in range(G):
                        for qc, (t0, n) in enumerate(QC):
                            if b or qc:
                                pe.wait_ge(max_done, i * 8 + l * 4 + b * 2 + qc) if qc else pe.wait_ge(p_ready, i * 8 + l * 4 + b * 2)
                            for e in range(2):
                                for j in range(4):
                                    r = slice(32 * j, 32 * j + 32)
                                    last = mm(psS[0:n, j, e * T:(e + 1) * T], Q[r, e, b, t0:t0 + n], K[r, e, b, :], start=True, stop=True)
                            last.then_inc(s_done, 1)
                            pe.wait_ge(max_done, i * 8 + l * 4 + b * 2 + qc + 1)
                            if qc == 0:
                                pe.wait_ge(v_ready, i * 2 + l + 1) if b == 0 else pe.wait_ge(o_ready, i * 4 + l * 2 + 1)
                            for e in range(2):
                                last = mm(psG[:, e * T + t0:e * T + t0 + n], M[0:n, e, :], c("negident")[0:n, 0:n], start=True, stop=True)
                        last.then_inc(place_done, 1)
                        pe.wait_ge(qm_ready, i * 4 + l * 2 + b + 1)
                        for kc, (t0, n) in enumerate(QC):
                            if kc:
                                pe.wait_ge(p_ready, i * 8 + l * 4 + b * 2 + kc)
                            for e in range(2):
                                for j in range(4):
                                    r = slice(32 * j, 32 * j + 32)
                                    last = mm(psS[0:n, j, e * T:(e + 1) * T], K[r, e, b, t0:t0 + n], Q[r, e, b, :], start=True, stop=True)
                            last.then_inc(st_done, 1)
                        pe.wait_ge(p_ready, i * 8 + l * 4 + b * 2 + 2)
                        for e in range(2):
                            for kc, (t0, n) in enumerate(QC):
                                for j in range(4):
                                    last = mm(psG[32 * j:32 * j + 32, e * T:(e + 1) * T], V[0:n, 2 * b + kc, 2 * j + e, :], P[0:n, kc, j, e * T:(e + 1) * T], start=kc == 0, stop=kc == 1, tile_position=(0, 32 * j))
                        last.then_inc(o_done, 1)
                    pe.wait_ge(o_ready, i * 4 + l * 2 + 2)
                    for b in range(G):
                        last = mm(psS[:, b, 0:2 * T], c("dsel"), O[:, b, :, :].rearrange("p e t -> p (e t)"), start=True, stop=True)
                    last.then_inc(den_done, 1)
                    pe.wait_ge(on_ready, i * 2 + l + 1)
                    for e in range(2):
                        last = mm(psG[:, 0:N].rearrange("p (g t) -> p g t", g=G), w(("woe", "woo")[e] + str(l)), O[:, :, e, :], start=e == 0, stop=e == 1)
                    last.then_inc(wo_done, 1)
                    norm(i, 2 * l + 1)
                    pe.wait_ge(hn_ready, i * 4 + 2 * l + 2)
                    for f in range(FC):
                        last = mm(psS[0:FW, f, 0:N], w(f"gate{l}", f * FW, (f + 1) * FW), hn, start=True, stop=True)
                    last.then_inc(g_done, 1)
                    pe.wait_ge(gs_ready, i * 2 + l + 1)
                    for f in range(FC):
                        last = mm(psS[0:FW, f, 0:N], w(f"up{l}", f * FW, (f + 1) * FW), hn, start=True, stop=True)
                    last.then_inc(u_done, 1)
                    pe.wait_ge(ff_ready, i * 2 + l + 1)
                    for f in range(FC):
                        last = mm(psG[:, 0:N], w(f"down{l}", f * D, (f + 1) * D)[0:FW, :], EF[0:FW, f, :], start=f == 0, stop=f == FC - 1)
                    last.then_inc(down_done, 1)
                norm(i, 4)
                pe.wait_ge(h_ready, i + 1)
                for d in range(2):
                    x, s = (H, Hr)[d], "fb"[d]
                    k = i * 2 + d + 1
                    mm(psA[:, 0:N], w(f"win{s}", 0, D), x[:, :], start=True, stop=True)
                    mm(psB[:, 0:N], w(f"win{s}", D, 2 * D), x[:, :], start=True, stop=True).then_inc(xz_done, 1)
                    pe.wait_ge(xs_ready, k)
                    mm(psY[0:DTR, 0:N], w(f"xdt{s}"), XZ[:, 0, :], start=True, stop=True)
                    mm(psA[0:96, 0:N], w(f"xbc{s}"), XZ[:, 0, :], start=True, stop=True).then_inc(bc_done, 1)
                    pe.wait_ge(dtin_ready, k)
                    mm(psY[:, 0:N], w(f"wdt{s}")[0:DTR, :], dtin[:, :], start=True, stop=True).then_inc(dtp_done, 1)
                    pe.wait_ge(bcs_ready, k)
                    for n in range(2 * NS + 2):
                        if n < 2 * NS:
                            if n >= 2:
                                pe.wait_ge(mul_done, i * 4 * NS + d * 2 * NS + n - 1)
                            mm(AB[n % 2][:, 0:N], bcsel[:, n, :], bc[:, :], start=True, stop=True).then_inc(bb_done, 1)
                        if n >= NS + 2:
                            q = n - NS - 2
                            pe.wait_ge(mul_done, i * 4 * NS + d * 2 * NS + NS + q + 1)
                            mm(psY[:, 0:N], c("ident"), dA[:, q, :], start=q == 0, stop=False)
                    mm(psY[:, 0:N], dskip[:, d, :], XZ[:, 0, :], start=False, stop=True).then_inc(y_done, 1)
                pe.wait_ge(ys_ready, i * 2 + 2)
                for d in range(2):
                    last = mm(psA[:, 0:N], w("wout" + "fb"[d]), YS[:, d, :], start=d == 0, stop=d == 1)
                last.then_inc(m_done, 1)
                pe.wait_ge(z_ready, i + 1)
                mm(psY[:, 0:N], c("mean"), Z[:, :], start=True, stop=True).then_inc(mean_done, 1)
                pe.wait_ge(sq2_ready, i + 1)
                mm(psY[:, 0:N], c("mean"), sq[:, :], start=True, stop=True).then_inc(var_done, 1)
                pe.wait_ge(h2_ready, i + 1)
                for q in range(NC4):
                    last = mm(psA[0:CT, q * E:(q + 1) * E], h2[:, q * CT:(q + 1) * CT], w("route"), start=True, stop=True)
                last.then_inc(lg_done, 1)
                for q in range(NC4):
                    last = nc.tensor.transpose(psB[0:CT, q * D:(q + 1) * D], h2[:, q * CT:(q + 1) * CT], c("ident"))
                last.then_inc(ht_done, 1)
                pe.wait_ge(sel_ready, i + 1)
                for q in range(NC4 + 1):
                    for p in range(min(q + 1, NC4)):
                        last = mm(psA[0:CT, q * E:(q + 1) * E], (before_h if p == q else ones_h)[0:CT, 0:CT], selh[:, p, :], start=p == 0, stop=p == min(q, NC4 - 1))
                last.then_inc(pos_done, 1)
            with pe.Fori(0, E) as e:
                pe.wait_ge(gathered, e * 32 + 32)
                for k in range(2):
                    last = nc.tensor.transpose(psS[:, 0, k * D:(k + 1) * D], ex[:, k, 0:D], c("ident"))
                last.then_inc(xt_done, 1)
                pe.wait_ge(xt_ready, e + 1)
                pe.wait_ge(mload, e * 32 + 32)
                mm(psS[0:MD, 1, 0:CAP], ew[:, 0:MD], exT, start=True, stop=True)
                mm(psS[0:MD, 2, 0:CAP], ew[:, MD:2 * MD], exT, start=True, stop=True).then_inc(e13_done, 1)
                pe.wait_ge(e_act, e + 1)
                for k in range(2):
                    last = mm(psS[:, 3, k * D:(k + 1) * D], ea[:, k * 128:(k + 1) * 128], ew[0:MD, D:2 * D], start=True, stop=True)
                last.then_inc(e2_done, 1)


def kernel(**x):
    import numpy as np
    import concourse.bacc as _bacc
    from concourse import mybir as _mybir
    from concourse.bass_utils import run_bass_kernel_spmd as _run

    a = {k: np.asarray(q) for k, q in x.items()}
    f4 = np.float32
    g = IMG // PATCH
    pt = a["x"].reshape(STEPS, G, CH, g, PATCH, g, PATCH).transpose(0, 2, 4, 6, 1, 3, 5)
    pt = np.ascontiguousarray(pt.reshape(STEPS, KP, 128, G * NP).transpose(0, 2, 1, 3))

    wts = np.zeros((128, W_N), f4)

    def put(to, cols, name, value):
        at, n = cols[name]
        value = value.reshape(value.shape[0], -1)
        to[0:value.shape[0], at:at + value.shape[1]] = value

    t = "L0_tok_"
    put(wts, W_COLS, "conv", a[t + "conv_w"].reshape(D, KP, 128).transpose(2, 1, 0))
    for l in range(2):
        qkv = a[t + f"qkv_{l}"].reshape(3, 4, 2, HD, D)
        for m, n in enumerate("qk"):
            for p, s in enumerate("eo"):
                padded = np.zeros((128, 4, 32), f4)
                padded[:, :, 0:HD] = qkv[m, :, p].transpose(2, 0, 1)
                put(wts, W_COLS, f"{n}{s}{l}", padded)
        put(wts, W_COLS, f"v{l}", a[t + f"qkv_{l}"][2 * D:].T)
        wo = a[t + f"wo_{l}"].T.reshape(4, 2, HD, D)
        for p, s in enumerate("eo"):
            padded = np.zeros((4, 32, D), f4)
            padded[:, 0:HD] = wo[:, p]
            put(wts, W_COLS, f"wo{s}{l}", padded.reshape(128, D))
        put(wts, W_COLS, f"gate{l}", a[t + f"gate_{l}"].T)
        put(wts, W_COLS, f"up{l}", a[t + f"up_{l}"].T)
        down = np.zeros((FC * FW, D), f4)
        down[0:FF] = a[t + f"down_{l}"].T
        put(wts, W_COLS, f"down{l}", down.reshape(FC, FW, D).transpose(1, 0, 2))
    m = "L0_attn_"
    for s in "fb":
        put(wts, W_COLS, f"win{s}", a[m + f"W_in_{s}"])
        put(wts, W_COLS, f"xdt{s}", a[m + f"W_xproj_{s}"][:, 0:DTR])
        put(wts, W_COLS, f"xbc{s}", np.concatenate([a[m + f"W_xproj_{s}"][:, DTR:]] * 3, axis=1))
        put(wts, W_COLS, f"wdt{s}", a[m + f"W_dt_{s}"])
        put(wts, W_COLS, f"wout{s}", a[m + f"W_out_{s}"])
    put(wts, W_COLS, "route", a["L0_ffn_gate_w"].T)

    vec = np.zeros((128, V_N), f4)
    put(vec, V_COLS, "convb", a[t + "conv_b"][:, None])
    put(vec, V_COLS, "cls", a[t + "cls_token"].reshape(D, 1))
    put(vec, V_COLS, "pos", a[t + "pos_emb"].reshape(T, D).T)
    put(vec, V_COLS, "lnf", a[t + "ln_f"][:, None])
    for l in range(2):
        put(vec, V_COLS, f"ln1{l}", a[t + f"ln1_{l}"][:, None])
        put(vec, V_COLS, f"ln2{l}", a[t + f"ln2_{l}"][:, None])
    for s in "fb":
        put(vec, V_COLS, f"taps{s}", a[m + f"W_conv_{s}"])
        put(vec, V_COLS, f"bconv{s}", a[m + f"b_conv_{s}"][:, None])
        put(vec, V_COLS, f"bdt{s}", a[m + f"b_dt_{s}"][:, None])
        put(vec, V_COLS, f"alog{s}", a[m + f"A_log_{s}"])
        put(vec, V_COLS, f"dskip{s}", a[m + f"D_{s}"][:, None])

    cst = np.zeros((128, C_N), f4)
    p = np.arange(128)
    dsel = np.zeros((128, 128), f4)
    for j in range(4):
        dsel[32 * j + HD, 32 * j:32 * j + 32] = 1
    put(cst, C_COLS, "ident", np.eye(128, dtype=f4))
    put(cst, C_COLS, "negident", -np.eye(128, dtype=f4))
    put(cst, C_COLS, "mean", np.full((128, 128), 1 / D, f4))
    put(cst, C_COLS, "dsel", dsel)
    put(cst, C_COLS, "before", np.triu(np.ones((128, 128), f4), 1))
    put(cst, C_COLS, "ones", np.ones((128, 128), f4))
    put(cst, C_COLS, "slot1", np.tile(np.arange(E) * CAP + 1.0, (128, 1)))
    tok = np.arange(NC4)[None] * CT + p[:, None]
    put(cst, C_COLS, "tok0", tok)
    put(cst, C_COLS, "valid", tok < N)
    put(cst, C_COLS, "unused", TOK + (np.arange(SLOTS + 128) // 2 % 128).reshape(128, -1))
    put(cst, C_COLS, "part1", -1.0 * (p >= 32)[:, None])
    put(cst, C_COLS, "part2", -1.0 * (p >= 64)[:, None])
    put(cst, C_COLS, "kone", 1.0 * (p % 32 == HD)[:, None])
    put(cst, C_COLS, "groupbefore", np.tile(np.tril(np.ones((GR, GR)), -1).reshape(1, -1), (128, 1)))
    bcsel = np.zeros((96, 2 * NS, D), f4)
    for r in range(96):
        bcsel[r, r % 32] = 1

    w13 = np.concatenate([a["L0_ffn_w1"], a["L0_ffn_w3"]], axis=2)
    arrays = {"patches": pt, "weights": wts, "vectors": vec, "consts": cst, "bcsel": bcsel.reshape(96, -1),
              "gate_b": a["L0_ffn_gate_b"], "w13": w13, "w2": a["L0_ffn_w2"]}
    arrays = {k: np.ascontiguousarray(q) for k, q in arrays.items()}
    nc = _bacc.Bacc("TRN2", target_bir_lowering=False, num_devices=1)
    args = [nc.dram_tensor(k, q.shape, _mybir.dt.from_np(q.dtype), kind="ExternalInput").ap() for k, q in arrays.items()]
    out = nc.dram_tensor("out", (B, T, D), _mybir.dt.float32, kind="ExternalOutput").ap()
    vit_mamba_moe(nc, *args, out)
    r = _run(nc, [arrays], core_ids=[0])
    return r.results[0]["out"]
```

```python
import concourse.bass as bass
from concourse import mybir
from contextlib import ExitStack

D = 128
B = 128
PATCH, IMG, CH = 16, 224, 3
NP = (IMG // PATCH) ** 2
T = NP + 1
G = 2
N = G * T
STEPS = B // G
KP = CH * PATCH * PATCH // 128
HEADS, HD = 8, 16
FF = 344
FC = 3
FW = -(-FF // FC)
NS = 16
DTR = 32
TAPS = 4
XW = T + TAPS - 1
E, GR, TOPG, TOPK, CAP, MD = 64, 8, 4, 8, 256, 64
ROUTE_SCALE = 2.5
CT = 99
NC4 = 4
PADN = NC4 * CT
ROW = D + E
TOK = B * T
SLOTS = E * CAP
NQ = 2
TP = NQ * CT
CHUNKS = [(b, q) for b in range(G) for q in range(NQ)]
NOSLOT = 1 << 20
PAD = CAP
ZP = 128
LOG1P_SERIES = 2.0 ** -8
BIG = 1e30
EPS_RMS, EPS_LN = 1e-6, 1e-5

QUARTERS = 8
QN = NS * 2 // QUARTERS
MULS = 2 * NS * 2
HBUF = 3
EXP_MAX = 1e18

ACT_FRONT, ACT_BACK, DVE_FRONT, DVE_BACK, DVE_ROUTE = 7, 3, 2, 17, 27

UNITS = ([(n, d) for n in ("project", "conv", "sigmoid", "gate") for d in range(2)]
         + [("xproj", 0), ("split", 0), ("xproj", 1), ("split", 1), ("dtproj", 0), ("dt", 0), ("dtproj", 1), ("dt", 1)]
         + [("decay", 0), ("decay", 1)])
for _g in range(QUARTERS):
    UNITS += [("input", _g, _k) for _k in range(QN)] + [("scan", _g)]
    UNITS += [("sum", _g - 1)] if _g else []
    UNITS += [("decay", _g + 2)] if _g + 2 < QUARTERS else []
    UNITS += [("output", _g, _k) for _k in range(QN)]
UNITS += [("sum", QUARTERS - 1), ("merge",), ("store",), ("route",)]
LAYER_STAGES = (["norm", "qkv"] + [f"{n}{c}" for c in range(len(CHUNKS)) for n in ("score", "turn")]
                + ["value", "turnback", "wo", "norm2", "gate", "sig", "up", "down"])
STAGES = ["conv"] + [f"{n}.{l}" for l in range(2) for n in LAYER_STAGES] + ["normf"]
WEIGHT = {"conv": 6, "norm": 3, "norm2": 3, "qkv": 5, "score": 6, "turn": 4, "value": 2, "turnback": 2, "wo": 3,
          "gate": 4, "sig": 4, "up": 4, "down": 4, "normf": 4}


def shares():
    w = [WEIGHT[n.split(".")[0].rstrip("0123") if n[0:4] in ("scor", "turn") else n.split(".")[0]] for n in STAGES]
    total, acc, out = sum(w), 0, {}
    for n, x in zip(STAGES, w):
        acc += x
        out[n] = len(UNITS) * acc // total
    return out


SHARE = shares()

def _cols(widths):
    at, out = 0, {}
    for name, w in widths:
        out[name] = (at, w)
        at += w
    return out, at


W_COLS, W_N = _cols(
    [("conv", KP * D)]
    + [(f"{n}{l}", w) for l in range(2) for n, w in (
        ("q", D), ("k", D), ("v", D), ("wo", D),
        ("gate", FC * FW), ("up", FC * FW), ("down", FC * D))]
    + [(f"{n}{d}", w) for d in "fb" for n, w in (
        ("win", 2 * D), ("xdt", DTR), ("xbc", 3 * 2 * NS), ("wdt", D), ("wout", D))]
    + [("route", E)])
V_COLS, V_N = _cols(
    [("convb", 1), ("cls", 1), ("pos", T), ("lnf", 1)]
    + [(f"{n}{l}", 1) for l in range(2) for n in ("ln1", "ln2")]
    + [(f"{n}{d}", w) for d in "fb" for n, w in (
        ("taps", TAPS), ("bconv", 1), ("bdt", 1), ("alog", NS), ("dskip", 1))])
C_COLS, C_N = _cols([("ident", D), ("mean", D), ("before", D), ("ones", D),
                     ("slot1", E), ("valid", NC4), ("tok0", NC4), ("part1", 1), ("part2", 1),
                     ("heads", HEADS), ("groupbefore", GR * GR), ("unused", SLOTS // 128)])


def vit_mamba_moe(nc, patches, weights, vectors, consts, bcsel_d, gate_b, w13, w2, out):
    f32, bf16, i32 = mybir.dt.float32, mybir.dt.bfloat16, mybir.dt.int32
    ACT = mybir.ActivationFunctionType
    ALU = mybir.AluOpType
    AX = mybir.AxisListType.X

    rows_d = nc.dram_tensor("rows_scratch", (TOK + PAD, ROW), f32, kind="Internal").ap()
    sum_d = nc.dram_tensor("sum_scratch", (TOK + PAD, D), f32, kind="Internal").ap()
    slot_d = nc.dram_tensor("slot_scratch", (SLOTS, 1), i32, kind="Internal").ap()

    ctx = ExitStack()
    with ctx:
        def sb(name, shape, dt=f32):
            return ctx.enter_context(nc.sbuf_tensor(name, shape, dt))

        def sem(name):
            return ctx.enter_context(nc.semaphore(name))

        wts = sb("wts", [128, W_N])
        vec = sb("vec", [128, V_N])
        cst = sb("cst", [128, C_N])

        def w(name, a=0, b=None):
            at, n = W_COLS[name]
            return wts[:, at + a:at + (n if b is None else b)]

        def v(name, a=0, b=None):
            at, n = V_COLS[name]
            return vec[:, at + a:at + (n if b is None else b)]

        def c(name, a=0, b=None):
            at, n = C_COLS[name]
            return cst[:, at + a:at + (n if b is None else b)]

        bcsel = sb("bcsel_h", [96, 2 * NS, D], bf16)
        before_h = sb("before_h", [128, D], bf16)
        ones_h = sb("ones_h", [128, D], bf16)
        posb = sb("posb", [128, T])
        cls0 = sb("cls0", [128, 1])
        aneg = sb("aneg", [128, 2, NS])
        dskip = sb("dskip", [128, 2, D])
        gateb = sb("gateb", [128, E])
        epsr = sb("epsr", [128, 2])

        pat = sb("pat", [128, KP, G * NP])
        X = sb("X", [128, G, T])
        sq = sb("sq", [128, N])
        rs = sb("rs", [128, N])
        Hn = sb("Hn", [128, G, TP])
        Q = sb("Q", [128, G, TP])
        K = sb("K", [128, G, TP])
        KM = sb("KM", [128, G, HEADS, TP])
        V = sb("V", [CT, G * NQ, HEADS, HD + 1])
        least_s = sb("least_s", [CT, HEADS])
        P = sb("P", [CT, HEADS, TP])
        PT = sb("PT", [CT, HEADS, NQ, CT])
        rden = sb("rden", [CT, HEADS])
        ON = sb("ON", [CT, HEADS, HD])
        OT = sb("OT", [128, G, TP])
        EF = sb("EF", [128, FC, N])
        H = sb("H", [128, PADN])
        Hr = sb("Hr", [128, N])
        XC = sb("XC", [128, 2, G, XW])
        XZ = sb("XZ", [128, 2, 2, N])
        SG = sb("SG", [128, 2, 2, N])
        dtin = sb("dtin", [DTR, 2, N])
        hi = sb("hi", [96, 2, N], bf16)
        res = sb("res", [96, N])
        mid = sb("mid", [96, N], bf16)
        bc = sb("bc", [96, 2, N], bf16)
        dt_ = sb("dt_", [128, 2, N])
        sp = sb("sp", [128, N])
        spl = sb("spl", [128, N])
        small = sb("small", [128, N], mybir.dt.uint32)
        u = sb("u", [128, 2, N])
        dA = sb("dA", [128, 2, QN, N])
        hs = sb("hs", [128, HBUF, QN, N])
        YS = sb("YS", [128, 2, PADN])
        stats = sb("stats", [CT, NC4, 6])
        mv = sb("mv", [CT, NC4, 2])
        rstd = sb("rstd", [CT, NC4])
        HW = sb("HW", [CT, NC4, ROW])
        h2 = sb("h2", [128, PADN])
        score = sb("score", [CT, NC4, E])
        t1 = sb("t1", [CT, NC4, E])
        ext = sb("ext", [CT, NC4 * GR, 12])
        pairs = sb("pairs", [CT, NC4 * GR, 4, 8])
        gs = sb("gs", [CT, NC4, GR])
        cmp1 = sb("cmp1", [CT, NC4, GR, GR])
        cmp2 = sb("cmp2", [CT, NC4, GR, GR])
        rank = sb("rank", [CT, NC4 * GR])
        masked = sb("masked", [CT, NC4, E])
        top8 = sb("top8", [CT, NC4, 8])
        rest = sb("rest", [CT, NC4, E])
        sel = sb("sel", [CT, NC4, E])
        selh = sb("selh", [CT, NC4, E], bf16)
        wsum = sb("wsum", [CT, NC4])
        winv = sb("winv", [CT, NC4])
        pos = sb("pos", [CT, NC4, E])
        base = sb("base", [CT, E])
        least = sb("least", [1, 1])
        open_ = sb("open", [1, 1], i32)
        slotf = sb("slotf", [CT, NC4, 8])
        noslot = sb("noslot", [CT, NC4, 8])
        sloti = sb("sloti", [CT, NC4 * 8], i32)
        tokf = sb("tokf", [CT, NC4])
        toki = sb("toki", [CT, NC4], i32)
        unused = sb("unused", [128, SLOTS // 128], i32)
        zeros = sb("zeros", [128, ROW])
        eidx = sb("eidx", [128, 2, 4], i32)

        psS = ctx.enter_context(nc.psum_tensor("psS", [128, 4, 512], f32))
        psG = ctx.enter_context(nc.psum_tensor("psG", [128, 512], f32))
        psA = ctx.enter_context(nc.psum_tensor("psA", [128, 512], f32))
        psB = ctx.enter_context(nc.psum_tensor("psB", [128, 512], f32))
        psY = ctx.enter_context(nc.psum_tensor("psY", [128, 512], f32))
        AB = [psA, psB]
        OT_AT = NQ * HEADS * (HD + 1)

        names = ("open_ready loaded patches_loaded pool_ready unused_ready rows_zeroed rows_stored init_stored hw_ready "
                 "routed_stored q_waited ht_ready hw_free conv_done sent_all pair_free all_added fin_ready mul_done half_summed "
                 "summed slot_ready pool_waited sent_a sent_b slots_free e_out added act_setup consts_ready act_front x_ready "
                 "sq_ready ms_done rs_ready q_done q_ready k_done k_ready p_ready o_done inv_ready g_done ge_ready ge1_ready "
                 "gsig_ready act_back xz_done xc_ready xconv_ready sge_ready sg1_ready sgr_ready bc_done hi_ready dtin_ready "
                 "res_ready mid_ready dtp_done dt_ready abs_ready spe_ready sp_ready scan_ready da_ready mv_ready rstd_ready "
                 "act_route ht_done h2_ready lg_done gl_ready gm_ready score_ready act_waited xt_done xt_ready e13_done e_exp "
                 "e_one e_ln e_sig fin_mv fin_ln fin_rs dve_setup weights_ready dve_front hn_ready v_done v_ready s_done "
                 "max_done on_ready wo_done gs_ready u_done ff_ready down_done h_ready dve_back xs_ready bcs_ready dtm_ready "
                 "dve_waited acc_done bb_done zeroed y_done ys_ready m_done dve_route sel_ready pos_done flag_set e_mul e_act "
                 "e2_done fin_sub fin_stats pe_waited act_read pe_read pool_read q_read dve_read km0_ready km1_ready t_done "
                 "pt_ready ont_done ot_ready").split()
        (open_ready, loaded, patches_loaded, pool_ready, unused_ready, rows_zeroed, rows_stored, init_stored, hw_ready,
         routed_stored, q_waited, ht_ready, hw_free, conv_done, sent_all, pair_free, all_added, fin_ready, mul_done,
         half_summed, summed, slot_ready, pool_waited, sent_a, sent_b, slots_free, e_out, added, act_setup,
         consts_ready, act_front, x_ready, sq_ready, ms_done, rs_ready, q_done, q_ready, k_done, k_ready, p_ready,
         o_done, inv_ready, g_done, ge_ready, ge1_ready, gsig_ready, act_back, xz_done, xc_ready, xconv_ready,
         sge_ready, sg1_ready, sgr_ready, bc_done, hi_ready, dtin_ready, res_ready, mid_ready, dtp_done, dt_ready,
         abs_ready, spe_ready, sp_ready, scan_ready, da_ready, mv_ready, rstd_ready, act_route, ht_done, h2_ready,
         lg_done, gl_ready, gm_ready, score_ready, act_waited, xt_done, xt_ready, e13_done, e_exp, e_one, e_ln, e_sig,
         fin_mv, fin_ln, fin_rs, dve_setup, weights_ready, dve_front, hn_ready, v_done, v_ready, s_done, max_done,
         on_ready, wo_done, gs_ready, u_done, ff_ready, down_done, h_ready, dve_back, xs_ready, bcs_ready, dtm_ready,
         dve_waited, acc_done, bb_done, zeroed, y_done, ys_ready, m_done, dve_route, sel_ready, pos_done, flag_set,
         e_mul, e_act, e2_done, fin_sub, fin_stats, pe_waited, act_read, pe_read, pool_read, q_read, dve_read,
         km0_ready, km1_ready, t_done, pt_ready, ont_done, ot_ready) = (sem(n) for n in names)
        slots_loaded, w_loaded, gathered = ([sem(f"{n}{b}") for b in range(2)] for n in ("slots_loaded", "w_loaded", "gathered"))
        fin_loaded, fin_stored = ([sem(f"{n}{b}") for b in range(HBUF)] for n in ("fin_loaded", "fin_stored"))

        ex = [pat[:, 2 * b:2 * b + 2, :].rearrange("p k n -> p (k n)")[:, 0:4 * ROW].rearrange("p (c r) -> p c r", r=ROW) for b in range(2)]
        eo = [EF[:, :, :].rearrange("p f n -> p (f n)")[:, 512 * b:512 * b + 4 * D].rearrange("p (c r) -> p c r", r=D) for b in range(2)]
        ew = [dA[:, b, 0:2, :].rearrange("p a n -> p (a n)")[:, 0:4 * D].rearrange("p (h n) -> p h n", h=2) for b in range(2)]
        exT = KM[:, 0, 0:4, :].rearrange("p h t -> p (h t)")[:, 0:2 * CAP]
        ea = KM[0:MD, 1, 0:4, :].rearrange("p h t -> p (h t)")[:, 0:2 * CAP]
        FT = 8
        FINAL = [(t, min(FT, T - t)) for t in range(0, T, FT)]
        fbuf = [hs[:, b, :, :].rearrange("p a t -> p (a t)")[:, 0:FT * D].rearrange("p (t d) -> p t d", d=D) for b in range(HBUF)]
        fst = [dA[:, b, 0, 0:6 * FT].rearrange("p (t s) -> p t s", s=6) for b in range(2)]
        fmv = [dA[:, b, 1, 0:2 * FT].rearrange("p (t s) -> p t s", s=2) for b in range(2)]
        frs = [dA[:, b, 2, 0:FT] for b in range(2)]

        Xf = X[:, :, :].rearrange("p g t -> p (g t)")
        Hnf = Hn[:, :, :].rearrange("p g t -> p (g t)")
        Hnt = Hn[:, :, 0:T]

        def interleaved(units, i):
            at = [0]

            def until(stage, part=1, parts=1):
                k = STAGES.index(stage)
                before = SHARE[STAGES[k - 1]] if k else 0
                units_here = SHARE[stage] - before
                ahead = units_here if parts == 1 else 2 + -(-(units_here - 2) * (part - 1) // (parts - 1))
                end = before + max(0, min(units_here, ahead))
                while at[0] < end:
                    kind, *args = UNITS[at[0]]
                    at[0] += 1
                    if kind in units:
                        units[kind](i, *args)
            return until

        def loop(eng, front_half, units):
            def no_units(stage, part=1, parts=1):
                return None

            if front_half:
                front_half(0, no_units)
            with eng.Fori(0, STEPS - 1) as i:
                until = interleaved(units, i)
                if front_half:
                    front_half(i + 1, until)
                until(STAGES[-1])
            interleaved(units, STEPS - 1)(STAGES[-1])

        def chain(eng, done, per):
            n = [0]

            def link(ins, i):
                n[0] = n[0] % per + 1
                ins.then_inc(done, 1)
                eng.wait_ge(done, i * per + n[0])
            link.count = n
            return link

        def while_open(eng, i, waited, flag_read, route):
            eng.wait_ge(open_ready, i + 1)
            eng.sem_inc(waited, 1)
            flag = eng.value_load(open_[0:1, 0:1], min_val=0, max_val=1)
            eng.sem_inc(flag_read, 1)
            with eng.If(flag):
                route(i)

        block = ctx.enter_context(nc.Block())

        @block.sync
        def _(q):
            q.dma_start(wts[:, :], weights).then_inc(loaded, 16)
            q.dma_start(vec[:, :], vectors).then_inc(loaded, 16)
            q.dma_start(cst[:, :], consts).then_inc(loaded, 16)
            q.dma_start(hs[0:96, 0:3, :, :].rearrange("p a b t -> p (a b t)")[:, 0:2 * NS * D], bcsel_d).then_inc(loaded, 16)
            q.dma_start(gateb[:, :], gate_b.rearrange("(a e) -> a e", a=1).to_broadcast([128, E])).then_inc(loaded, 16)
            q.dma_start(pat[:, :, :], patches[0]).then_inc(patches_loaded, 16)
            q.wait_ge(pool_ready, 13)
            q.wait_ge(unused_ready, 1)
            q.dma_start(rows_d.rearrange("(p t) r -> p t r", p=ZP), zeros[0:ZP, :].unsqueeze(1).to_broadcast([ZP, (TOK + PAD) // ZP, ROW])).then_inc(rows_zeroed, 16)
            q.dma_start(sum_d[TOK:TOK + PAD, :].rearrange("(c p) r -> p c r", c=2), zeros[:, 0:D].unsqueeze(1).to_broadcast([128, 2, D])).then_inc(rows_stored, 16)
            q.dma_start(slot_d.rearrange("(p a) o -> p (a o)", p=128), unused[:, :]).then_inc(init_stored, 16)

            def route(i):
                q.wait_ge(rows_zeroed, 16)
                q.wait_ge(hw_ready, i + 1)
                for lo, nch, n in ((0, NC4 - 1, CT), (NC4 - 1, 1, N - (NC4 - 1) * CT)):
                    dst = rows_d[bass.ds(i * N + lo * CT, nch * n), :].rearrange("(c p) r -> p c r", p=n)
                    q.dma_start(dst, HW[0:n, lo:lo + nch, :]).then_inc(routed_stored, 16)
                q.wait_ge(routed_stored, i * 32 + 32)
                q.sem_inc(q_waited, 1)

            def store(b):
                q.wait_ge(ht_ready, b + 1)
                for lo, nch, n in ((0, NC4 - 1, CT), (NC4 - 1, 1, N - (NC4 - 1) * CT)):
                    dst = sum_d[bass.ds(b * N + lo * CT, nch * n), :].rearrange("(c p) r -> p c r", p=n)
                    q.dma_start(dst, HW[0:n, lo:lo + nch, 0:D]).then_inc(rows_stored, 16)
                while_open(q, b, q_waited, q_read, route)
                q.sem_inc(hw_free, 1)

            def patches_of(i):
                q.wait_ge(conv_done, i)
                q.dma_start(pat[:, :, :], patches[bass.ds(i, 1)].rearrange("o p k n -> (o p) k n")).then_inc(patches_loaded, 16)

            q.sem_inc(hw_free, 1)
            with q.Fori(0, STEPS - 1) as i:
                patches_of(i + 1)
                store(i)
            store(STEPS - 1)
            q.wait_ge(sent_all, 1)
            q.wait_ge(rows_stored, 16 + 32 * STEPS)
            with q.Fori(0, E // 4) as e:
                for b in range(2):
                    q.wait_ge(pair_free, e * 2 + b + 1)
                    first = e * 4 + 2 * b
                    q.dma_start(eidx[:, b, :].rearrange("p (h k) -> p h k", h=2), slot_d[bass.ds(first * CAP, 2 * CAP), :].rearrange("(h p k) o -> p h (k o)", h=2, p=128)).then_inc(slots_loaded[b], 16)
                    q.dma_start(ew[b][:, :, 0:D], w13[bass.ds(first, 2)].rearrange("h p n -> p h n")).then_inc(w_loaded[b], 16)
                    q.dma_start(ew[b][0:MD, :, D:2 * D], w2[bass.ds(first, 2)].rearrange("h p n -> p h n")).then_inc(w_loaded[b], 16)
            q.wait_ge(all_added, 1)
            r3 = sum_d[0:TOK, :].rearrange("(p t) d -> p t d", p=B)

            def load(n):
                t, m = FINAL[n]
                if n >= HBUF:
                    q.wait_ge(fin_stored[n % HBUF], 16 * (n // HBUF))
                q.dma_start(fbuf[n % HBUF][0:B, 0:m, :], r3[:, t:t + m, :]).then_inc(fin_loaded[n % HBUF], 16)

            for n in range(HBUF - 1):
                load(n)
            for n, (t, m) in enumerate(FINAL):
                if n + HBUF - 1 < len(FINAL):
                    load(n + HBUF - 1)
                q.wait_ge(fin_ready, n + 1)
                q.dma_start(out[:, t:t + m, :], fbuf[n % HBUF][0:B, 0:m, :]).then_inc(fin_stored[n % HBUF], 16)
            for b in range(HBUF):
                q.wait_ge(fin_stored[b], 16 * len(FINAL[b::HBUF]))

        @block.gpsimd
        def _(pool):
            nc.gpsimd.memset(V[:, :, :, :], 0.0).then_inc(pool_ready, 1)
            pool.wait_ge(pool_ready, 1)
            nc.gpsimd.memset(V[:, :, :, HD:HD + 1], 1.0).then_inc(pool_ready, 1)
            nc.gpsimd.memset(Hn[:, :, T:TP], 0.0).then_inc(pool_ready, 1)
            nc.gpsimd.memset(P[:, :, T:TP], 0.0).then_inc(pool_ready, 1)
            nc.gpsimd.memset(XC[:, :, :, :], 0.0).then_inc(pool_ready, 1)
            nc.gpsimd.memset(HW[:, :, :], 0.0).then_inc(pool_ready, 1)
            nc.gpsimd.memset(h2[:, :], 0.0).then_inc(pool_ready, 1)
            nc.gpsimd.memset(zeros[:, :], 0.0).then_inc(pool_ready, 1)
            nc.gpsimd.memset(epsr[:, 0:1], EPS_RMS).then_inc(pool_ready, 1)
            nc.gpsimd.memset(epsr[:, 1:2], EPS_LN).then_inc(pool_ready, 1)
            nc.gpsimd.memset(base[:, :], 0.0).then_inc(pool_ready, 1)
            nc.gpsimd.memset(H[:, N:PADN], 0.0).then_inc(pool_ready, 1)
            nc.gpsimd.memset(YS[:, :, N:PADN], 0.0).then_inc(pool_ready, 1)
            pool.wait_ge(init_stored, 16)

            def sum_(i, g):
                pool.wait_ge(mul_done, i * MULS + (g + 1) * 2 * QN)
                nc.gpsimd.tensor_tensor(hs[:, g % HBUF, 0:2, :], hs[:, g % HBUF, 0:2, :], hs[:, g % HBUF, 2:4, :], ALU.add).then_inc(half_summed, 1)
                pool.wait_ge(half_summed, i * QUARTERS + g + 1)
                nc.gpsimd.tensor_tensor(hs[:, g % HBUF, 0, :], hs[:, g % HBUF, 0, :], hs[:, g % HBUF, 1, :], ALU.add).then_inc(summed, 1)

            def route(i):
                pool.wait_ge(slot_ready, i + 1)
                pool.sem_inc(pool_waited, 1)
                for j in range(NC4 * 8):
                    nc.gpsimd.indirect_dma_start(
                        out=slot_d[:, :], out_offset=bass.IndirectOffsetOnAxis(ap=sloti[:, j:j + 1], axis=0),
                        in_=toki[:, j // 8:j // 8 + 1], in_offset=None,
                        bounds_check=SLOTS - 1, oob_is_err=False).then_inc(sent_a if j % 2 else sent_b, 16)
                pool.wait_ge(sent_a, i * 256 + 256)
                pool.wait_ge(sent_b, i * 256 + 256)
                pool.sem_inc(pool_waited, 1)

            def route_unit(i):
                while_open(pool, i, pool_waited, pool_read, route)
                pool.sem_inc(slots_free, 1)

            def front_half(i, until):
                for l in range(2):
                    until(f"qkv.{l}")
                    pool.wait_ge(k_ready, i * 2 + l + 1)
                    nc.gpsimd.tensor_tensor(KM[:, 1, :, :], K[:, 1:2, :].to_broadcast([128, HEADS, TP]), c("heads").unsqueeze(2).to_broadcast([128, HEADS, TP]), ALU.mult).then_inc(km1_ready, 1)

            pool.sem_inc(slots_free, 1)
            loop(pool, front_half, {"sum": sum_, "route": route_unit})
            pool.sem_inc(sent_all, 1)
            pool.wait_ge(rows_stored, 16 + 32 * STEPS)
            pool.sem_inc(pair_free, 2)

            def gather(e, b):
                pool.wait_ge(slots_loaded[b], e * 16 + 16)
                pool.sem_inc(pool_waited, 1)
                for k in range(4):
                    nc.gpsimd.indirect_dma_start(
                        out=ex[b][:, k, :], out_offset=None, in_=rows_d[:, :],
                        in_offset=bass.IndirectOffsetOnAxis(ap=eidx[:, b, k:k + 1], axis=0)).then_inc(gathered[b], 16)

            def add(p, b):
                pool.wait_ge(e_out, p + 1)
                pool.sem_inc(pool_waited, 1)
                for h in range(2):
                    for k in range(2):
                        nc.gpsimd.indirect_dma_start(
                            out=sum_d[:, :], out_offset=bass.IndirectOffsetOnAxis(ap=eidx[:, b, 2 * h + k:2 * h + k + 1], axis=0),
                            in_=eo[b][:, 2 * h + k, :], in_offset=None, compute_op=ALU.add).then_inc(added, 16)
                    pool.wait_ge(added, p * 64 + 32 * h + 32)
                    pool.sem_inc(pool_waited, 1)
                pool.sem_inc(pair_free, 1)

            gather(0, 0)
            with pool.Fori(0, E // 4 - 1) as e:
                gather(e, 1)
                add(2 * e, 0)
                gather(e + 1, 0)
                add(2 * e + 1, 1)
            gather(E // 4 - 1, 1)
            add(E // 2 - 2, 0)
            add(E // 2 - 1, 1)
            pool.sem_inc(all_added, 1)

        @block.scalar
        def _(act):
            act.preload_act_table_set("natural_log_exp_and_others")
            setup = chain(act, act_setup, 100)
            act.wait_ge(loaded, 16 * 5)
            act.wait_ge(pool_ready, 13)
            nc.scalar.activation(bcsel[:, :, :], hs[0:96, :, :, :].rearrange("p a b t -> p (a b t)")[:, 0:2 * NS * D].rearrange("p (n d) -> p n d", d=D), ACT.Copy)
            nc.scalar.activation(before_h[:, :], c("before"), ACT.Copy)
            nc.scalar.activation(ones_h[:, :], c("ones"), ACT.Copy)
            for n, d in enumerate("fb"):
                setup(nc.scalar.activation(aneg[:, n, :], v(f"alog{d}"), ACT.Exp), 0)
            setup(nc.scalar.activation(aneg[:, :, :], aneg[:, :, :], ACT.Copy, scale=-1.0), 0)
            nc.scalar.activation(epsr[:, :], epsr[:, :], ACT.Copy).then_inc(consts_ready, 1)

            front = chain(act, act_front, ACT_FRONT)

            def square(i, m):
                act.wait_ge(x_ready, i * 5 + 1 + m)
                nc.scalar.activation(sq[:, :], Xf, ACT.Square).then_inc(sq_ready, 1)

            def root(i, m):
                act.wait_ge(ms_done, i * 5 + m + 1)
                front(nc.scalar.activation(rs[:, :], psG[:, 0:N], ACT.Ln, bias=epsr[:, 0:1]), i)
                nc.scalar.activation(rs[:, :], rs[:, :], ACT.Exp, scale=-0.5).then_inc(rs_ready, 1)

            def front_half(i, until):
                until("conv")
                square(i, 0)
                for l in range(2):
                    s = f".{l}"
                    until("norm" + s)
                    root(i, 2 * l)
                    until("qkv" + s)
                    act.wait_ge(q_done, i * 2 + l + 1)
                    nc.scalar.activation(Q[:, :, :].rearrange("p g t -> p (g t)"), psS[:, 0, 0:G * TP], ACT.Copy, scale=-(HD ** -0.5)).then_inc(q_ready, 1)
                    act.wait_ge(k_done, i * 2 + l + 1)
                    nc.scalar.activation(K[:, :, :].rearrange("p g t -> p (g t)"), psS[:, 1, 0:G * TP], ACT.Copy).then_inc(k_ready, 1)
                    for n in range(len(CHUNKS)):
                        k = i * 16 + l * 8 + n * 2
                        until(f"score{n}" + s)
                        for h in range(2):
                            act.wait_ge(max_done, k + h + 1)
                            for m in range(4 * h, 4 * h + 4):
                                last = nc.scalar.activation(P[:, m, 0:T], psS[0:CT, m // 2, m % 2 * T:(m % 2 + 1) * T], ACT.Exp, bias=least_s[:, m:m + 1], scale=-1.0)
                            last.then_inc(p_ready, 1)
                        until(f"turn{n}" + s)
                        if n:
                            act.wait_ge(o_done, i * 8 + l * 4 + n)
                        for h in range(2):
                            act.wait_ge(t_done, k + h + 1)
                            nc.scalar.activation(PT[:, 4 * h:4 * h + 4, :, :].rearrange("p (j e) c t -> p j (e c t)", e=2), psS[0:CT, 2 * h:2 * h + 2, 0:2 * TP], ACT.Copy).then_inc(pt_ready, 1)
                    until("wo" + s)
                    square(i, 2 * l + 1)
                    until("norm2" + s)
                    root(i, 2 * l + 1)
                    until("gate" + s)
                    act.wait_ge(g_done, i * 2 + l + 1)
                    nc.scalar.activation(EF[0:FW, :, :], psS[0:FW, 0:FC, 0:N], ACT.Exp, scale=-1.0).then_inc(ge_ready, 1)
                    until("sig" + s)
                    act.wait_ge(ge1_ready, i * 2 + l + 1)
                    front(nc.scalar.activation(EF[0:FW, :, :], EF[0:FW, :, :], ACT.Ln), i)
                    nc.scalar.activation(EF[0:FW, :, :], EF[0:FW, :, :], ACT.Exp, scale=-1.0).then_inc(gsig_ready, 1)
                    until("down" + s)
                    square(i, 2 * l + 2)
                until("normf")
                root(i, 4)

            back = chain(act, act_back, ACT_BACK)

            def project(i, d):
                act.wait_ge(xz_done, i * 2 + d + 1)
                nc.scalar.activation(XC[:, d, :, TAPS - 1:XW], psA[:, 0:N].rearrange("p (g t) -> p g t", g=G), ACT.Copy)
                nc.scalar.activation(XZ[:, d, 1, :], psB[:, 0:N], ACT.Copy).then_inc(xc_ready, 1)

            def sigmoid(i, d):
                act.wait_ge(xconv_ready, i * 2 + d + 1)
                nc.scalar.activation(SG[:, d, :, :], XZ[:, d, :, :], ACT.Exp, scale=-1.0).then_inc(sge_ready, 1)

            def gate(i, d):
                act.wait_ge(sg1_ready, i * 2 + d + 1)
                back(nc.scalar.activation(SG[:, d, :, :], SG[:, d, :, :], ACT.Ln), i)
                nc.scalar.activation(SG[:, d, :, :], SG[:, d, :, :], ACT.Exp, scale=-1.0).then_inc(sgr_ready, 1)

            def split(i, d):
                k = i * 2 + d + 1
                act.wait_ge(bc_done, k)
                nc.scalar.activation(hi[:, d, :], psA[0:96, 0:N], ACT.Copy).then_inc(hi_ready, 1)
                nc.scalar.activation(dtin[:, d, :], psY[0:DTR, 0:N], ACT.Copy).then_inc(dtin_ready, 1)
                act.wait_ge(res_ready, k)
                nc.scalar.activation(mid[:, :], res[:, :], ACT.Copy).then_inc(mid_ready, 1)

            def step_size(i, d):
                k = i * 2 + d + 1
                act.wait_ge(dtp_done, k)
                if d:
                    act.wait_ge(dt_ready, k - 1)
                nc.scalar.activation(sp[:, :], psY[:, 0:N], ACT.Abs, bias=v("bdt" + "fb"[d])).then_inc(abs_ready, 1)
                act.wait_ge(abs_ready, k)
                nc.scalar.activation(sp[:, :], sp[:, :], ACT.Exp, scale=-1.0).then_inc(spe_ready, 1)
                act.wait_ge(spe_ready, k)
                nc.scalar.activation(spl[:, :], sp[:, :], ACT.Ln, bias=1.0).then_inc(sp_ready, 1)

            def decay(i, g):
                d = g // (QUARTERS // 2)
                if g % (QUARTERS // 2) < 2:
                    act.wait_ge(dt_ready, i * 2 + d + 1)
                if g >= 2:
                    act.wait_ge(scan_ready, i * QUARTERS + g - 1)
                for k in range(QN):
                    n = g % (QUARTERS // 2) * QN + k
                    last = nc.scalar.activation(dA[:, g % 2, k, :], dt_[:, d, :], ACT.Exp, scale=aneg[:, d, n:n + 1])
                last.then_inc(da_ready, 1)

            def merge(i):
                act.wait_ge(mv_ready, i + 1)
                back(nc.scalar.activation(rstd[:, :], mv[:, :, 1], ACT.Ln, bias=epsr[0:CT, 1:2]), i)
                nc.scalar.activation(rstd[:, :], rstd[:, :], ACT.Exp, scale=-0.5).then_inc(rstd_ready, 1)

            routing = chain(act, act_route, 2)

            def route(i):
                act.wait_ge(ht_done, i + 1)
                nc.scalar.activation(h2[:, :], psB[:, 0:PADN], ACT.Copy).then_inc(h2_ready, 1)
                act.wait_ge(lg_done, i + 1)
                flat = t1[:, :, :].rearrange("p c e -> p (c e)")
                routing(nc.scalar.activation(flat, psA[0:CT, 0:NC4 * E], ACT.Abs), i)
                routing(nc.scalar.activation(flat, flat, ACT.Exp, scale=-1.0), i)
                nc.scalar.activation(flat, flat, ACT.Ln, bias=1.0).then_inc(gl_ready, 1)
                act.wait_ge(gm_ready, i + 1)
                nc.scalar.activation(score[:, :, :], t1[:, :, :], ACT.Exp).then_inc(score_ready, 1)

            loop(act, front_half, {
                "project": project, "sigmoid": sigmoid, "gate": gate, "split": split, "dt": step_size, "decay": decay,
                "merge": merge, "route": lambda i: while_open(act, i, act_waited, act_read, route)})
            assert front.count[0] == ACT_FRONT and back.count[0] == ACT_BACK, (front.count, back.count)

            with act.Fori(0, E // 2) as p:
                act.wait_ge(xt_done, p + 1)
                nc.scalar.activation(exT, psS[:, 0, 0:2 * CAP], ACT.Copy).then_inc(xt_ready, 1)
                act.wait_ge(e13_done, p + 1)
                nc.scalar.activation(ea, psS[0:MD, 1, 0:2 * CAP], ACT.Exp, scale=-1.0).then_inc(e_exp, 1)
                act.wait_ge(e_one, p + 1)
                nc.scalar.activation(ea, ea, ACT.Ln).then_inc(e_ln, 1)
                act.wait_ge(e_ln, p + 1)
                nc.scalar.activation(ea, ea, ACT.Exp, scale=-1.0).then_inc(e_sig, 1)
            for n, (t, m) in enumerate(FINAL):
                act.wait_ge(fin_mv, n + 1)
                nc.scalar.activation(frs[n % 2][0:B, 0:m], fmv[n % 2][0:B, 0:m, 1], ACT.Ln, bias=epsr[0:B, 1:2]).then_inc(fin_ln, 1)
                act.wait_ge(fin_ln, n + 1)
                nc.scalar.activation(frs[n % 2][0:B, 0:m], frs[n % 2][0:B, 0:m], ACT.Exp, scale=-0.5).then_inc(fin_rs, 1)

        @block.vector
        def _(dve):
            setup = chain(dve, dve_setup, 100)
            dve.wait_ge(loaded, 16 * 5)
            for l in range(2):
                for n in ("q", "k", "v"):
                    nc.vector.tensor_scalar(w(f"{n}{l}"), w(f"{n}{l}"), v(f"ln1{l}"), None, ALU.mult)
                for n in ("gate", "up"):
                    nc.vector.tensor_scalar(w(f"{n}{l}"), w(f"{n}{l}"), v(f"ln2{l}"), None, ALU.mult)
            for n, d in enumerate("fb"):
                nc.vector.tensor_scalar(dskip[:, n, :], c("ident"), v(f"dskip{d}"), None, ALU.mult)
            nc.vector.tensor_scalar(posb[:, :], v("pos"), v("convb"), None, ALU.add)
            nc.vector.tensor_tensor(cls0[:, :], v("cls"), v("pos", 0, 1), ALU.add)
            nc.vector.tensor_copy(tokf[:, :], c("tok0")[0:CT, :])
            setup(nc.vector.tensor_copy(unused[:, :], c("unused")), 0)
            nc.vector.tensor_copy(open_[:, :], c("ones")[0:1, 0:1]).then_inc(open_ready, 1)
            dve.wait_ge(pool_ready, 13)
            dve.wait_ge(consts_ready, 1)
            dve.sem_inc(unused_ready, 1)
            dve.sem_inc(weights_ready, 1)

            front = chain(dve, dve_front, DVE_FRONT)

            def apply_norm(i, m):
                dve.wait_ge(rs_ready, i * 5 + m + 1)
                nc.vector.tensor_tensor(Hnt, X[:, :, :], rs[:, :].rearrange("p (g t) -> p g t", g=G), ALU.mult).then_inc(hn_ready, 1)

            def front_half(i, until):
                until("conv")
                dve.wait_ge(conv_done, i + 1)
                front(nc.vector.tensor_tensor(X[:, :, 1:T], psG[:, 0:G * NP].rearrange("p (g t) -> p g t", g=G), posb[:, 1:T].unsqueeze(1).to_broadcast([128, G, NP]), ALU.add), i)
                nc.vector.tensor_copy(X[:, :, 0:1], cls0[:, :].unsqueeze(1).to_broadcast([128, G, 1])).then_inc(x_ready, 1)
                for l in range(2):
                    s = f".{l}"
                    until("norm" + s)
                    apply_norm(i, 2 * l)
                    until("qkv" + s)
                    dve.wait_ge(k_ready, i * 2 + l + 1)
                    nc.vector.tensor_tensor(KM[:, 0, :, :], K[:, 0:1, :].to_broadcast([128, HEADS, TP]), c("heads").unsqueeze(2).to_broadcast([128, HEADS, TP]), ALU.mult).then_inc(km0_ready, 1)
                    dve.wait_ge(v_done, i * 2 + l + 1)
                    nc.vector.tensor_copy(V[:, :, :, 0:HD], psG[0:CT, :].rearrange("p (c h d) -> p c h d", c=G * NQ, h=HEADS)).then_inc(v_ready, 1)

                    def divide(n):
                        k = i * 8 + l * 4 + n + 1
                        at = n % 2 * HEADS * (HD + 1)
                        sums = psG[0:CT, at:at + HEADS * (HD + 1)].rearrange("p (h d) -> p h d", h=HEADS)
                        dve.wait_ge(o_done, k)
                        nc.vector.reciprocal(rden[:, :], sums[:, :, HD]).then_inc(inv_ready, 1)
                        dve.wait_ge(inv_ready, k)
                        nc.vector.tensor_tensor(ON[:, :, :], sums[:, :, 0:HD], rden[:, :].unsqueeze(2).to_broadcast([CT, HEADS, HD]), ALU.mult).then_inc(on_ready, 1)

                    def take_turned(n):
                        b, q = CHUNKS[n]
                        dve.wait_ge(ont_done, i * 8 + l * 4 + n + 1)
                        nc.vector.tensor_copy(OT[:, b, q * CT:(q + 1) * CT], psG[:, OT_AT + q * CT:OT_AT + (q + 1) * CT]).then_inc(ot_ready, 1)

                    for n in range(len(CHUNKS)):
                        until(f"score{n}" + s)
                        for h in range(2):
                            dve.wait_ge(s_done, i * 16 + l * 8 + n * 2 + h + 1)
                            nc.vector.tensor_reduce(least_s[:, 4 * h:4 * h + 4], psS[0:CT, 2 * h:2 * h + 2, 0:2 * T].rearrange("p j (e t) -> p j e t", e=2), axis=AX, op=ALU.min).then_inc(max_done, 1)
                        if n:
                            divide(n - 1)
                        until(f"turn{n}" + s)
                        if n:
                            take_turned(n - 1)
                    until("value" + s)
                    divide(len(CHUNKS) - 1)
                    until("turnback" + s)
                    take_turned(len(CHUNKS) - 1)
                    until("wo" + s)
                    dve.wait_ge(wo_done, i * 2 + l + 1)
                    nc.vector.tensor_tensor(Xf, Xf, psG[:, 0:N], ALU.add).then_inc(x_ready, 1)
                    until("norm2" + s)
                    apply_norm(i, 2 * l + 1)
                    until("gate" + s)
                    dve.wait_ge(ge_ready, i * 2 + l + 1)
                    nc.vector.tensor_scalar(EF[0:FW, :, :], EF[0:FW, :, :], EXP_MAX, 1.0, ALU.min, ALU.add).then_inc(ge1_ready, 1)
                    until("sig" + s)
                    dve.wait_ge(gsig_ready, i * 2 + l + 1)
                    nc.vector.tensor_tensor(EF[0:FW, :, :], EF[0:FW, :, :], psS[0:FW, 0:FC, 0:N], ALU.mult).then_inc(gs_ready, 1)
                    until("up" + s)
                    dve.wait_ge(u_done, i * 2 + l + 1)
                    nc.vector.tensor_tensor(EF[0:FW, :, :], EF[0:FW, :, :], psS[0:FW, 0:FC, 0:N], ALU.mult).then_inc(ff_ready, 1)
                    until("down" + s)
                    dve.wait_ge(down_done, i * 2 + l + 1)
                    nc.vector.tensor_tensor(Xf, Xf, psG[:, 0:N], ALU.add).then_inc(x_ready, 1)
                until("normf")
                dve.wait_ge(rs_ready, i * 5 + 5)
                front(nc.vector.scalar_tensor_tensor(out=H[:, 0:N], in0=Xf, scalar=v("lnf"), in1=rs[:, :], op0=ALU.mult, op1=ALU.mult), i)
                nc.vector.tensor_copy(Hr[:, :], H[:, 0:N][:, ::-1]).then_inc(h_ready, 1)

            back = chain(dve, dve_back, DVE_BACK)

            def conv(i, d):
                dve.wait_ge(xc_ready, i * 2 + d + 1)
                xconv = XZ[:, d, 0, :].rearrange("p (g t) -> p g t", g=G)
                back(nc.vector.tensor_scalar(xconv, XC[:, d, :, 0:T], v("taps" + "fb"[d], 0, 1), v("bconv" + "fb"[d]), ALU.mult, ALU.add), i)
                for tap in range(1, TAPS):
                    ins = nc.vector.scalar_tensor_tensor(out=xconv, in0=XC[:, d, :, tap:tap + T], scalar=v("taps" + "fb"[d], tap, tap + 1), in1=xconv, op0=ALU.mult, op1=ALU.add)
                    if tap < TAPS - 1:
                        back(ins, i)
                    else:
                        ins.then_inc(xconv_ready, 1)

            def sigmoid(i, d):
                dve.wait_ge(sge_ready, i * 2 + d + 1)
                nc.vector.tensor_scalar(SG[:, d, :, :], SG[:, d, :, :], EXP_MAX, 1.0, ALU.min, ALU.add).then_inc(sg1_ready, 1)

            def gate(i, d):
                dve.wait_ge(sgr_ready, i * 2 + d + 1)
                nc.vector.tensor_tensor(XZ[:, d, :, :], XZ[:, d, :, :], SG[:, d, :, :], ALU.mult).then_inc(xs_ready, 1)

            def split(i, d):
                if d:
                    dve.wait_ge(bcs_ready, i * 2 + 1)
                dve.wait_ge(hi_ready, i * 2 + d + 1)
                nc.vector.scalar_tensor_tensor(out=res[:, :], in0=hi[:, d, :], scalar=c("part1")[0:96, :], in1=psA[0:96, 0:N], op0=ALU.mult, op1=ALU.add).then_inc(res_ready, 1)
                dve.wait_ge(mid_ready, i * 2 + d + 1)
                nc.vector.scalar_tensor_tensor(out=bc[:, d, :], in0=mid[:, :], scalar=c("part2")[0:96, :], in1=res[:, :], op0=ALU.mult, op1=ALU.add).then_inc(bcs_ready, 1)

            def step_size(i, d):
                k = i * 2 + d + 1
                dve.wait_ge(abs_ready, k)
                nc.vector.tensor_scalar(dt_[:, d, :], psY[:, 0:N], v("bdt" + "fb"[d]), 0.0, ALU.add, ALU.max).then_inc(dtm_ready, 1)
                dve.wait_ge(spe_ready, k)
                nc.vector.tensor_scalar(small[:, :], sp[:, :], LOG1P_SERIES, None, ALU.is_lt)
                back(nc.vector.tensor_scalar(u[:, d, :], sp[:, :], 1 / 3, -0.5, ALU.mult, ALU.add), i)
                back(nc.vector.tensor_tensor(u[:, d, :], u[:, d, :], sp[:, :], ALU.mult), i)
                dve.wait_ge(sp_ready, k)
                back(nc.vector.scalar_tensor_tensor(out=u[:, d, :], in0=u[:, d, :], scalar=1.0, in1=sp[:, :], op0=ALU.add, op1=ALU.mult), i)
                dve.sem_inc(dve_waited, 1)
                back(nc.vector.copy_predicated(spl[:, :], small[:, :], u[:, d, :]), i)
                dve.wait_ge(dtm_ready, k)
                nc.vector.tensor_tensor(dt_[:, d, :], dt_[:, d, :], spl[:, :], ALU.add).then_inc(dt_ready, 1)
                dve.wait_ge(dt_ready, k)
                back(nc.vector.tensor_tensor(u[:, d, :], dt_[:, d, :], XZ[:, d, 0, :], ALU.mult), i)

            def input_(i, g, k):
                m = 2 * QN * g + k
                if k == 0 and g >= HBUF:
                    dve.wait_ge(acc_done, i * QUARTERS + g - HBUF + 1)
                dve.wait_ge(bb_done, i * MULS + m + 1)
                nc.vector.tensor_tensor(hs[:, g % HBUF, k, :], u[:, g // (QUARTERS // 2), :], AB[m % 2][:, 0:N], ALU.mult).then_inc(mul_done, 1)

            def scan(i, g):
                dve.wait_ge(da_ready, i * QUARTERS + g + 1)
                nc.vector.memset(dA[:, g % 2, :, :].rearrange("p n (g t) -> p (n g) t", g=G)[:, :, 0:1], 0.0).then_inc(zeroed, 1)
                dve.wait_ge(zeroed, i * QUARTERS + g + 1)
                dve.wait_ge(mul_done, i * MULS + 2 * QN * g + QN)
                h = hs[:, g % HBUF, :, :].rearrange("p n t -> p (n t)")
                nc.vector.tensor_tensor_scan(h, dA[:, g % 2, :, :].rearrange("p n t -> p (n t)"), h, 0.0, ALU.mult, ALU.add).then_inc(scan_ready, 1)

            def output(i, g, k):
                m = 2 * QN * g + QN + k
                if k == 0:
                    dve.wait_ge(scan_ready, i * QUARTERS + g + 1)
                dve.wait_ge(bb_done, i * MULS + m + 1)
                nc.vector.tensor_tensor(hs[:, g % HBUF, k, :], hs[:, g % HBUF, k, :], AB[m % 2][:, 0:N], ALU.mult).then_inc(mul_done, 1)

            def sum_(i, g):
                if g % (QUARTERS // 2) == QUARTERS // 2 - 1:
                    d = g // (QUARTERS // 2)
                    dve.wait_ge(y_done, i * 2 + d + 1)
                    nc.vector.tensor_tensor(YS[:, d, 0:N][:, ::-1] if d else YS[:, d, 0:N], psY[:, 0:N], XZ[:, d, 1, :], ALU.mult).then_inc(ys_ready, 1)

            def merge(i):
                dve.wait_ge(m_done, i + 1)
                tokens = psA[0:CT, 0:NC4 * D].rearrange("p (c d) -> p c d", c=NC4)
                for q in range(NC4):
                    last = nc.vector.bn_stats(stats[:, q, :], tokens[:, q, :])
                back(last, i)
                dve.sem_inc(dve_waited, 1)
                for q in range(NC4):
                    last = nc.vector.bn_aggr(mv[:, q, :], stats[:, q, :])
                last.then_inc(mv_ready, 1)
                dve.wait_ge(mv_ready, i + 1)
                dve.wait_ge(rstd_ready, i + 1)
                dve.wait_ge(rows_stored, i * 32 + 16)
                dve.wait_ge(hw_free, i + 1)
                for q in range(NC4):
                    last = nc.vector.tensor_scalar(HW[:, q, 0:D], tokens[:, q, :], mv[:, q, 0:1], rstd[:, q:q + 1], ALU.subtract, ALU.mult)
                last.then_inc(ht_ready, 1)

            routing = chain(dve, dve_route, DVE_ROUTE)

            def route(i):
                dve.wait_ge(gl_ready, i + 1)
                nc.vector.scalar_tensor_tensor(out=t1[:, :, :].rearrange("p c e -> p (c e)"), in0=psA[0:CT, 0:NC4 * E], scalar=0.0, in1=t1[:, :, :].rearrange("p c e -> p (c e)"), op0=ALU.min, op1=ALU.subtract).then_inc(gm_ready, 1)
                dve.wait_ge(score_ready, i + 1)
                routing(nc.vector.tensor_tensor(ext[:, :, 0:8].rearrange("p (c g) k -> p c g k", c=NC4), score[:, :, :].rearrange("p c (g k) -> p c g k", k=8), gateb[0:CT, :].rearrange("p (g k) -> p g k", k=8).unsqueeze(1).to_broadcast([CT, NC4, GR, 8]), ALU.add), i)
                routing(nc.vector.tensor_copy(ext[:, :, 8:12], ext[:, :, 0:4]), i)
                for s in range(1, 5):
                    last = nc.vector.tensor_tensor(pairs[:, :, s - 1, :], ext[:, :, 0:8], ext[:, :, s:s + 8], ALU.add)
                routing(last, i)
                routing(nc.vector.tensor_reduce(gs[:, :, :].rearrange("p c g -> p (c g)"), pairs[:, :, :, :].rearrange("p m s k -> p m (s k)"), axis=AX, op=ALU.max), i)
                them = gs[:, :, :].unsqueeze(2).to_broadcast([CT, NC4, GR, GR])
                mine = gs[:, :, :].unsqueeze(3).to_broadcast([CT, NC4, GR, GR])
                routing(nc.vector.tensor_tensor(cmp1[:, :, :, :], them, mine, ALU.is_gt), i)
                routing(nc.vector.tensor_tensor(cmp2[:, :, :, :], them, mine, ALU.is_equal), i)
                fore = c("groupbefore")[0:CT, :].unsqueeze(1).to_broadcast([CT, NC4, GR * GR])
                c1, c2 = (x[:, :, :, :].rearrange("p c g h -> p c (g h)") for x in (cmp1, cmp2))
                routing(nc.vector.tensor_tensor(c2, c2, fore, ALU.mult), i)
                routing(nc.vector.tensor_tensor(c1, c1, c2, ALU.add), i)
                routing(nc.vector.tensor_reduce(rank[:, :], cmp1[:, :, :, :].rearrange("p c g h -> p (c g) h"), axis=AX, op=ALU.add), i)
                routing(nc.vector.tensor_scalar(rank[:, :], rank[:, :], float(TOPG), -BIG, ALU.is_ge, ALU.mult), i)
                m8 = masked[:, :, :].rearrange("p c (g k) -> p (c g) k", k=8)
                routing(nc.vector.tensor_tensor(m8, ext[:, :, 0:8], rank[:, :].unsqueeze(2).to_broadcast([CT, NC4 * GR, 8]), ALU.add), i)
                dve.sem_inc(dve_waited, 1)
                for q in range(NC4):
                    last = nc.vector.max(top8[:, q, :], masked[:, q, :])
                routing(last, i)
                dve.sem_inc(dve_waited, 1)
                for q in range(NC4):
                    last = nc.vector.match_replace(out=rest[:, q, :], in_to_replace=top8[:, q, :], in_values=masked[:, q, :], imm_value=-3e38)
                routing(last, i)
                routing(nc.vector.tensor_tensor(sel[:, :, :], rest[:, :, :], masked[:, :, :], ALU.not_equal), i)
                routing(nc.vector.tensor_tensor(score[:, :, :], score[:, :, :], sel[:, :, :], ALU.mult), i)
                routing(nc.vector.tensor_reduce(wsum[:, :], score[:, :, :], axis=AX, op=ALU.add), i)
                routing(nc.vector.reciprocal(winv[:, :], wsum[:, :]), i)
                routing(nc.vector.tensor_tensor(sel[:, :, :], sel[:, :, :], c("valid")[0:CT, :].unsqueeze(2).to_broadcast([CT, NC4, E]), ALU.mult), i)
                nc.vector.tensor_copy(selh[:, :, :], sel[:, :, :]).then_inc(sel_ready, 1)
                nc.vector.scalar_tensor_tensor(out=HW[:, :, D:ROW], in0=score[:, :, :], scalar=ROUTE_SCALE, in1=winv[:, :].unsqueeze(2).to_broadcast([CT, NC4, E]), op0=ALU.mult, op1=ALU.mult).then_inc(hw_ready, 1)
                dve.wait_ge(pos_done, i + 1)
                routing(nc.vector.tensor_tensor(pos[:, :, :], psA[0:CT, 0:NC4 * E].rearrange("p (c e) -> p c e", c=NC4), base[:, :].unsqueeze(1).to_broadcast([CT, NC4, E]), ALU.add), i)
                routing(nc.vector.tensor_tensor(base[:, :], base[:, :], psA[0:CT, NC4 * E:NC4 * E + E], ALU.add), i)
                routing(nc.vector.scalar_tensor_tensor(out=sel[:, :, :], in0=pos[:, :, :], scalar=float(CAP), in1=sel[:, :, :], op0=ALU.is_lt, op1=ALU.mult), i)
                routing(nc.vector.tensor_tensor(pos[:, :, :], pos[:, :, :], c("slot1")[0:CT, :].unsqueeze(1).to_broadcast([CT, NC4, E]), ALU.add), i)
                routing(nc.vector.tensor_tensor(pos[:, :, :], pos[:, :, :], sel[:, :, :], ALU.mult), i)
                dve.sem_inc(dve_waited, 1)
                for q in range(NC4):
                    last = nc.vector.max(slotf[:, q, :], pos[:, q, :])
                routing(last, i)
                routing(nc.vector.tensor_scalar(noslot[:, :, :], slotf[:, :, :], 0.0, float(NOSLOT), ALU.is_equal, ALU.mult), i)
                dve.wait_ge(slots_free, i + 1)
                nc.vector.scalar_tensor_tensor(out=sloti[:, :], in0=slotf[:, :, :].rearrange("p c k -> p (c k)"), scalar=-1.0, in1=noslot[:, :, :].rearrange("p c k -> p (c k)"), op0=ALU.add, op1=ALU.add)
                routing(nc.vector.tensor_copy(toki[:, :], tokf[:, :]), i)
                nc.vector.tensor_scalar(tokf[:, :], tokf[:, :], float(N), None, ALU.add).then_inc(slot_ready, 1)
                routing(nc.vector.tensor_reduce(least[:, :], base[0:1, :], axis=AX, op=ALU.min), i)
                for flag_read in (act_read, pe_read, pool_read, q_read):
                    dve.wait_ge(flag_read, i + 1)
                nc.vector.tensor_scalar(open_[:, :], least[:, :], float(CAP), None, ALU.is_lt).then_inc(flag_set, 1)
                dve.wait_ge(flag_set, i + 1)
                dve.sem_inc(dve_waited, 1)

            def route_unit(i):
                while_open(dve, i, dve_waited, dve_read, route)
                dve.sem_inc(open_ready, 1)

            loop(dve, front_half, {
                "conv": conv, "sigmoid": sigmoid, "gate": gate, "split": split, "dt": step_size, "input": input_,
                "scan": scan, "output": output, "sum": sum_, "merge": merge, "route": route_unit})
            assert (front.count[0], back.count[0], routing.count[0]) == (DVE_FRONT, DVE_BACK, DVE_ROUTE), (front.count, back.count, routing.count)

            with dve.Fori(0, E // 4) as e:
                for b in range(2):
                    k = 2 * e + b + 1
                    dve.wait_ge(e_exp, k)
                    nc.vector.tensor_scalar(ea, ea, EXP_MAX, 1.0, ALU.min, ALU.add).then_inc(e_one, 1)
                    dve.wait_ge(e_sig, k)
                    nc.vector.tensor_tensor(ea, ea, psS[0:MD, 1, 0:2 * CAP], ALU.mult).then_inc(e_mul, 1)
                    dve.wait_ge(e_mul, k)
                    nc.vector.tensor_tensor(ea, ea, psS[0:MD, 2, 0:2 * CAP], ALU.mult).then_inc(e_act, 1)
                    dve.wait_ge(e2_done, k)
                    for q in range(4):
                        ins = nc.vector.tensor_scalar(eo[b][:, q, :], psS[:, 3, q * D:(q + 1) * D], ex[b][:, q, bass.ds(e * 4 + 2 * b + q // 2 + D, 1)], None, ALU.mult)
                    ins.then_inc(e_out, 1)
            def normalise(n):
                t, m = FINAL[n]
                buf, f = fbuf[n % HBUF], n % 2
                dve.wait_ge(fin_rs, n + 1)
                nc.vector.tensor_tensor(buf[0:B, 0:m, :], buf[0:B, 0:m, :], fmv[f][0:B, 0:m, 0:1].to_broadcast([B, m, D]), ALU.subtract).then_inc(fin_sub, 1)
                dve.wait_ge(fin_sub, n + 1)
                nc.vector.tensor_tensor(buf[0:B, 0:m, :], buf[0:B, 0:m, :], frs[f][0:B, 0:m].unsqueeze(2).to_broadcast([B, m, D]), ALU.mult).then_inc(fin_ready, 1)

            for n, (t, m) in enumerate(FINAL):
                dve.wait_ge(fin_loaded[n % HBUF], 16 * (n // HBUF + 1))
                for q in range(m):
                    last = nc.vector.bn_stats(fst[n % 2][0:B, q, :], fbuf[n % HBUF][0:B, q, :])
                last.then_inc(fin_stats, 1)
                dve.wait_ge(fin_stats, n + 1)
                for q in range(m):
                    last = nc.vector.bn_aggr(fmv[n % 2][0:B, q, :], fst[n % 2][0:B, q, :])
                last.then_inc(fin_mv, 1)
                if n:
                    normalise(n - 1)
            normalise(len(FINAL) - 1)

        @block.tensor
        def _(pe):
            mm = nc.tensor.matmul
            pe.wait_ge(weights_ready, 1)

            def mean_square(i, m):
                pe.wait_ge(sq_ready, i * 5 + m + 1)
                mm(psG[:, 0:N], c("mean"), sq[:, :], start=True, stop=True).then_inc(ms_done, 1)

            def front_half(i, until):
                until("conv", 1, KP)
                pe.wait_ge(patches_loaded, i * 16 + 16)
                if not isinstance(i, int):
                    pe.wait_ge(h_ready, i)
                for k in range(KP):
                    last = mm(psG[:, 0:G * NP], w("conv", k * D, (k + 1) * D), pat[:, k, :], start=k == 0, stop=k == KP - 1)
                    until("conv", k + 1, KP)
                last.then_inc(conv_done, 1)
                for l in range(2):
                    s = f".{l}"
                    until("norm" + s)
                    mean_square(i, 2 * l)
                    until("qkv" + s, 1, 5)
                    pe.wait_ge(hn_ready, i * 4 + 2 * l + 1)
                    for m, n in enumerate("qk"):
                        mm(psS[:, m, 0:G * TP], w(f"{n}{l}"), Hnf, start=True, stop=True).then_inc((q_done, k_done)[m], 1)
                        until("qkv" + s, m + 2, 5)
                    for b, q in CHUNKS:
                        at = (b * NQ + q) * D
                        last = mm(psG[0:CT, at:at + D], Hn[:, b, q * CT:(q + 1) * CT], w(f"v{l}"), start=True, stop=True)
                        if q:
                            until("qkv" + s, 4 + b, 5)
                    last.then_inc(v_done, 1)

                    def values(n):
                        b, q = CHUNKS[n]
                        pe.wait_ge(pt_ready, i * 16 + l * 8 + n * 2 + 2)
                        if n:
                            pe.wait_ge(ot_ready, i * 8 + l * 4 + n)
                        for m in range(HEADS):
                            at = (n % 2 * HEADS + m) * (HD + 1)
                            for k in range(NQ):
                                last = mm(psG[0:CT, at:at + HD + 1], PT[:, m, k, :], V[:, b * NQ + k, m, :], start=k == 0, stop=k == NQ - 1)
                        last.then_inc(o_done, 1)

                    def turn_back(n):
                        q = n % 2
                        pe.wait_ge(on_ready, i * 8 + l * 4 + n + 1)
                        nc.tensor.transpose(psG[:, OT_AT + q * CT:OT_AT + (q + 1) * CT], ON[:, :, :].rearrange("p h d -> p (h d)"), c("ident")[0:CT, 0:CT]).then_inc(ont_done, 1)

                    for n, (b, q) in enumerate(CHUNKS):
                        stage = f"score{n}" + s
                        k = i * 16 + l * 8 + n * 2
                        until(stage, 1, 6)
                        if n == 0:
                            pe.wait_ge(q_ready, i * 2 + l + 1)
                            pe.wait_ge(km0_ready, i * 2 + l + 1)
                        if n == NQ:
                            pe.wait_ge(km1_ready, i * 2 + l + 1)
                        for h in range(2):
                            if n:
                                pe.wait_ge(pt_ready, k - 2 + h + 1)
                            for j in (2 * h, 2 * h + 1):
                                last = mm(psS[0:CT, j, 0:2 * T].rearrange("p (e t) -> p e t", e=2), Q[:, b, q * CT:(q + 1) * CT], KM[:, b, 2 * j:2 * j + 2, 0:T], start=True, stop=True)
                                if j % 2:
                                    last.then_inc(s_done, 1)
                                until(stage, 2 + j, 6)
                        if n:
                            if n == 1:
                                pe.wait_ge(v_ready, i * 2 + l + 1)
                            values(n - 1)
                        until(stage)
                        stage = f"turn{n}" + s
                        until(stage, 1, 3)
                        for h in range(2):
                            pe.wait_ge(p_ready, k + h + 1)
                            for m in range(4 * h, 4 * h + 4):
                                for e in range(NQ):
                                    at = (m % 2 * NQ + e) * CT
                                    last = nc.tensor.transpose(psS[0:CT, m // 2, at:at + CT], P[:, m, e * CT:(e + 1) * CT], c("ident")[0:CT, 0:CT])
                            last.then_inc(t_done, 1)
                            until(stage, 2 + h, 3)
                        if n:
                            turn_back(n - 1)
                    until("value" + s, 1, 2)
                    values(len(CHUNKS) - 1)
                    until("value" + s)
                    until("turnback" + s, 1, 2)
                    turn_back(len(CHUNKS) - 1)
                    until("turnback" + s)
                    until("wo" + s, 1, 2)
                    pe.wait_ge(ot_ready, i * 8 + l * 4 + len(CHUNKS))
                    last = mm(psG[:, 0:N].rearrange("p (g t) -> p g t", g=G), w(f"wo{l}"), OT[:, :, 0:T], start=True, stop=True)
                    last.then_inc(wo_done, 1)
                    until("wo" + s)
                    until("norm2" + s)
                    mean_square(i, 2 * l + 1)
                    until("gate" + s, 1, 4)
                    pe.wait_ge(hn_ready, i * 4 + 2 * l + 2)
                    for f in range(FC):
                        last = mm(psS[0:FW, f, 0:N].rearrange("p (g t) -> p g t", g=G), w(f"gate{l}", f * FW, (f + 1) * FW), Hnt, start=True, stop=True)
                        until("gate" + s, 2 + f, 4)
                    last.then_inc(g_done, 1)
                    until("sig" + s)
                    until("up" + s, 1, 4)
                    pe.wait_ge(gs_ready, i * 2 + l + 1)
                    for f in range(FC):
                        last = mm(psS[0:FW, f, 0:N].rearrange("p (g t) -> p g t", g=G), w(f"up{l}", f * FW, (f + 1) * FW), Hnt, start=True, stop=True)
                        until("up" + s, 2 + f, 4)
                    last.then_inc(u_done, 1)
                    until("down" + s, 1, 4)
                    pe.wait_ge(ff_ready, i * 2 + l + 1)
                    for f in range(FC):
                        last = mm(psG[:, 0:N], w(f"down{l}", f * D, (f + 1) * D)[0:FW, :], EF[0:FW, f, :], start=f == 0, stop=f == FC - 1)
                        until("down" + s, 2 + f, 4)
                    last.then_inc(down_done, 1)
                until("normf")
                mean_square(i, 4)

            def project(i, d):
                s = "fb"[d]
                if d:
                    pe.wait_ge(xc_ready, i * 2 + 1)
                else:
                    pe.wait_ge(h_ready, i + 1)
                    pe.wait_ge(open_ready, i + 1)
                x = Hr[:, :] if d else H[:, 0:N]
                mm(psA[:, 0:N], w(f"win{s}", 0, D), x, start=True, stop=True)
                mm(psB[:, 0:N], w(f"win{s}", D, 2 * D), x, start=True, stop=True).then_inc(xz_done, 1)

            def xproj(i, d):
                pe.wait_ge(xs_ready, i * 2 + d + 1)
                if d:
                    pe.wait_ge(dtin_ready, i * 2 + 1)
                    pe.wait_ge(res_ready, i * 2 + 1)
                mm(psY[0:DTR, 0:N], w("xdt" + "fb"[d]), XZ[:, d, 0, :], start=True, stop=True)
                mm(psA[0:96, 0:N], w("xbc" + "fb"[d]), XZ[:, d, 0, :], start=True, stop=True).then_inc(bc_done, 1)

            def dtproj(i, d):
                pe.wait_ge(dtin_ready, i * 2 + 2)
                if d:
                    pe.wait_ge(dtm_ready, i * 2 + 1)
                mm(psY[:, 0:N], w("wdt" + "fb"[d])[0:DTR, :], dtin[:, d, :], start=True, stop=True).then_inc(dtp_done, 1)

            def broadcast(i, g, m, row):
                d = g // (QUARTERS // 2)
                if m == 0:
                    pe.wait_ge(bcs_ready, i * 2 + 2)
                if m >= 2:
                    pe.wait_ge(mul_done, i * MULS + m - 1)
                mm(AB[m % 2][:, 0:N], bcsel[:, row, :], bc[:, d, :], start=True, stop=True).then_inc(bb_done, 1)

            def input_(i, g, k):
                broadcast(i, g, 2 * QN * g + k, g % (QUARTERS // 2) * QN + k)

            def output(i, g, k):
                broadcast(i, g, 2 * QN * g + QN + k, NS + g % (QUARTERS // 2) * QN + k)

            def sum_(i, g):
                d, q = divmod(g, QUARTERS // 2)
                if q == 0:
                    pe.wait_ge(dt_ready, i * 2 + 2) if d == 0 else pe.wait_ge(ys_ready, i * 2 + 1)
                pe.wait_ge(summed, i * QUARTERS + g + 1)
                mm(psY[:, 0:N], c("ident"), hs[:, g % HBUF, 0, :], start=q == 0, stop=False).then_inc(acc_done, 1)
                if q == QUARTERS // 2 - 1:
                    mm(psY[:, 0:N], dskip[:, d, :], XZ[:, d, 0, :], start=False, stop=True).then_inc(y_done, 1)

            def merge(i):
                pe.wait_ge(ys_ready, i * 2 + 2)
                for q in range(NC4):
                    at = slice(q * CT, (q + 1) * CT)
                    to = psA[0:CT, q * D:(q + 1) * D]
                    mm(to, H[:, at], c("ident"), start=True, stop=False)
                    mm(to, YS[:, 0, at], w("woutf"), start=False, stop=False)
                    last = mm(to, YS[:, 1, at], w("woutb"), start=False, stop=True)
                last.then_inc(m_done, 1)

            def route(i):
                pe.wait_ge(ht_ready, i + 1)
                for q in range(NC4):
                    last = nc.tensor.transpose(psB[:, q * CT:(q + 1) * CT], HW[:, q, 0:D], c("ident")[0:CT, 0:CT])
                last.then_inc(ht_done, 1)
                pe.wait_ge(h2_ready, i + 1)
                for q in range(NC4):
                    last = mm(psA[0:CT, q * E:(q + 1) * E], h2[:, q * CT:(q + 1) * CT], w("route"), start=True, stop=True)
                last.then_inc(lg_done, 1)
                pe.wait_ge(sel_ready, i + 1)
                for q in range(NC4 + 1):
                    for p in range(min(q + 1, NC4)):
                        last = mm(psA[0:CT, q * E:(q + 1) * E], (before_h if p == q else ones_h)[0:CT, 0:CT], selh[:, p, :], start=p == 0, stop=p == min(q, NC4 - 1))
                last.then_inc(pos_done, 1)

            loop(pe, front_half, {
                "project": project, "xproj": xproj, "dtproj": dtproj, "input": input_, "output": output, "sum": sum_,
                "merge": merge, "route": lambda i: while_open(pe, i, pe_waited, pe_read, route)})

            with pe.Fori(0, E // 4) as e:
                for b in range(2):
                    p = 2 * e + b + 1
                    pe.wait_ge(gathered[b], e * 64 + 64)
                    for k in range(4):
                        last = nc.tensor.transpose(psS[:, 0, k * D:(k + 1) * D], ex[b][:, k, 0:D], c("ident"))
                    last.then_inc(xt_done, 1)
                    pe.wait_ge(xt_ready, p)
                    pe.wait_ge(w_loaded[b], e * 32 + 32)
                    for h in range(2):
                        for k in range(2):
                            last = mm(psS[0:MD, 1 + k, h * CAP:(h + 1) * CAP], ew[b][:, h, k * MD:(k + 1) * MD], exT[:, h * CAP:(h + 1) * CAP], start=True, stop=True)
                    last.then_inc(e13_done, 1)
                    pe.wait_ge(e_act, p)
                    for k in range(4):
                        last = mm(psS[:, 3, k * D:(k + 1) * D], ea[:, k * 128:(k + 1) * 128], ew[b][0:MD, k // 2, D:2 * D], start=True, stop=True)
                    last.then_inc(e2_done, 1)


def kernel(**x):
    import numpy as np
    import concourse.bacc as _bacc
    from concourse import mybir as _mybir
    from concourse.bass_utils import run_bass_kernel_spmd as _run

    a = {k: np.asarray(q) for k, q in x.items()}
    f4 = np.float32
    g = IMG // PATCH
    pt = a["x"].reshape(STEPS, G, CH, g, PATCH, g, PATCH).transpose(0, 2, 4, 6, 1, 3, 5)
    pt = np.ascontiguousarray(pt.reshape(STEPS, KP, 128, G * NP).transpose(0, 2, 1, 3))

    wts = np.zeros((128, W_N), f4)

    def put(to, cols, name, value):
        at, n = cols[name]
        value = value.reshape(value.shape[0], -1)
        to[0:value.shape[0], at:at + value.shape[1]] = value

    t = "L0_tok_"
    put(wts, W_COLS, "conv", a[t + "conv_w"].reshape(D, KP, 128).transpose(2, 1, 0))
    for l in range(2):
        for m, n in enumerate("qkv"):
            put(wts, W_COLS, f"{n}{l}", a[t + f"qkv_{l}"][m * D:(m + 1) * D].T)
        put(wts, W_COLS, f"wo{l}", a[t + f"wo_{l}"].T)
        put(wts, W_COLS, f"gate{l}", a[t + f"gate_{l}"].T)
        put(wts, W_COLS, f"up{l}", a[t + f"up_{l}"].T)
        down = np.zeros((FC * FW, D), f4)
        down[0:FF] = a[t + f"down_{l}"].T
        put(wts, W_COLS, f"down{l}", down.reshape(FC, FW, D).transpose(1, 0, 2))
    m = "L0_attn_"
    for s in "fb":
        put(wts, W_COLS, f"win{s}", a[m + f"W_in_{s}"])
        put(wts, W_COLS, f"xdt{s}", a[m + f"W_xproj_{s}"][:, 0:DTR])
        put(wts, W_COLS, f"xbc{s}", np.concatenate([a[m + f"W_xproj_{s}"][:, DTR:]] * 3, axis=1))
        put(wts, W_COLS, f"wdt{s}", a[m + f"W_dt_{s}"])
        put(wts, W_COLS, f"wout{s}", a[m + f"W_out_{s}"])
    put(wts, W_COLS, "route", a["L0_ffn_gate_w"].T)

    vec = np.zeros((128, V_N), f4)
    put(vec, V_COLS, "convb", a[t + "conv_b"][:, None])
    put(vec, V_COLS, "cls", a[t + "cls_token"].reshape(D, 1))
    put(vec, V_COLS, "pos", a[t + "pos_emb"].reshape(T, D).T)
    put(vec, V_COLS, "lnf", a[t + "ln_f"][:, None])
    for l in range(2):
        put(vec, V_COLS, f"ln1{l}", a[t + f"ln1_{l}"][:, None])
        put(vec, V_COLS, f"ln2{l}", a[t + f"ln2_{l}"][:, None])
    for s in "fb":
        put(vec, V_COLS, f"taps{s}", a[m + f"W_conv_{s}"])
        put(vec, V_COLS, f"bconv{s}", a[m + f"b_conv_{s}"][:, None])
        put(vec, V_COLS, f"bdt{s}", a[m + f"b_dt_{s}"][:, None])
        put(vec, V_COLS, f"alog{s}", a[m + f"A_log_{s}"])
        put(vec, V_COLS, f"dskip{s}", a[m + f"D_{s}"][:, None])

    cst = np.zeros((128, C_N), f4)
    p = np.arange(128)
    put(cst, C_COLS, "ident", np.eye(128, dtype=f4))
    put(cst, C_COLS, "mean", np.full((128, 128), 1 / D, f4))
    put(cst, C_COLS, "before", np.triu(np.ones((128, 128), f4), 1))
    put(cst, C_COLS, "ones", np.ones((128, 128), f4))
    put(cst, C_COLS, "slot1", np.tile(np.arange(E) * CAP + 1.0, (128, 1)))
    tok = np.arange(NC4)[None] * CT + p[:, None]
    put(cst, C_COLS, "tok0", tok)
    put(cst, C_COLS, "valid", tok < N)
    put(cst, C_COLS, "unused", TOK + (np.arange(SLOTS) % PAD).reshape(128, -1))
    put(cst, C_COLS, "part1", -1.0 * (p >= 32)[:, None])
    put(cst, C_COLS, "part2", -1.0 * (p >= 64)[:, None])
    put(cst, C_COLS, "heads", p[:, None] // HD == np.arange(HEADS)[None])
    put(cst, C_COLS, "groupbefore", np.tile(np.tril(np.ones((GR, GR)), -1).reshape(1, -1), (128, 1)))
    bcsel = np.zeros((96, 2 * NS, D), f4)
    for r in range(96):
        bcsel[r, r % 32] = 1

    w13 = np.concatenate([a["L0_ffn_w1"], a["L0_ffn_w3"]], axis=2)
    arrays = {"patches": pt, "weights": wts, "vectors": vec, "consts": cst, "bcsel": bcsel.reshape(96, -1),
              "gate_b": a["L0_ffn_gate_b"], "w13": w13, "w2": a["L0_ffn_w2"]}
    arrays = {k: np.ascontiguousarray(q) for k, q in arrays.items()}
    nc = _bacc.Bacc("TRN2", target_bir_lowering=False, num_devices=1)
    args = [nc.dram_tensor(k, q.shape, _mybir.dt.from_np(q.dtype), kind="ExternalInput").ap() for k, q in arrays.items()]
    out = nc.dram_tensor("out", (B, T, D), _mybir.dt.float32, kind="ExternalOutput").ap()
    vit_mamba_moe(nc, *args, out)
    r = _run(nc, [arrays], core_ids=[0])
    return r.results[0]["out"]
```

```python
import concourse.bass as bass
from concourse import mybir
from contextlib import ExitStack

D = 128
B = 128
PATCH, IMG, CH = 16, 224, 3
NP = (IMG // PATCH) ** 2
T = NP + 1
G = 2
N = G * T
STEPS = B // G
KP = CH * PATCH * PATCH // 128
HEADS, HD = 8, 16
FF = 344
FC = 3
FW = -(-FF // FC)
NS = 16
DTR = 32
TAPS = 4
XW = T + TAPS - 1
E, GR, TOPG, TOPK, CAP, MD = 64, 8, 4, 8, 256, 64
ROUTE_SCALE = 2.5
CT = 99
NC4 = 4
PADN = NC4 * CT
ROW = D + E
TOK = B * T
SLOTS = E * CAP
NQ = 2
TP = NQ * CT
ROUNDS = [(q, h) for q in range(NQ) for h in range(2)]
NOSLOT = 1 << 20
PAD = CAP
ZP = 128
LOG1P_SERIES = 2.0 ** -8
BIG = 1e30
EPS_RMS, EPS_LN = 1e-6, 1e-5

QUARTERS = 8
QN = NS * 2 // QUARTERS
MULS = 2 * NS * 2
HBUF = 3
EXP_MAX = 1e18

ACT_FRONT, ACT_BACK, DVE_FRONT, DVE_BACK, DVE_ROUTE = 18, 2, 4, 16, 27

UNITS = [("project", 0), ("-sum", QUARTERS - 1), ("project", 1), ("conv", 0), ("-merge",), ("keep",), ("conv", 1), ("sigmoid", 0),
         ("leave",), ("-route",), ("sigmoid", 1), ("gate", 0), ("gate", 1),
         ("xproj", 0), ("split", 0), ("xproj", 1), ("split", 1), ("dtproj", 0), ("dt", 0), ("dtproj", 1), ("dt", 1)]
UNITS += [("decay", 0, k) for k in range(QN)]
for _g in range(QUARTERS):
    for _k in range(QN):
        UNITS += [("decay", 1, _k)] if _g == 0 else []
        UNITS += [("input", _g, _k)]
    UNITS += [("scan", _g)] + ([("sum", _g - 1)] if _g else [])
    for _k in range(QN):
        UNITS += [("decay", _g + 2, _k)] if _g + 2 < QUARTERS else []
        UNITS += [("output", _g, _k)]
LAYER_STAGES = (["norm", "qkv"] + [f"{n}{k}" for k in range(4) for n in ("score", "turn")]
                + ["value", "den", "wo", "norm2", "gate", "sig", "up", "down"])
STAGES = [f"{n}.{b}" for n in ["conv"] + [f"{n}.{l}" for l in range(2) for n in LAYER_STAGES] + ["normf"] for b in range(G)]
WEIGHT = {"conv": 6, "norm.0": 3, "norm.1": 3, "norm2.0": 10.2, "norm2.1": 5.22, "qkv.0": 2.5, "qkv.1": 2.88,
          "score.0": 6, "score.1": 6, "turn.0": 4, "turn.1": 4, "value.0": 1.94, "value.1": 1.44, "den.0": 2.61,
          "den.1": 2.25, "wo.0": 3.52, "wo.1": 3, "gate.0": 2.4, "gate.1": 2.4, "sig.0": 4, "sig.1": 4.6, "up.0":
          5.4, "up.1": 2.4, "down.0": 4, "down.1": 4, "normf": 4}
COST = {"project": 2, "conv": 2, "sigmoid": 2, "gate": 3, "xproj": 2.55, "split": 2.88, "dtproj": 0.65, "dt": 4,
        "decay": 0.3, "input": 0.5, "scan": 2, "output": 0.5, "sum": 0.61, "merge": 4, "keep": 0.3, "leave": 0,
        "route": 0.8}


def shares():
    def key(stage):
        name, *layer = stage.split(".")[:-1]
        return ".".join([name.rstrip("0123") if name != "norm2" else name] + layer)

    w = [WEIGHT[key(n)] for n in STAGES]
    cost = [COST[u[0].strip("-")] for u in UNITS]
    out, acc, k, used = {}, 0, 0, 0
    for n, x in zip(STAGES, w):
        acc += x
        while k < len(UNITS) and used + cost[k] / 2 <= acc / sum(w) * sum(cost):
            used += cost[k]
            k += 1
        out[n] = k
    out[STAGES[-1]] = out[STAGES[-2]] = len(UNITS)
    return out


SHARE = shares()

def _cols(widths):
    at, out = 0, {}
    for name, w in widths:
        out[name] = (at, w)
        at += w
    return out, at


W_COLS, W_N = _cols(
    [("conv", KP * D)]
    + [(f"{n}{l}", w) for l in range(2) for n, w in (
        ("q", D), ("k", D), ("v", D), ("woe", D), ("woo", D),
        ("gate", FC * FW), ("up", FC * FW), ("down", FC * D))]
    + [(f"{n}{d}", w) for d in "fb" for n, w in (
        ("win", 2 * D), ("xdt", DTR), ("xbc", 3 * 2 * NS), ("wdt", D), ("wout", D))]
    + [("route", E)])
V_COLS, V_N = _cols(
    [("convb", 1), ("cls", 1), ("pos", T), ("lnf", 1)]
    + [(f"{n}{l}", 1) for l in range(2) for n in ("ln1", "ln2")]
    + [(f"{n}{d}", w) for d in "fb" for n, w in (
        ("taps", TAPS), ("bconv", 1), ("bdt", 1), ("alog", NS), ("dskip", 1))])
C_COLS, C_N = _cols([("ident", D), ("mean", D), ("dsel", D), ("before", D), ("ones", D),
                     ("slot1", E), ("valid", NC4), ("tok0", NC4), ("part1", 1), ("part2", 1),
                     ("heads", HEADS), ("groupbefore", GR * GR), ("unused", SLOTS // 128)])


def vit_mamba_moe(nc, patches, weights, vectors, consts, bcsel_d, gate_b, w13, w2, out):
    f32, bf16, i32 = mybir.dt.float32, mybir.dt.bfloat16, mybir.dt.int32
    ACT = mybir.ActivationFunctionType
    ALU = mybir.AluOpType
    AX = mybir.AxisListType.X

    rows_d = nc.dram_tensor("rows_scratch", (TOK + PAD, ROW), f32, kind="Internal").ap()
    sum_d = nc.dram_tensor("sum_scratch", (TOK + PAD, D), f32, kind="Internal").ap()
    slot_d = nc.dram_tensor("slot_scratch", (SLOTS, 1), i32, kind="Internal").ap()

    ctx = ExitStack()
    with ctx:
        def sb(name, shape, dt=f32):
            return ctx.enter_context(nc.sbuf_tensor(name, shape, dt))

        def sem(name):
            return ctx.enter_context(nc.semaphore(name))

        wts = sb("wts", [128, W_N])
        vec = sb("vec", [128, V_N])
        cst = sb("cst", [128, C_N])

        def w(name, a=0, b=None):
            at, n = W_COLS[name]
            return wts[:, at + a:at + (n if b is None else b)]

        def v(name, a=0, b=None):
            at, n = V_COLS[name]
            return vec[:, at + a:at + (n if b is None else b)]

        def c(name, a=0, b=None):
            at, n = C_COLS[name]
            return cst[:, at + a:at + (n if b is None else b)]

        bcsel = sb("bcsel_h", [96, 2 * NS, D], bf16)
        before_h = sb("before_h", [128, D], bf16)
        ones_h = sb("ones_h", [128, D], bf16)
        posb = sb("posb", [128, T])
        cls0 = sb("cls0", [128, 1])
        aneg = sb("aneg", [128, 2, NS])
        dskip = sb("dskip", [128, 2, D])
        gateb = sb("gateb", [128, E])
        epsr = sb("epsr", [128, 2])

        pat = sb("pat", [128, KP, G * NP])
        X = sb("X", [128, G, T])
        sq = sb("sq", [128, G, T])
        rs = sb("rs", [128, G, T])
        Hn = sb("Hn", [128, G, TP])
        Q = sb("Q", [128, G, TP])
        K = sb("K", [128, G, TP])
        KM = sb("KM", [128, G, HEADS, TP])
        V = sb("V", [CT, G, NQ, HEADS, 32])
        least_s = sb("least_s", [CT, G, HEADS // 2])
        P = sb("P", [CT, G, HEADS // 2, TP])
        PT = sb("PT", [CT, G, HEADS, NQ, CT])
        O = sb("O", [128, G, 2, TP])
        R = sb("R", [128, G, 2 * TP])
        EF = sb("EF", [128, G, FC, T])
        H = sb("H", [128, N])
        Hr = sb("Hr", [128, N])
        HB = sb("HB", [128, PADN])
        XC = sb("XC", [128, 2, G, XW])
        XZ = sb("XZ", [128, 2, 2, N])
        SG = sb("SG", [128, 2, 2, N])
        dtin = sb("dtin", [DTR, 2, N])
        hi = sb("hi", [96, 2, N], bf16)
        res = sb("res", [96, N])
        mid = sb("mid", [96, N], bf16)
        bc = sb("bc", [96, 2, N], bf16)
        dt_ = sb("dt_", [128, 2, N])
        sp = sb("sp", [128, N])
        spl = sb("spl", [128, N])
        small = sb("small", [128, N], mybir.dt.uint32)
        u = sb("u", [128, 2, N])
        dA = sb("dA", [128, 2, QN, N])
        hs = sb("hs", [128, HBUF, QN, N])
        YS = sb("YS", [128, 2, PADN])
        stats = sb("stats", [CT, NC4, 6])
        mv = sb("mv", [CT, NC4, 2])
        rstd = sb("rstd", [CT, NC4])
        HW = sb("HW", [CT, NC4, ROW])
        h2 = sb("h2", [128, PADN])
        score = sb("score", [CT, NC4, E])
        t1 = sb("t1", [CT, NC4, E])
        ext = sb("ext", [CT, NC4 * GR, 12])
        pairs = sb("pairs", [CT, NC4 * GR, 4, 8])
        gs = sb("gs", [CT, NC4, GR])
        cmp1 = sb("cmp1", [CT, NC4, GR, GR])
        cmp2 = sb("cmp2", [CT, NC4, GR, GR])
        rank = sb("rank", [CT, NC4 * GR])
        masked = sb("masked", [CT, NC4, E])
        top8 = sb("top8", [CT, NC4, 8])
        rest = sb("rest", [CT, NC4, E])
        sel = sb("sel", [CT, NC4, E])
        selh = sb("selh", [CT, NC4, E], bf16)
        wsum = sb("wsum", [CT, NC4])
        winv = sb("winv", [CT, NC4])
        pos = sb("pos", [CT, NC4, E])
        base = sb("base", [CT, E])
        least = sb("least", [1, 1])
        open_ = sb("open", [1, 1], i32)
        slotf = sb("slotf", [CT, NC4, 8])
        noslot = sb("noslot", [CT, NC4, 8])
        sloti = sb("sloti", [CT, NC4 * 8], i32)
        tokf = sb("tokf", [CT, NC4])
        toki = sb("toki", [CT, NC4], i32)
        unused = sb("unused", [128, SLOTS // 128], i32)
        zeros = sb("zeros", [128, ROW])
        eidx = sb("eidx", [128, 4, 4], i32)

        psS = ctx.enter_context(nc.psum_tensor("psS", [128, 4, 512], f32))
        psG = ctx.enter_context(nc.psum_tensor("psG", [128, 512], f32))
        psA = ctx.enter_context(nc.psum_tensor("psA", [128, 512], f32))
        psB = ctx.enter_context(nc.psum_tensor("psB", [128, 512], f32))
        psY = ctx.enter_context(nc.psum_tensor("psY", [128, 512], f32))
        AB = [psA, psB]

        names = ("open_ready loaded patches_loaded pool_ready unused_ready rows_zeroed rows_stored init_stored hw_ready "
                 "routed_stored q_waited ht_ready hw_free conv_done sent_all pair_free all_added fin_ready mul_done half_summed "
                 "summed slot_ready pool_waited sent_a sent_b slots_free e_out added act_setup consts_ready act_front x_ready "
                 "sq_ready ms_done rs_ready q_done q_ready k_ready p_ready o_done inv_ready g_done ge_ready ge1_ready gsig_ready "
                 "act_back xz_done xc_ready xconv_ready sge_ready sg1_ready sgr_ready bc_done hi_ready dtin_ready res_ready "
                 "mid_ready dtp_done dt_ready abs_ready spe_ready sp_ready scan_ready da_ready mv_ready rstd_ready act_route "
                 "ht_done h2_ready lg_done gl_ready gm_ready score_ready act_waited xt_done xt_ready e13_done e_exp e_one e_ln "
                 "e_sig fin_mv fin_ln fin_rs dve_setup weights_ready dve_front hn_ready v_done v_ready s_done max_done on_ready "
                 "wo_done gs_ready u_done ff_ready down_done h_ready dve_back xs_ready bcs_ready dtm_ready dve_waited acc_done "
                 "bb_done zeroed y_done ys_ready m_done dve_route sel_ready pos_done flag_set e_mul e_act e2_done fin_sub "
                 "fin_stats pe_waited act_read pe_read pool_read q_read dve_read km0_ready km1_ready t_done pt_ready o_ready "
                 "den_done act_merge dve_merge h_kept").split()
        (open_ready, loaded, patches_loaded, pool_ready, unused_ready, rows_zeroed, rows_stored, init_stored, hw_ready,
         routed_stored, q_waited, ht_ready, hw_free, conv_done, sent_all, pair_free, all_added, fin_ready, mul_done,
         half_summed, summed, slot_ready, pool_waited, sent_a, sent_b, slots_free, e_out, added, act_setup,
         consts_ready, act_front, x_ready, sq_ready, ms_done, rs_ready, q_done, q_ready, k_ready, p_ready, o_done,
         inv_ready, g_done, ge_ready, ge1_ready, gsig_ready, act_back, xz_done, xc_ready, xconv_ready, sge_ready,
         sg1_ready, sgr_ready, bc_done, hi_ready, dtin_ready, res_ready, mid_ready, dtp_done, dt_ready, abs_ready,
         spe_ready, sp_ready, scan_ready, da_ready, mv_ready, rstd_ready, act_route, ht_done, h2_ready, lg_done,
         gl_ready, gm_ready, score_ready, act_waited, xt_done, xt_ready, e13_done, e_exp, e_one, e_ln, e_sig, fin_mv,
         fin_ln, fin_rs, dve_setup, weights_ready, dve_front, hn_ready, v_done, v_ready, s_done, max_done, on_ready,
         wo_done, gs_ready, u_done, ff_ready, down_done, h_ready, dve_back, xs_ready, bcs_ready, dtm_ready, dve_waited,
         acc_done, bb_done, zeroed, y_done, ys_ready, m_done, dve_route, sel_ready, pos_done, flag_set, e_mul, e_act,
         e2_done, fin_sub, fin_stats, pe_waited, act_read, pe_read, pool_read, q_read, dve_read, km0_ready, km1_ready,
         t_done, pt_ready, o_ready, den_done, act_merge, dve_merge, h_kept) = (sem(n) for n in names)
        w_loaded, gathered = ([sem(f"{n}{b}") for b in range(2)] for n in ("w_loaded", "gathered"))
        slots_loaded = [sem(f"slots_loaded{c}") for c in range(4)]
        fin_loaded, fin_stored = ([sem(f"{n}{b}") for b in range(HBUF)] for n in ("fin_loaded", "fin_stored"))

        ex = [pat[:, 2 * b:2 * b + 2, :].rearrange("p k n -> p (k n)")[:, 0:4 * ROW].rearrange("p (c r) -> p c r", r=ROW) for b in range(2)]
        eo = [EF[:, :, :, :].rearrange("p g f t -> p (g f t)")[:, 512 * b:512 * b + 4 * D].rearrange("p (c r) -> p c r", r=D) for b in range(2)]
        ew = [dA[:, b, 0:2, :].rearrange("p a n -> p (a n)")[:, 0:4 * D].rearrange("p (h n) -> p h n", h=2) for b in range(2)]
        exT = KM[:, 0, 0:4, :].rearrange("p h t -> p (h t)")[:, 0:2 * CAP]
        ea = KM[0:MD, 1, 0:4, :].rearrange("p h t -> p (h t)")[:, 0:2 * CAP]
        FT = 8
        FINAL = [(t, min(FT, T - t)) for t in range(0, T, FT)]
        fbuf = [hs[:, b, :, :].rearrange("p a t -> p (a t)")[:, 0:FT * D].rearrange("p (t d) -> p t d", d=D) for b in range(HBUF)]
        fst = [dA[:, b, 0, 0:6 * FT].rearrange("p (t s) -> p t s", s=6) for b in range(2)]
        fmv = [dA[:, b, 1, 0:2 * FT].rearrange("p (t s) -> p t s", s=2) for b in range(2)]
        frs = [dA[:, b, 2, 0:FT] for b in range(2)]

        def bank(b, n, width):
            return psS[:, 2 * b + n, 0:width]

        def slices(b):
            return psS[0:FW, 2 * b:2 * b + 2, :].rearrange("p n (c t) -> p (n c) t", c=2)[:, 0:FC, 0:T]


        def interleaved(units, i, first=False):
            at = [0]

            def until(stage, part=1, parts=1):
                k = STAGES.index(stage)
                before = SHARE[STAGES[k - 1]] if k else 0
                units_here = SHARE[stage] - before
                ahead = units_here if parts == 1 else 2 + -(-(units_here - 2) * (part - 1) // (parts - 1))
                end = before + max(0, min(units_here, ahead))
                while at[0] < end:
                    kind, *args = UNITS[at[0]]
                    at[0] += 1
                    if kind in units:
                        units[kind](i, *args)
                    elif kind[1:] in units and not first:
                        units[kind[1:]](i - 1, *args)
            return until

        def loop(eng, front_half, units):
            def no_units(stage, part=1, parts=1):
                return None

            front_half(0, no_units)
            until = interleaved(units, 0, first=True)
            front_half(1, until)
            until(STAGES[-1])
            with eng.Fori(0, STEPS - 2) as i:
                until = interleaved(units, i + 1)
                front_half(i + 2, until)
                until(STAGES[-1])
            interleaved(units, STEPS - 1)(STAGES[-1])
            for kind, *args in UNITS:
                if kind[0] == "-" and kind[1:] in units:
                    units[kind[1:]](STEPS - 1, *args)

        def is_first(i):
            return isinstance(i, int) and i == 0

        def chain(eng, done, per):
            n = [0]

            def link(ins, i):
                n[0] = n[0] % per + 1
                ins.then_inc(done, 1)
                eng.wait_ge(done, i * per + n[0])
            link.count = n
            return link

        def while_open(eng, i, waited, flag_read, route):
            eng.wait_ge(open_ready, i + 1)
            eng.sem_inc(waited, 1)
            flag = eng.value_load(open_[0:1, 0:1], min_val=0, max_val=1)
            eng.sem_inc(flag_read, 1)
            with eng.If(flag):
                route(i)

        block = ctx.enter_context(nc.Block())

        @block.sync
        def _(q):
            q.dma_start(wts[:, :], weights).then_inc(loaded, 16)
            q.dma_start(vec[:, :], vectors).then_inc(loaded, 16)
            q.dma_start(cst[:, :], consts).then_inc(loaded, 16)
            q.dma_start(hs[0:96, 0:3, :, :].rearrange("p a b t -> p (a b t)")[:, 0:2 * NS * D], bcsel_d).then_inc(loaded, 16)
            q.dma_start(gateb[:, :], gate_b.rearrange("(a e) -> a e", a=1).to_broadcast([128, E])).then_inc(loaded, 16)
            q.dma_start(pat[:, :, :], patches[0]).then_inc(patches_loaded, 16)
            q.wait_ge(pool_ready, 13)
            q.wait_ge(unused_ready, 1)
            q.dma_start(rows_d.rearrange("(p t) r -> p t r", p=ZP), zeros[0:ZP, :].unsqueeze(1).to_broadcast([ZP, (TOK + PAD) // ZP, ROW])).then_inc(rows_zeroed, 16)
            q.dma_start(sum_d[TOK:TOK + PAD, :].rearrange("(c p) r -> p c r", c=2), zeros[:, 0:D].unsqueeze(1).to_broadcast([128, 2, D])).then_inc(rows_stored, 16)
            q.dma_start(slot_d.rearrange("(p a) o -> p (a o)", p=128), unused[:, :]).then_inc(init_stored, 16)

            def route(i):
                q.wait_ge(rows_zeroed, 16)
                q.wait_ge(hw_ready, i + 1)
                for lo, nch, n in ((0, NC4 - 1, CT), (NC4 - 1, 1, N - (NC4 - 1) * CT)):
                    dst = rows_d[bass.ds(i * N + lo * CT, nch * n), :].rearrange("(c p) r -> p c r", p=n)
                    q.dma_start(dst, HW[0:n, lo:lo + nch, :]).then_inc(routed_stored, 16)
                q.wait_ge(routed_stored, i * 32 + 32)
                q.sem_inc(q_waited, 1)

            def store(b):
                q.wait_ge(ht_ready, b + 1)
                for lo, nch, n in ((0, NC4 - 1, CT), (NC4 - 1, 1, N - (NC4 - 1) * CT)):
                    dst = sum_d[bass.ds(b * N + lo * CT, nch * n), :].rearrange("(c p) r -> p c r", p=n)
                    q.dma_start(dst, HW[0:n, lo:lo + nch, 0:D]).then_inc(rows_stored, 16)
                while_open(q, b, q_waited, q_read, route)
                q.sem_inc(hw_free, 1)

            def patches_of(i):
                q.wait_ge(conv_done, i * G)
                q.dma_start(pat[:, :, :], patches[bass.ds(i, 1)].rearrange("o p k n -> (o p) k n")).then_inc(patches_loaded, 16)

            q.sem_inc(hw_free, 1)
            patches_of(1)
            with q.Fori(0, STEPS - 2) as i:
                patches_of(i + 2)
                store(i)
            store(STEPS - 2)
            store(STEPS - 1)
            q.wait_ge(sent_all, 1)
            q.wait_ge(rows_zeroed, 16)
            q.wait_ge(rows_stored, 16 + 32 * STEPS)

            def load_slots(p, c):
                q.dma_start(eidx[:, c, :].rearrange("p (h k) -> p h k", h=2), slot_d[bass.ds(p * 2 * CAP, 2 * CAP), :].rearrange("(h p k) o -> p h (k o)", h=2, p=128)).then_inc(slots_loaded[c], 16)

            def load_pair(p, c, more=True):
                b = c % 2
                q.wait_ge(pair_free, p + 1)
                if more:
                    load_slots(p + 2, (c + 2) % 4)
                q.dma_start(ew[b][:, :, 0:D], w13[bass.ds(p * 2, 2)].rearrange("h p n -> p h n")).then_inc(w_loaded[b], 16)
                q.dma_start(ew[b][0:MD, :, D:2 * D], w2[bass.ds(p * 2, 2)].rearrange("h p n -> p h n")).then_inc(w_loaded[b], 16)

            for n in range(2):
                load_slots(n, n)
            with q.Fori(0, E // 8 - 1) as e:
                for n in range(4):
                    load_pair(e * 4 + n, n)
            for n in range(4):
                load_pair(E // 2 - 4 + n, n, more=n < 2)
            q.wait_ge(all_added, 1)
            r3 = sum_d[0:TOK, :].rearrange("(p t) d -> p t d", p=B)

            def load(n):
                t, m = FINAL[n]
                if n >= HBUF:
                    q.wait_ge(fin_stored[n % HBUF], 16 * (n // HBUF))
                q.dma_start(fbuf[n % HBUF][0:B, 0:m, :], r3[:, t:t + m, :]).then_inc(fin_loaded[n % HBUF], 16)

            for n in range(HBUF - 1):
                load(n)
            for n, (t, m) in enumerate(FINAL):
                if n + HBUF - 1 < len(FINAL):
                    load(n + HBUF - 1)
                q.wait_ge(fin_ready, n + 1)
                q.dma_start(out[:, t:t + m, :], fbuf[n % HBUF][0:B, 0:m, :]).then_inc(fin_stored[n % HBUF], 16)
            for b in range(HBUF):
                q.wait_ge(fin_stored[b], 16 * len(FINAL[b::HBUF]))

        @block.gpsimd
        def _(pool):
            nc.gpsimd.memset(V[:, :, :, :, :], 0.0).then_inc(pool_ready, 1)
            pool.wait_ge(pool_ready, 1)
            nc.gpsimd.memset(V[:, :, :, :, HD:HD + 1], 1.0).then_inc(pool_ready, 1)
            nc.gpsimd.memset(Hn[:, :, T:TP], 0.0).then_inc(pool_ready, 1)
            nc.gpsimd.memset(P[:, :, :, T:TP], 0.0).then_inc(pool_ready, 1)
            nc.gpsimd.memset(XC[:, :, :, :], 0.0).then_inc(pool_ready, 1)
            nc.gpsimd.memset(HW[:, :, :], 0.0).then_inc(pool_ready, 1)
            nc.gpsimd.memset(h2[:, :], 0.0).then_inc(pool_ready, 1)
            nc.gpsimd.memset(zeros[:, :], 0.0).then_inc(pool_ready, 1)
            nc.gpsimd.memset(epsr[:, 0:1], EPS_RMS).then_inc(pool_ready, 1)
            nc.gpsimd.memset(epsr[:, 1:2], EPS_LN).then_inc(pool_ready, 1)
            nc.gpsimd.memset(base[:, :], 0.0).then_inc(pool_ready, 1)
            nc.gpsimd.memset(HB[:, N:PADN], 0.0).then_inc(pool_ready, 1)
            nc.gpsimd.memset(YS[:, :, N:PADN], 0.0).then_inc(pool_ready, 1)
            pool.wait_ge(init_stored, 16)

            def sum_(i, g):
                pool.wait_ge(mul_done, i * MULS + (g + 1) * 2 * QN)
                nc.gpsimd.tensor_tensor(hs[:, g % HBUF, 0:2, :], hs[:, g % HBUF, 0:2, :], hs[:, g % HBUF, 2:4, :], ALU.add).then_inc(half_summed, 1)
                pool.wait_ge(half_summed, i * QUARTERS + g + 1)
                nc.gpsimd.tensor_tensor(hs[:, g % HBUF, 0, :], hs[:, g % HBUF, 0, :], hs[:, g % HBUF, 1, :], ALU.add).then_inc(summed, 1)

            def keep(i):
                pool.wait_ge(h_ready, i + 1)
                if not is_first(i):
                    pool.wait_ge(m_done, i)
                pool.sem_inc(pool_waited, 1)
                nc.gpsimd.tensor_copy(HB[:, 0:N], H[:, :]).then_inc(h_kept, 1)

            def route(i):
                pool.wait_ge(slot_ready, i + 1)
                pool.sem_inc(pool_waited, 1)
                for j in range(NC4 * 8):
                    nc.gpsimd.indirect_dma_start(
                        out=slot_d[:, :], out_offset=bass.IndirectOffsetOnAxis(ap=sloti[:, j:j + 1], axis=0),
                        in_=toki[:, j // 8:j // 8 + 1], in_offset=None,
                        bounds_check=SLOTS - 1, oob_is_err=False).then_inc(sent_a if j % 2 else sent_b, 16)
                pool.wait_ge(sent_a, i * 256 + 256)
                pool.wait_ge(sent_b, i * 256 + 256)
                pool.sem_inc(pool_waited, 1)

            def route_unit(i):
                while_open(pool, i, pool_waited, pool_read, route)
                pool.sem_inc(slots_free, 1)

            def front_half(i, until):
                for l in range(2):
                    until(f"qkv.{l}.1")
                    pool.wait_ge(k_ready, i * 4 + l * 2 + 2)
                    nc.gpsimd.tensor_tensor(KM[:, 1, :, :], K[:, 1:2, :].to_broadcast([128, HEADS, TP]), c("heads").unsqueeze(2).to_broadcast([128, HEADS, TP]), ALU.mult).then_inc(km1_ready, 1)

            pool.sem_inc(slots_free, 1)
            loop(pool, front_half, {"sum": sum_, "keep": keep, "route": route_unit})
            pool.sem_inc(sent_all, 1)
            pool.wait_ge(rows_stored, 16 + 32 * STEPS)
            pool.sem_inc(pair_free, 2)

            def gather(e, c, h):
                if h == 0:
                    pool.wait_ge(slots_loaded[c], e * 16 + 16)
                    pool.sem_inc(pool_waited, 1)
                for k in (2 * h, 2 * h + 1):
                    nc.gpsimd.indirect_dma_start(
                        out=ex[c % 2][:, k, :], out_offset=None, in_=rows_d[:, :],
                        in_offset=bass.IndirectOffsetOnAxis(ap=eidx[:, c, k:k + 1], axis=0)).then_inc(gathered[c % 2], 16)

            def add(e, c, more=True):
                p = e * 4 + c
                pool.wait_ge(e_out, p + 1)
                pool.sem_inc(pool_waited, 1)
                for h in range(2):
                    for k in (2 * h, 2 * h + 1):
                        nc.gpsimd.indirect_dma_start(
                            out=sum_d[:, :], out_offset=bass.IndirectOffsetOnAxis(ap=eidx[:, c, k:k + 1], axis=0),
                            in_=eo[c % 2][:, k, :], in_offset=None, compute_op=ALU.add).then_inc(added, 16)
                    if more:
                        gather(e + (c + 2) // 4, (c + 2) % 4, h)
                    pool.wait_ge(added, p * 64 + 32 * h + 32)
                    pool.sem_inc(pool_waited, 1)
                pool.sem_inc(pair_free, 1)

            for n in range(2):
                for h in range(2):
                    gather(0, n, h)
            with pool.Fori(0, E // 8 - 1) as e:
                for n in range(4):
                    add(e, n)
            for n in range(4):
                add(E // 8 - 1, n, more=n < 2)
            pool.sem_inc(all_added, 1)

        @block.scalar
        def _(act):
            act.preload_act_table_set("natural_log_exp_and_others")
            setup = chain(act, act_setup, 100)
            act.wait_ge(loaded, 16 * 5)
            act.wait_ge(pool_ready, 13)
            nc.scalar.activation(bcsel[:, :, :], hs[0:96, :, :, :].rearrange("p a b t -> p (a b t)")[:, 0:2 * NS * D].rearrange("p (n d) -> p n d", d=D), ACT.Copy)
            nc.scalar.activation(before_h[:, :], c("before"), ACT.Copy)
            nc.scalar.activation(ones_h[:, :], c("ones"), ACT.Copy)
            for n, d in enumerate("fb"):
                setup(nc.scalar.activation(aneg[:, n, :], v(f"alog{d}"), ACT.Exp), 0)
            setup(nc.scalar.activation(aneg[:, :, :], aneg[:, :, :], ACT.Copy, scale=-1.0), 0)
            nc.scalar.activation(epsr[:, :], epsr[:, :], ACT.Copy).then_inc(consts_ready, 1)

            front = chain(act, act_front, ACT_FRONT)

            def square(i, m, b):
                act.wait_ge(x_ready, i * 10 + m * 2 + b + 1)
                nc.scalar.activation(sq[:, b, :], X[:, b, :], ACT.Square).then_inc(sq_ready, 1)

            def root(i, m, b):
                act.wait_ge(ms_done, i * 10 + m * 2 + b + 1)
                front(nc.scalar.activation(rs[:, b, :], bank(b, 0, T), ACT.Ln, bias=epsr[:, 0:1]), i)
                nc.scalar.activation(rs[:, b, :], rs[:, b, :], ACT.Exp, scale=-0.5).then_inc(rs_ready, 1)

            def front_half(i, until):
                for b in range(G):
                    until(f"conv.{b}")
                    square(i, 0, b)
                for l in range(2):
                    for b in range(G):
                        until(f"norm.{l}.{b}")
                        root(i, 2 * l, b)
                    for b in range(G):
                        until(f"qkv.{l}.{b}")
                        act.wait_ge(q_done, i * 4 + l * 2 + b + 1)
                        nc.scalar.activation(K[:, b, :], psS[:, 2 * b, TP:2 * TP], ACT.Copy).then_inc(k_ready, 1)
                        nc.scalar.activation(Q[:, b, :], psS[:, 2 * b, 0:TP], ACT.Copy, scale=-(HD ** -0.5)).then_inc(q_ready, 1)

                    def take_values(q, b):
                        act.wait_ge(o_done, i * 8 + l * 4 + q * 2 + b + 1)
                        nc.scalar.activation(O[:, b, :, q * CT:(q + 1) * CT], psG[:, 0:2 * CT].rearrange("p (e t) -> p e t", e=2), ACT.Copy).then_inc(o_ready, 1)

                    for n, (q, h) in enumerate(ROUNDS):
                        for b in range(G):
                            k = i * 16 + l * 8 + n * 2 + b + 1
                            until(f"score{n}.{l}.{b}")
                            act.wait_ge(max_done, k)
                            for m in range(HEADS // 2):
                                last = nc.scalar.activation(P[:, b, m, 0:T], psS[0:CT, 2 * b + m // 2, m % 2 * T:(m % 2 + 1) * T], ACT.Exp, bias=least_s[:, b, m:m + 1], scale=-1.0)
                            last.then_inc(p_ready, 1)
                        for b in range(G):
                            k = i * 16 + l * 8 + n * 2 + b + 1
                            until(f"turn{n}.{l}.{b}")
                            if n == 2:
                                take_values(0, b)
                            act.wait_ge(t_done, k)
                            nc.scalar.activation(PT[:, b, 4 * h:4 * h + 4, :, :].rearrange("p (j e) c t -> p j (e c t)", e=2), psS[0:CT, 2 * b:2 * b + 2, 0:2 * TP], ACT.Copy).then_inc(pt_ready, 1)
                    for b in range(G):
                        until(f"value.{l}.{b}")
                        take_values(1, b)
                    for b in range(G):
                        until(f"den.{l}.{b}")
                        act.wait_ge(den_done, i * 4 + l * 2 + b + 1)
                        front(nc.scalar.activation(R[:, b, :], bank(b, 0, 2 * TP), ACT.Ln), i)
                        nc.scalar.activation(R[:, b, :], R[:, b, :], ACT.Exp, scale=-1.0).then_inc(inv_ready, 1)
                    for b in range(G):
                        until(f"wo.{l}.{b}")
                        square(i, 2 * l + 1, b)
                    for b in range(G):
                        until(f"norm2.{l}.{b}")
                        root(i, 2 * l + 1, b)
                    for b in range(G):
                        until(f"gate.{l}.{b}")
                        act.wait_ge(g_done, i * 4 + l * 2 + b + 1)
                        nc.scalar.activation(EF[0:FW, b, :, :], slices(b), ACT.Exp, scale=-1.0).then_inc(ge_ready, 1)
                    for b in range(G):
                        until(f"sig.{l}.{b}")
                        act.wait_ge(ge1_ready, i * 4 + l * 2 + b + 1)
                        front(nc.scalar.activation(EF[0:FW, b, :, :], EF[0:FW, b, :, :], ACT.Ln), i)
                        nc.scalar.activation(EF[0:FW, b, :, :], EF[0:FW, b, :, :], ACT.Exp, scale=-1.0).then_inc(gsig_ready, 1)
                    for b in range(G):
                        until(f"down.{l}.{b}")
                        square(i, 2 * l + 2, b)
                for b in range(G):
                    until(f"normf.{b}")
                    root(i, 4, b)

            back = chain(act, act_back, ACT_BACK)

            def project(i, d):
                act.wait_ge(xz_done, i * 2 + d + 1)
                if d and not is_first(i):
                    act.wait_ge(ys_ready, i * 2)
                nc.scalar.activation(XC[:, d, :, TAPS - 1:XW], psA[:, 0:N].rearrange("p (g t) -> p g t", g=G), ACT.Copy)
                nc.scalar.activation(XZ[:, d, 1, :], psB[:, 0:N], ACT.Copy).then_inc(xc_ready, 1)

            def sigmoid(i, d):
                act.wait_ge(xconv_ready, i * 2 + d + 1)
                nc.scalar.activation(SG[:, d, :, :], XZ[:, d, :, :], ACT.Exp, scale=-1.0).then_inc(sge_ready, 1)

            def gate(i, d):
                act.wait_ge(sg1_ready, i * 2 + d + 1)
                back(nc.scalar.activation(SG[:, d, :, :], SG[:, d, :, :], ACT.Ln), i)
                nc.scalar.activation(SG[:, d, :, :], SG[:, d, :, :], ACT.Exp, scale=-1.0).then_inc(sgr_ready, 1)

            def split(i, d):
                k = i * 2 + d + 1
                act.wait_ge(bc_done, k)
                nc.scalar.activation(hi[:, d, :], psA[0:96, 0:N], ACT.Copy).then_inc(hi_ready, 1)
                nc.scalar.activation(dtin[:, d, :], psY[0:DTR, 0:N], ACT.Copy).then_inc(dtin_ready, 1)
                act.wait_ge(res_ready, k)
                nc.scalar.activation(mid[:, :], res[:, :], ACT.Copy).then_inc(mid_ready, 1)

            def step_size(i, d):
                k = i * 2 + d + 1
                act.wait_ge(dtp_done, k)
                if d:
                    act.wait_ge(dt_ready, k - 1)
                nc.scalar.activation(sp[:, :], psY[:, 0:N], ACT.Abs, bias=v("bdt" + "fb"[d])).then_inc(abs_ready, 1)
                act.wait_ge(abs_ready, k)
                nc.scalar.activation(sp[:, :], sp[:, :], ACT.Exp, scale=-1.0).then_inc(spe_ready, 1)
                act.wait_ge(spe_ready, k)
                nc.scalar.activation(spl[:, :], sp[:, :], ACT.Ln, bias=1.0).then_inc(sp_ready, 1)

            def decay(i, g, k):
                d = g // (QUARTERS // 2)
                if k == 0 and g % (QUARTERS // 2) < 2:
                    act.wait_ge(dt_ready, i * 2 + d + 1)
                if k == 0 and g >= 2:
                    act.wait_ge(scan_ready, i * QUARTERS + g - 1)
                n = g % (QUARTERS // 2) * QN + k
                last = nc.scalar.activation(dA[:, g % 2, k, :], dt_[:, d, :], ACT.Exp, scale=aneg[:, d, n:n + 1])
                if k == QN - 1:
                    last.then_inc(da_ready, 1)

            def merge(i):
                act.wait_ge(mv_ready, i + 1)
                merging(nc.scalar.activation(rstd[:, :], mv[:, :, 1], ACT.Ln, bias=epsr[0:CT, 1:2]), i)
                nc.scalar.activation(rstd[:, :], rstd[:, :], ACT.Exp, scale=-0.5).then_inc(rstd_ready, 1)

            routing = chain(act, act_route, 2)
            merging = chain(act, act_merge, 1)

            def route(i):
                act.wait_ge(ht_done, i + 1)
                nc.scalar.activation(h2[:, :], psB[:, 0:PADN], ACT.Copy).then_inc(h2_ready, 1)
                act.wait_ge(lg_done, i + 1)
                flat = t1[:, :, :].rearrange("p c e -> p (c e)")
                routing(nc.scalar.activation(flat, psA[0:CT, 0:NC4 * E], ACT.Abs), i)
                routing(nc.scalar.activation(flat, flat, ACT.Exp, scale=-1.0), i)
                nc.scalar.activation(flat, flat, ACT.Ln, bias=1.0).then_inc(gl_ready, 1)
                act.wait_ge(gm_ready, i + 1)
                nc.scalar.activation(score[:, :, :], t1[:, :, :], ACT.Exp).then_inc(score_ready, 1)

            loop(act, front_half, {
                "project": project, "sigmoid": sigmoid, "gate": gate, "split": split, "dt": step_size, "decay": decay,
                "merge": merge, "route": lambda i: while_open(act, i, act_waited, act_read, route)})
            assert front.count[0] == ACT_FRONT and back.count[0] == ACT_BACK, (front.count, back.count)

            with act.Fori(0, E // 2) as p:
                act.wait_ge(xt_done, p + 1)
                nc.scalar.activation(exT, psS[:, 0, 0:2 * CAP], ACT.Copy).then_inc(xt_ready, 1)
                act.wait_ge(e13_done, p + 1)
                nc.scalar.activation(ea, psS[0:MD, 1, 0:2 * CAP], ACT.Exp, scale=-1.0).then_inc(e_exp, 1)
                act.wait_ge(e_one, p + 1)
                nc.scalar.activation(ea, ea, ACT.Ln).then_inc(e_ln, 1)
                act.wait_ge(e_ln, p + 1)
                nc.scalar.activation(ea, ea, ACT.Exp, scale=-1.0).then_inc(e_sig, 1)
            for n, (t, m) in enumerate(FINAL):
                act.wait_ge(fin_mv, n + 1)
                nc.scalar.activation(frs[n % 2][0:B, 0:m], fmv[n % 2][0:B, 0:m, 1], ACT.Ln, bias=epsr[0:B, 1:2]).then_inc(fin_ln, 1)
                act.wait_ge(fin_ln, n + 1)
                nc.scalar.activation(frs[n % 2][0:B, 0:m], frs[n % 2][0:B, 0:m], ACT.Exp, scale=-0.5).then_inc(fin_rs, 1)

        @block.vector
        def _(dve):
            setup = chain(dve, dve_setup, 100)
            dve.wait_ge(loaded, 16 * 5)
            for l in range(2):
                for n in ("q", "k", "v"):
                    nc.vector.tensor_scalar(w(f"{n}{l}"), w(f"{n}{l}"), v(f"ln1{l}"), None, ALU.mult)
                for n in ("gate", "up"):
                    nc.vector.tensor_scalar(w(f"{n}{l}"), w(f"{n}{l}"), v(f"ln2{l}"), None, ALU.mult)
            for n, d in enumerate("fb"):
                nc.vector.tensor_scalar(dskip[:, n, :], c("ident"), v(f"dskip{d}"), None, ALU.mult)
            nc.vector.tensor_scalar(posb[:, :], v("pos"), v("convb"), None, ALU.add)
            nc.vector.tensor_tensor(cls0[:, :], v("cls"), v("pos", 0, 1), ALU.add)
            nc.vector.tensor_copy(tokf[:, :], c("tok0")[0:CT, :])
            setup(nc.vector.tensor_copy(unused[:, :], c("unused")), 0)
            nc.vector.tensor_copy(open_[:, :], c("ones")[0:1, 0:1]).then_inc(open_ready, 1)
            dve.wait_ge(pool_ready, 13)
            dve.wait_ge(consts_ready, 1)
            dve.sem_inc(unused_ready, 1)
            dve.sem_inc(weights_ready, 1)

            front = chain(dve, dve_front, DVE_FRONT)

            def apply_norm(i, m, b):
                dve.wait_ge(rs_ready, i * 10 + m * 2 + b + 1)
                nc.vector.tensor_tensor(Hn[:, b, 0:T], X[:, b, :], rs[:, b, :], ALU.mult).then_inc(hn_ready, 1)

            def front_half(i, until):
                for b in range(G):
                    until(f"conv.{b}")
                    dve.wait_ge(conv_done, i * 2 + b + 1)
                    front(nc.vector.tensor_tensor(X[:, b, 1:T], bank(b, 0, NP), posb[:, 1:T], ALU.add), i)
                    nc.vector.tensor_copy(X[:, b, 0:1], cls0[:, :]).then_inc(x_ready, 1)
                for l in range(2):
                    for b in range(G):
                        until(f"norm.{l}.{b}")
                        apply_norm(i, 2 * l, b)
                    for b in range(G):
                        k = i * 4 + l * 2 + b + 1
                        until(f"qkv.{l}.{b}")
                        if b == 0:
                            dve.wait_ge(k_ready, k)
                            nc.vector.tensor_tensor(KM[:, 0, :, :], K[:, 0:1, :].to_broadcast([128, HEADS, TP]), c("heads").unsqueeze(2).to_broadcast([128, HEADS, TP]), ALU.mult).then_inc(km0_ready, 1)
                        dve.wait_ge(v_done, k)
                        nc.vector.tensor_copy(V[:, b, :, :, 0:HD], psS[0:CT, 2 * b + 1, 0:NQ * D].rearrange("p (c h d) -> p c h d", c=NQ, h=HEADS)).then_inc(v_ready, 1)
                    for n, (q, h) in enumerate(ROUNDS):
                        for b in range(G):
                            until(f"score{n}.{l}.{b}")
                            dve.wait_ge(s_done, i * 16 + l * 8 + n * 2 + b + 1)
                            nc.vector.tensor_reduce(least_s[:, b, :], psS[0:CT, 2 * b:2 * b + 2, 0:2 * T].rearrange("p j (e t) -> p j e t", e=2), axis=AX, op=ALU.min).then_inc(max_done, 1)
                        for b in range(G):
                            until(f"turn{n}.{l}.{b}")
                    for b in range(G):
                        until(f"value.{l}.{b}")
                    for b in range(G):
                        until(f"den.{l}.{b}")
                        dve.wait_ge(inv_ready, i * 4 + l * 2 + b + 1)
                        Ob = O[:, b, :, :].rearrange("p e t -> p (e t)")
                        nc.vector.tensor_tensor(Ob, Ob, R[:, b, :], ALU.mult).then_inc(on_ready, 1)
                    for b in range(G):
                        until(f"wo.{l}.{b}")
                        dve.wait_ge(wo_done, i * 4 + l * 2 + b + 1)
                        nc.vector.tensor_tensor(X[:, b, :], X[:, b, :], bank(b, 0, T), ALU.add).then_inc(x_ready, 1)
                    for b in range(G):
                        until(f"norm2.{l}.{b}")
                        apply_norm(i, 2 * l + 1, b)
                    for b in range(G):
                        until(f"gate.{l}.{b}")
                        dve.wait_ge(ge_ready, i * 4 + l * 2 + b + 1)
                        nc.vector.tensor_scalar(EF[0:FW, b, :, :], EF[0:FW, b, :, :], EXP_MAX, 1.0, ALU.min, ALU.add).then_inc(ge1_ready, 1)
                    for b in range(G):
                        until(f"sig.{l}.{b}")
                        dve.wait_ge(gsig_ready, i * 4 + l * 2 + b + 1)
                        nc.vector.tensor_tensor(EF[0:FW, b, :, :], EF[0:FW, b, :, :], slices(b), ALU.mult).then_inc(gs_ready, 1)
                    for b in range(G):
                        until(f"up.{l}.{b}")
                        dve.wait_ge(u_done, i * 4 + l * 2 + b + 1)
                        nc.vector.tensor_tensor(EF[0:FW, b, :, :], EF[0:FW, b, :, :], slices(b), ALU.mult).then_inc(ff_ready, 1)
                    for b in range(G):
                        until(f"down.{l}.{b}")
                        dve.wait_ge(down_done, i * 4 + l * 2 + b + 1)
                        nc.vector.tensor_tensor(X[:, b, :], X[:, b, :], bank(b, 0, T), ALU.add).then_inc(x_ready, 1)
                for b in range(G):
                    until(f"normf.{b}")
                    if not b and not is_first(i):
                        dve.wait_ge(h_kept, i)
                        dve.wait_ge(xc_ready, i * 2)
                    dve.wait_ge(rs_ready, i * 10 + 8 + b + 1)
                    front(nc.vector.scalar_tensor_tensor(out=H[:, b * T:(b + 1) * T], in0=X[:, b, :], scalar=v("lnf"), in1=rs[:, b, :], op0=ALU.mult, op1=ALU.mult), i)
                nc.vector.tensor_copy(Hr[:, :], H[:, ::-1]).then_inc(h_ready, 1)

            back = chain(dve, dve_back, DVE_BACK)

            def conv(i, d):
                dve.wait_ge(xc_ready, i * 2 + d + 1)
                xconv = XZ[:, d, 0, :].rearrange("p (g t) -> p g t", g=G)
                back(nc.vector.tensor_scalar(xconv, XC[:, d, :, 0:T], v("taps" + "fb"[d], 0, 1), v("bconv" + "fb"[d]), ALU.mult, ALU.add), i)
                for tap in range(1, TAPS):
                    ins = nc.vector.scalar_tensor_tensor(out=xconv, in0=XC[:, d, :, tap:tap + T], scalar=v("taps" + "fb"[d], tap, tap + 1), in1=xconv, op0=ALU.mult, op1=ALU.add)
                    if tap < TAPS - 1:
                        back(ins, i)
                    else:
                        ins.then_inc(xconv_ready, 1)

            def sigmoid(i, d):
                dve.wait_ge(sge_ready, i * 2 + d + 1)
                nc.vector.tensor_scalar(SG[:, d, :, :], SG[:, d, :, :], EXP_MAX, 1.0, ALU.min, ALU.add).then_inc(sg1_ready, 1)

            def gate(i, d):
                dve.wait_ge(sgr_ready, i * 2 + d + 1)
                nc.vector.tensor_tensor(XZ[:, d, :, :], XZ[:, d, :, :], SG[:, d, :, :], ALU.mult).then_inc(xs_ready, 1)

            def split(i, d):
                if d:
                    dve.wait_ge(bcs_ready, i * 2 + 1)
                dve.wait_ge(hi_ready, i * 2 + d + 1)
                nc.vector.scalar_tensor_tensor(out=res[:, :], in0=hi[:, d, :], scalar=c("part1")[0:96, :], in1=psA[0:96, 0:N], op0=ALU.mult, op1=ALU.add).then_inc(res_ready, 1)
                dve.wait_ge(mid_ready, i * 2 + d + 1)
                nc.vector.scalar_tensor_tensor(out=bc[:, d, :], in0=mid[:, :], scalar=c("part2")[0:96, :], in1=res[:, :], op0=ALU.mult, op1=ALU.add).then_inc(bcs_ready, 1)

            def step_size(i, d):
                k = i * 2 + d + 1
                dve.wait_ge(abs_ready, k)
                nc.vector.tensor_scalar(dt_[:, d, :], psY[:, 0:N], v("bdt" + "fb"[d]), 0.0, ALU.add, ALU.max).then_inc(dtm_ready, 1)
                dve.wait_ge(spe_ready, k)
                nc.vector.tensor_scalar(small[:, :], sp[:, :], LOG1P_SERIES, None, ALU.is_lt)
                back(nc.vector.tensor_scalar(u[:, d, :], sp[:, :], 1 / 3, -0.5, ALU.mult, ALU.add), i)
                back(nc.vector.tensor_tensor(u[:, d, :], u[:, d, :], sp[:, :], ALU.mult), i)
                dve.wait_ge(sp_ready, k)
                back(nc.vector.scalar_tensor_tensor(out=u[:, d, :], in0=u[:, d, :], scalar=1.0, in1=sp[:, :], op0=ALU.add, op1=ALU.mult), i)
                dve.sem_inc(dve_waited, 1)
                back(nc.vector.copy_predicated(spl[:, :], small[:, :], u[:, d, :]), i)
                dve.wait_ge(dtm_ready, k)
                nc.vector.tensor_tensor(dt_[:, d, :], dt_[:, d, :], spl[:, :], ALU.add).then_inc(dt_ready, 1)
                dve.wait_ge(dt_ready, k)
                back(nc.vector.tensor_tensor(u[:, d, :], dt_[:, d, :], XZ[:, d, 0, :], ALU.mult), i)

            def input_(i, g, k):
                m = 2 * QN * g + k
                if k == 0 and g >= HBUF:
                    dve.wait_ge(acc_done, i * QUARTERS + g - HBUF + 1)
                dve.wait_ge(bb_done, i * MULS + m + 1)
                nc.vector.tensor_tensor(hs[:, g % HBUF, k, :], u[:, g // (QUARTERS // 2), :], AB[m % 2][:, 0:N], ALU.mult).then_inc(mul_done, 1)

            def scan(i, g):
                dve.wait_ge(da_ready, i * QUARTERS + g + 1)
                nc.vector.memset(dA[:, g % 2, :, :].rearrange("p n (g t) -> p (n g) t", g=G)[:, :, 0:1], 0.0).then_inc(zeroed, 1)
                dve.wait_ge(zeroed, i * QUARTERS + g + 1)
                dve.wait_ge(mul_done, i * MULS + 2 * QN * g + QN)
                h = hs[:, g % HBUF, :, :].rearrange("p n t -> p (n t)")
                nc.vector.tensor_tensor_scan(h, dA[:, g % 2, :, :].rearrange("p n t -> p (n t)"), h, 0.0, ALU.mult, ALU.add).then_inc(scan_ready, 1)

            def output(i, g, k):
                m = 2 * QN * g + QN + k
                if k == 0:
                    dve.wait_ge(scan_ready, i * QUARTERS + g + 1)
                dve.wait_ge(bb_done, i * MULS + m + 1)
                nc.vector.tensor_tensor(hs[:, g % HBUF, k, :], hs[:, g % HBUF, k, :], AB[m % 2][:, 0:N], ALU.mult).then_inc(mul_done, 1)

            def sum_(i, g):
                if g % (QUARTERS // 2) == QUARTERS // 2 - 1:
                    d = g // (QUARTERS // 2)
                    dve.wait_ge(y_done, i * 2 + d + 1)
                    nc.vector.tensor_tensor(YS[:, d, 0:N][:, ::-1] if d else YS[:, d, 0:N], psY[:, 0:N], XZ[:, d, 1, :], ALU.mult).then_inc(ys_ready, 1)

            def merge(i):
                dve.wait_ge(m_done, i + 1)
                tokens = psY[0:CT, 0:NC4 * D].rearrange("p (c d) -> p c d", c=NC4)
                for q in range(NC4):
                    last = nc.vector.bn_stats(stats[:, q, :], tokens[:, q, :])
                merging(last, i)
                dve.sem_inc(dve_waited, 1)
                for q in range(NC4):
                    last = nc.vector.bn_aggr(mv[:, q, :], stats[:, q, :])
                last.then_inc(mv_ready, 1)
                dve.wait_ge(mv_ready, i + 1)
                dve.wait_ge(rstd_ready, i + 1)
                dve.wait_ge(rows_stored, i * 32 + 16)
                dve.wait_ge(hw_free, i + 1)
                for q in range(NC4):
                    last = nc.vector.tensor_scalar(HW[:, q, 0:D], tokens[:, q, :], mv[:, q, 0:1], rstd[:, q:q + 1], ALU.subtract, ALU.mult)
                last.then_inc(ht_ready, 1)

            routing = chain(dve, dve_route, DVE_ROUTE)
            merging = chain(dve, dve_merge, 1)

            def route(i):
                dve.wait_ge(gl_ready, i + 1)
                nc.vector.scalar_tensor_tensor(out=t1[:, :, :].rearrange("p c e -> p (c e)"), in0=psA[0:CT, 0:NC4 * E], scalar=0.0, in1=t1[:, :, :].rearrange("p c e -> p (c e)"), op0=ALU.min, op1=ALU.subtract).then_inc(gm_ready, 1)
                dve.wait_ge(score_ready, i + 1)
                routing(nc.vector.tensor_tensor(ext[:, :, 0:8].rearrange("p (c g) k -> p c g k", c=NC4), score[:, :, :].rearrange("p c (g k) -> p c g k", k=8), gateb[0:CT, :].rearrange("p (g k) -> p g k", k=8).unsqueeze(1).to_broadcast([CT, NC4, GR, 8]), ALU.add), i)
                routing(nc.vector.tensor_copy(ext[:, :, 8:12], ext[:, :, 0:4]), i)
                for s in range(1, 5):
                    last = nc.vector.tensor_tensor(pairs[:, :, s - 1, :], ext[:, :, 0:8], ext[:, :, s:s + 8], ALU.add)
                routing(last, i)
                routing(nc.vector.tensor_reduce(gs[:, :, :].rearrange("p c g -> p (c g)"), pairs[:, :, :, :].rearrange("p m s k -> p m (s k)"), axis=AX, op=ALU.max), i)
                them = gs[:, :, :].unsqueeze(2).to_broadcast([CT, NC4, GR, GR])
                mine = gs[:, :, :].unsqueeze(3).to_broadcast([CT, NC4, GR, GR])
                routing(nc.vector.tensor_tensor(cmp1[:, :, :, :], them, mine, ALU.is_gt), i)
                routing(nc.vector.tensor_tensor(cmp2[:, :, :, :], them, mine, ALU.is_equal), i)
                fore = c("groupbefore")[0:CT, :].unsqueeze(1).to_broadcast([CT, NC4, GR * GR])
                c1, c2 = (x[:, :, :, :].rearrange("p c g h -> p c (g h)") for x in (cmp1, cmp2))
                routing(nc.vector.tensor_tensor(c2, c2, fore, ALU.mult), i)
                routing(nc.vector.tensor_tensor(c1, c1, c2, ALU.add), i)
                routing(nc.vector.tensor_reduce(rank[:, :], cmp1[:, :, :, :].rearrange("p c g h -> p (c g) h"), axis=AX, op=ALU.add), i)
                routing(nc.vector.tensor_scalar(rank[:, :], rank[:, :], float(TOPG), -BIG, ALU.is_ge, ALU.mult), i)
                m8 = masked[:, :, :].rearrange("p c (g k) -> p (c g) k", k=8)
                routing(nc.vector.tensor_tensor(m8, ext[:, :, 0:8], rank[:, :].unsqueeze(2).to_broadcast([CT, NC4 * GR, 8]), ALU.add), i)
                dve.sem_inc(dve_waited, 1)
                for q in range(NC4):
                    last = nc.vector.max(top8[:, q, :], masked[:, q, :])
                routing(last, i)
                dve.sem_inc(dve_waited, 1)
                for q in range(NC4):
                    last = nc.vector.match_replace(out=rest[:, q, :], in_to_replace=top8[:, q, :], in_values=masked[:, q, :], imm_value=-3e38)
                routing(last, i)
                routing(nc.vector.tensor_tensor(sel[:, :, :], rest[:, :, :], masked[:, :, :], ALU.not_equal), i)
                routing(nc.vector.tensor_tensor(score[:, :, :], score[:, :, :], sel[:, :, :], ALU.mult), i)
                routing(nc.vector.tensor_reduce(wsum[:, :], score[:, :, :], axis=AX, op=ALU.add), i)
                routing(nc.vector.reciprocal(winv[:, :], wsum[:, :]), i)
                routing(nc.vector.tensor_tensor(sel[:, :, :], sel[:, :, :], c("valid")[0:CT, :].unsqueeze(2).to_broadcast([CT, NC4, E]), ALU.mult), i)
                nc.vector.tensor_copy(selh[:, :, :], sel[:, :, :]).then_inc(sel_ready, 1)
                nc.vector.scalar_tensor_tensor(out=HW[:, :, D:ROW], in0=score[:, :, :], scalar=ROUTE_SCALE, in1=winv[:, :].unsqueeze(2).to_broadcast([CT, NC4, E]), op0=ALU.mult, op1=ALU.mult).then_inc(hw_ready, 1)
                dve.wait_ge(pos_done, i + 1)
                routing(nc.vector.tensor_tensor(pos[:, :, :], psA[0:CT, 0:NC4 * E].rearrange("p (c e) -> p c e", c=NC4), base[:, :].unsqueeze(1).to_broadcast([CT, NC4, E]), ALU.add), i)
                routing(nc.vector.tensor_tensor(base[:, :], base[:, :], psA[0:CT, NC4 * E:NC4 * E + E], ALU.add), i)
                routing(nc.vector.scalar_tensor_tensor(out=sel[:, :, :], in0=pos[:, :, :], scalar=float(CAP), in1=sel[:, :, :], op0=ALU.is_lt, op1=ALU.mult), i)
                routing(nc.vector.tensor_tensor(pos[:, :, :], pos[:, :, :], c("slot1")[0:CT, :].unsqueeze(1).to_broadcast([CT, NC4, E]), ALU.add), i)
                routing(nc.vector.tensor_tensor(pos[:, :, :], pos[:, :, :], sel[:, :, :], ALU.mult), i)
                dve.sem_inc(dve_waited, 1)
                for q in range(NC4):
                    last = nc.vector.max(slotf[:, q, :], pos[:, q, :])
                routing(last, i)
                routing(nc.vector.tensor_scalar(noslot[:, :, :], slotf[:, :, :], 0.0, float(NOSLOT), ALU.is_equal, ALU.mult), i)
                dve.wait_ge(slots_free, i + 1)
                nc.vector.scalar_tensor_tensor(out=sloti[:, :], in0=slotf[:, :, :].rearrange("p c k -> p (c k)"), scalar=-1.0, in1=noslot[:, :, :].rearrange("p c k -> p (c k)"), op0=ALU.add, op1=ALU.add)
                routing(nc.vector.tensor_copy(toki[:, :], tokf[:, :]), i)
                nc.vector.tensor_scalar(tokf[:, :], tokf[:, :], float(N), None, ALU.add).then_inc(slot_ready, 1)
                routing(nc.vector.tensor_reduce(least[:, :], base[0:1, :], axis=AX, op=ALU.min), i)
                for flag_read in (act_read, pe_read, pool_read, q_read):
                    dve.wait_ge(flag_read, i + 1)
                nc.vector.tensor_scalar(open_[:, :], least[:, :], float(CAP), None, ALU.is_lt).then_inc(flag_set, 1)
                dve.wait_ge(flag_set, i + 1)
                dve.sem_inc(dve_waited, 1)

            def route_unit(i):
                while_open(dve, i, dve_waited, dve_read, route)
                dve.sem_inc(open_ready, 1)

            loop(dve, front_half, {
                "conv": conv, "sigmoid": sigmoid, "gate": gate, "split": split, "dt": step_size, "input": input_,
                "scan": scan, "output": output, "sum": sum_, "merge": merge, "route": route_unit})
            assert (front.count[0], back.count[0], routing.count[0]) == (DVE_FRONT, DVE_BACK, DVE_ROUTE), (front.count, back.count, routing.count)

            with dve.Fori(0, E // 4) as e:
                for b in range(2):
                    k = 2 * e + b + 1
                    dve.wait_ge(e_exp, k)
                    nc.vector.tensor_scalar(ea, ea, EXP_MAX, 1.0, ALU.min, ALU.add).then_inc(e_one, 1)
                    dve.wait_ge(e_sig, k)
                    nc.vector.tensor_tensor(ea, ea, psS[0:MD, 1, 0:2 * CAP], ALU.mult).then_inc(e_mul, 1)
                    dve.wait_ge(e_mul, k)
                    nc.vector.tensor_tensor(ea, ea, psS[0:MD, 2, 0:2 * CAP], ALU.mult).then_inc(e_act, 1)
                    dve.wait_ge(pair_free, k)
                    dve.wait_ge(e2_done, k)
                    for q in range(4):
                        ins = nc.vector.tensor_scalar(eo[b][:, q, :], psS[:, 3, q * D:(q + 1) * D], ex[b][:, q, bass.ds(e * 4 + 2 * b + q // 2 + D, 1)], None, ALU.mult)
                    ins.then_inc(e_out, 1)
            def normalise(n):
                t, m = FINAL[n]
                buf, f = fbuf[n % HBUF], n % 2
                dve.wait_ge(fin_rs, n + 1)
                nc.vector.tensor_tensor(buf[0:B, 0:m, :], buf[0:B, 0:m, :], fmv[f][0:B, 0:m, 0:1].to_broadcast([B, m, D]), ALU.subtract).then_inc(fin_sub, 1)
                dve.wait_ge(fin_sub, n + 1)
                nc.vector.tensor_tensor(buf[0:B, 0:m, :], buf[0:B, 0:m, :], frs[f][0:B, 0:m].unsqueeze(2).to_broadcast([B, m, D]), ALU.mult).then_inc(fin_ready, 1)

            for n, (t, m) in enumerate(FINAL):
                dve.wait_ge(fin_loaded[n % HBUF], 16 * (n // HBUF + 1))
                for q in range(m):
                    last = nc.vector.bn_stats(fst[n % 2][0:B, q, :], fbuf[n % HBUF][0:B, q, :])
                last.then_inc(fin_stats, 1)
                dve.wait_ge(fin_stats, n + 1)
                for q in range(m):
                    last = nc.vector.bn_aggr(fmv[n % 2][0:B, q, :], fst[n % 2][0:B, q, :])
                last.then_inc(fin_mv, 1)
                if n:
                    normalise(n - 1)
            normalise(len(FINAL) - 1)

        @block.tensor
        def _(pe):
            mm = nc.tensor.matmul
            pe.wait_ge(weights_ready, 1)

            def mean_square(i, m, b):
                pe.wait_ge(sq_ready, i * 10 + m * 2 + b + 1)
                mm(bank(b, 0, T), c("mean"), sq[:, b, :], start=True, stop=True).then_inc(ms_done, 1)

            def front_half(i, until):
                for b in range(G):
                    stage = f"conv.{b}"
                    until(stage, 1, KP + 1)
                    if b == 0:
                        pe.wait_ge(patches_loaded, i * 16 + 16)
                        if not is_first(i):
                            pe.wait_ge(h_ready, i)
                    for k in range(KP):
                        last = mm(bank(b, 0, NP), w("conv", k * D, (k + 1) * D), pat[:, k, b * NP:(b + 1) * NP], start=k == 0, stop=k == KP - 1)
                        until(stage, k + 2, KP + 1)
                    last.then_inc(conv_done, 1)
                for l in range(2):
                    for b in range(G):
                        until(f"norm.{l}.{b}")
                        mean_square(i, 2 * l, b)
                    for b in range(G):
                        stage = f"qkv.{l}.{b}"
                        until(stage, 1, 4)
                        pe.wait_ge(hn_ready, i * 8 + 4 * l + b + 1)
                        mm(psS[:, 2 * b, TP:2 * TP], w(f"k{l}"), Hn[:, b, :], start=True, stop=True)
                        until(stage, 2, 4)
                        mm(psS[:, 2 * b, 0:TP], w(f"q{l}"), Hn[:, b, :], start=True, stop=True).then_inc(q_done, 1)
                        until(stage, 3, 4)
                        for q in range(NQ):
                            last = mm(psS[0:CT, 2 * b + 1, q * D:(q + 1) * D], Hn[:, b, q * CT:(q + 1) * CT], w(f"v{l}"), start=True, stop=True)
                        last.then_inc(v_done, 1)
                        until(stage)

                    def values(q, b):
                        pe.wait_ge(pt_ready, i * 16 + l * 8 + (2 * q + 1) * 2 + b + 1)
                        if q or b:
                            pe.wait_ge(o_ready, i * 8 + l * 4 + q * 2 + b)
                        for e in range(2):
                            for k in range(NQ):
                                for j in range(4):
                                    last = mm(psG[32 * j:32 * j + 32, e * CT:(e + 1) * CT], V[:, b, k, 2 * j + e, :], PT[:, b, 2 * j + e, k, :], start=k == 0, stop=k == NQ - 1, tile_position=(0, 32 * j))
                        last.then_inc(o_done, 1)

                    for n, (q, h) in enumerate(ROUNDS):
                        for b in range(G):
                            stage = f"score{n}.{l}.{b}"
                            k = i * 16 + l * 8 + n * 2 + b + 1
                            until(stage, 1, 3)
                            if n == 0:
                                pe.wait_ge(q_ready, i * 4 + l * 2 + b + 1)
                                pe.wait_ge((km0_ready, km1_ready)[b], i * 2 + l + 1)
                                pe.wait_ge(v_ready, i * 4 + l * 2 + b + 1)
                            else:
                                pe.wait_ge(pt_ready, k - 2)
                            for j in range(2):
                                m = 4 * h + 2 * j
                                last = mm(psS[0:CT, 2 * b + j, 0:2 * T].rearrange("p (e t) -> p e t", e=2), Q[:, b, q * CT:(q + 1) * CT], KM[:, b, m:m + 2, 0:T], start=True, stop=True)
                                if j:
                                    last.then_inc(s_done, 1)
                                until(stage, 2 + j, 3)
                        for b in range(G):
                            stage = f"turn{n}.{l}.{b}"
                            if n == 2:
                                values(0, b)
                            until(stage, 1, 2)
                            pe.wait_ge(p_ready, i * 16 + l * 8 + n * 2 + b + 1)
                            for m in range(HEADS // 2):
                                for e in range(NQ):
                                    at = (m % 2 * NQ + e) * CT
                                    last = nc.tensor.transpose(psS[0:CT, 2 * b + m // 2, at:at + CT], P[:, b, m, e * CT:(e + 1) * CT], c("ident")[0:CT, 0:CT])
                            last.then_inc(t_done, 1)
                            until(stage)
                    for b in range(G):
                        until(f"value.{l}.{b}", 1, 2)
                        values(1, b)
                        until(f"value.{l}.{b}")
                    for b in range(G):
                        until(f"den.{l}.{b}", 1, 2)
                        pe.wait_ge(o_ready, i * 8 + l * 4 + 2 + b + 1)
                        mm(bank(b, 0, 2 * TP), c("dsel"), O[:, b, :, :].rearrange("p e t -> p (e t)"), start=True, stop=True).then_inc(den_done, 1)
                        until(f"den.{l}.{b}")
                    for b in range(G):
                        until(f"wo.{l}.{b}", 1, 2)
                        pe.wait_ge(on_ready, i * 4 + l * 2 + b + 1)
                        for e in range(2):
                            last = mm(bank(b, 0, T), w(("woe", "woo")[e] + str(l)), O[:, b, e, 0:T], start=e == 0, stop=e == 1)
                        last.then_inc(wo_done, 1)
                        until(f"wo.{l}.{b}")
                    for b in range(G):
                        until(f"norm2.{l}.{b}")
                        mean_square(i, 2 * l + 1, b)
                    for b in range(G):
                        until(f"gate.{l}.{b}", 1, 3)
                        pe.wait_ge(hn_ready, i * 8 + 4 * l + 2 + b + 1)
                        for f in range(FC):
                            last = mm(slices(b)[:, f, :], w(f"gate{l}", f * FW, (f + 1) * FW), Hn[:, b, 0:T], start=True, stop=True)
                            if f == 1:
                                until(f"gate.{l}.{b}", 2, 3)
                        last.then_inc(g_done, 1)
                        until(f"gate.{l}.{b}")
                    for b in range(G):
                        until(f"sig.{l}.{b}")
                    for b in range(G):
                        until(f"up.{l}.{b}", 1, 3)
                        pe.wait_ge(gs_ready, i * 4 + l * 2 + b + 1)
                        for f in range(FC):
                            last = mm(slices(b)[:, f, :], w(f"up{l}", f * FW, (f + 1) * FW), Hn[:, b, 0:T], start=True, stop=True)
                            if f == 1:
                                until(f"up.{l}.{b}", 2, 3)
                        last.then_inc(u_done, 1)
                        until(f"up.{l}.{b}")
                    for b in range(G):
                        until(f"down.{l}.{b}", 1, 3)
                        pe.wait_ge(ff_ready, i * 4 + l * 2 + b + 1)
                        for f in range(FC):
                            last = mm(bank(b, 0, T), w(f"down{l}", f * D, (f + 1) * D)[0:FW, :], EF[0:FW, b, f, :], start=f == 0, stop=f == FC - 1)
                            if f == 1:
                                until(f"down.{l}.{b}", 2, 3)
                        last.then_inc(down_done, 1)
                        until(f"down.{l}.{b}")
                for b in range(G):
                    until(f"normf.{b}")
                    mean_square(i, 4, b)

            def project(i, d):
                s = "fb"[d]
                if d:
                    pe.wait_ge(xc_ready, i * 2 + 1)
                else:
                    pe.wait_ge(h_ready, i + 1)
                    if not is_first(i):
                        pe.wait_ge(mul_done, i * MULS)
                        pe.wait_ge(open_ready, i)
                x = (H, Hr)[d][:, :]
                mm(psA[:, 0:N], w(f"win{s}", 0, D), x, start=True, stop=True)
                mm(psB[:, 0:N], w(f"win{s}", D, 2 * D), x, start=True, stop=True).then_inc(xz_done, 1)

            def xproj(i, d):
                pe.wait_ge(xs_ready, i * 2 + d + 1)
                if d:
                    pe.wait_ge(dtin_ready, i * 2 + 1)
                    pe.wait_ge(res_ready, i * 2 + 1)
                elif not is_first(i):
                    pe.wait_ge(ht_ready, i)
                    pe.wait_ge(open_ready, i + 1)
                else:
                    pe.wait_ge(xc_ready, 2)
                mm(psY[0:DTR, 0:N], w("xdt" + "fb"[d]), XZ[:, d, 0, :], start=True, stop=True)
                mm(psA[0:96, 0:N], w("xbc" + "fb"[d]), XZ[:, d, 0, :], start=True, stop=True).then_inc(bc_done, 1)

            def dtproj(i, d):
                pe.wait_ge(dtin_ready, i * 2 + 2)
                if d:
                    pe.wait_ge(dtm_ready, i * 2 + 1)
                mm(psY[:, 0:N], w("wdt" + "fb"[d])[0:DTR, :], dtin[:, d, :], start=True, stop=True).then_inc(dtp_done, 1)

            def broadcast(i, g, m, row):
                d = g // (QUARTERS // 2)
                if m == 0:
                    pe.wait_ge(bcs_ready, i * 2 + 2)
                if m >= 2:
                    pe.wait_ge(mul_done, i * MULS + m - 1)
                mm(AB[m % 2][:, 0:N], bcsel[:, row, :], bc[:, d, :], start=True, stop=True).then_inc(bb_done, 1)

            def input_(i, g, k):
                broadcast(i, g, 2 * QN * g + k, g % (QUARTERS // 2) * QN + k)

            def output(i, g, k):
                broadcast(i, g, 2 * QN * g + QN + k, NS + g % (QUARTERS // 2) * QN + k)

            def sum_(i, g):
                d, q = divmod(g, QUARTERS // 2)
                if q == 0:
                    pe.wait_ge(dt_ready, i * 2 + 2) if d == 0 else pe.wait_ge(ys_ready, i * 2 + 1)
                pe.wait_ge(summed, i * QUARTERS + g + 1)
                mm(psY[:, 0:N], c("ident"), hs[:, g % HBUF, 0, :], start=q == 0, stop=False).then_inc(acc_done, 1)
                if q == QUARTERS // 2 - 1:
                    mm(psY[:, 0:N], dskip[:, d, :], XZ[:, d, 0, :], start=False, stop=True).then_inc(y_done, 1)

            def leave(i):
                pe.wait_ge(xc_ready, i * 2 + 2)
                pe.sem_inc(pe_waited, 1)

            def merge(i):
                pe.wait_ge(ys_ready, i * 2 + 2)
                pe.wait_ge(h_kept, i + 1)
                for q in range(NC4):
                    at = slice(q * CT, (q + 1) * CT)
                    to = psY[0:CT, q * D:(q + 1) * D]
                    mm(to, HB[:, at], c("ident"), start=True, stop=False)
                    mm(to, YS[:, 0, at], w("woutf"), start=False, stop=False)
                    last = mm(to, YS[:, 1, at], w("woutb"), start=False, stop=True)
                last.then_inc(m_done, 1)

            def route(i):
                pe.wait_ge(ht_ready, i + 1)
                for q in range(NC4):
                    last = nc.tensor.transpose(psB[:, q * CT:(q + 1) * CT], HW[:, q, 0:D], c("ident")[0:CT, 0:CT])
                last.then_inc(ht_done, 1)
                pe.wait_ge(h2_ready, i + 1)
                for q in range(NC4):
                    last = mm(psA[0:CT, q * E:(q + 1) * E], h2[:, q * CT:(q + 1) * CT], w("route"), start=True, stop=True)
                last.then_inc(lg_done, 1)
                pe.wait_ge(sel_ready, i + 1)
                for q in range(NC4 + 1):
                    for p in range(min(q + 1, NC4)):
                        last = mm(psA[0:CT, q * E:(q + 1) * E], (before_h if p == q else ones_h)[0:CT, 0:CT], selh[:, p, :], start=p == 0, stop=p == min(q, NC4 - 1))
                last.then_inc(pos_done, 1)

            loop(pe, front_half, {
                "project": project, "xproj": xproj, "dtproj": dtproj, "input": input_, "output": output, "sum": sum_,
                "merge": merge, "leave": leave, "route": lambda i: while_open(pe, i, pe_waited, pe_read, route)})

            with pe.Fori(0, E // 4) as e:
                for b in range(2):
                    p = 2 * e + b + 1
                    pe.wait_ge(gathered[b], e * 64 + 64)
                    for k in range(4):
                        last = nc.tensor.transpose(psS[:, 0, k * D:(k + 1) * D], ex[b][:, k, 0:D], c("ident"))
                    last.then_inc(xt_done, 1)
                    pe.wait_ge(xt_ready, p)
                    pe.wait_ge(w_loaded[b], e * 32 + 32)
                    for h in range(2):
                        for k in range(2):
                            last = mm(psS[0:MD, 1 + k, h * CAP:(h + 1) * CAP], ew[b][:, h, k * MD:(k + 1) * MD], exT[:, h * CAP:(h + 1) * CAP], start=True, stop=True)
                    last.then_inc(e13_done, 1)
                    pe.wait_ge(e_act, p)
                    for k in range(4):
                        last = mm(psS[:, 3, k * D:(k + 1) * D], ea[:, k * 128:(k + 1) * 128], ew[b][0:MD, k // 2, D:2 * D], start=True, stop=True)
                    last.then_inc(e2_done, 1)


def kernel(**x):
    import numpy as np
    import concourse.bacc as _bacc
    from concourse import mybir as _mybir
    from concourse.bass_utils import run_bass_kernel_spmd as _run

    a = {k: np.asarray(q) for k, q in x.items()}
    f4 = np.float32
    g = IMG // PATCH
    pt = a["x"].reshape(STEPS, G, CH, g, PATCH, g, PATCH).transpose(0, 2, 4, 6, 1, 3, 5)
    pt = np.ascontiguousarray(pt.reshape(STEPS, KP, 128, G * NP).transpose(0, 2, 1, 3))

    wts = np.zeros((128, W_N), f4)

    def put(to, cols, name, value):
        at, n = cols[name]
        value = value.reshape(value.shape[0], -1)
        to[0:value.shape[0], at:at + value.shape[1]] = value

    t = "L0_tok_"
    put(wts, W_COLS, "conv", a[t + "conv_w"].reshape(D, KP, 128).transpose(2, 1, 0))
    for l in range(2):
        for m, n in enumerate("qkv"):
            put(wts, W_COLS, f"{n}{l}", a[t + f"qkv_{l}"][m * D:(m + 1) * D].T)
        wo = a[t + f"wo_{l}"].T.reshape(4, 2, HD, D)
        for p, s in enumerate("eo"):
            padded = np.zeros((4, 32, D), f4)
            padded[:, 0:HD] = wo[:, p]
            put(wts, W_COLS, f"wo{s}{l}", padded.reshape(128, D))
        put(wts, W_COLS, f"gate{l}", a[t + f"gate_{l}"].T)
        put(wts, W_COLS, f"up{l}", a[t + f"up_{l}"].T)
        down = np.zeros((FC * FW, D), f4)
        down[0:FF] = a[t + f"down_{l}"].T
        put(wts, W_COLS, f"down{l}", down.reshape(FC, FW, D).transpose(1, 0, 2))
    m = "L0_attn_"
    for s in "fb":
        put(wts, W_COLS, f"win{s}", a[m + f"W_in_{s}"])
        put(wts, W_COLS, f"xdt{s}", a[m + f"W_xproj_{s}"][:, 0:DTR])
        put(wts, W_COLS, f"xbc{s}", np.concatenate([a[m + f"W_xproj_{s}"][:, DTR:]] * 3, axis=1))
        put(wts, W_COLS, f"wdt{s}", a[m + f"W_dt_{s}"])
        put(wts, W_COLS, f"wout{s}", a[m + f"W_out_{s}"])
    put(wts, W_COLS, "route", a["L0_ffn_gate_w"].T)

    vec = np.zeros((128, V_N), f4)
    put(vec, V_COLS, "convb", a[t + "conv_b"][:, None])
    put(vec, V_COLS, "cls", a[t + "cls_token"].reshape(D, 1))
    put(vec, V_COLS, "pos", a[t + "pos_emb"].reshape(T, D).T)
    put(vec, V_COLS, "lnf", a[t + "ln_f"][:, None])
    for l in range(2):
        put(vec, V_COLS, f"ln1{l}", a[t + f"ln1_{l}"][:, None])
        put(vec, V_COLS, f"ln2{l}", a[t + f"ln2_{l}"][:, None])
    for s in "fb":
        put(vec, V_COLS, f"taps{s}", a[m + f"W_conv_{s}"])
        put(vec, V_COLS, f"bconv{s}", a[m + f"b_conv_{s}"][:, None])
        put(vec, V_COLS, f"bdt{s}", a[m + f"b_dt_{s}"][:, None])
        put(vec, V_COLS, f"alog{s}", a[m + f"A_log_{s}"])
        put(vec, V_COLS, f"dskip{s}", a[m + f"D_{s}"][:, None])

    cst = np.zeros((128, C_N), f4)
    p = np.arange(128)
    dsel = np.zeros((128, 128), f4)
    for j in range(4):
        dsel[32 * j + HD, 32 * j:32 * j + 32] = 1
    put(cst, C_COLS, "dsel", dsel)
    put(cst, C_COLS, "ident", np.eye(128, dtype=f4))
    put(cst, C_COLS, "mean", np.full((128, 128), 1 / D, f4))
    put(cst, C_COLS, "before", np.triu(np.ones((128, 128), f4), 1))
    put(cst, C_COLS, "ones", np.ones((128, 128), f4))
    put(cst, C_COLS, "slot1", np.tile(np.arange(E) * CAP + 1.0, (128, 1)))
    tok = np.arange(NC4)[None] * CT + p[:, None]
    put(cst, C_COLS, "tok0", tok)
    put(cst, C_COLS, "valid", tok < N)
    put(cst, C_COLS, "unused", TOK + (np.arange(SLOTS) % PAD).reshape(128, -1))
    put(cst, C_COLS, "part1", -1.0 * (p >= 32)[:, None])
    put(cst, C_COLS, "part2", -1.0 * (p >= 64)[:, None])
    put(cst, C_COLS, "heads", p[:, None] // HD == np.arange(HEADS)[None])
    put(cst, C_COLS, "groupbefore", np.tile(np.tril(np.ones((GR, GR)), -1).reshape(1, -1), (128, 1)))
    bcsel = np.zeros((96, 2 * NS, D), f4)
    for r in range(96):
        bcsel[r, r % 32] = 1

    w13 = np.concatenate([a["L0_ffn_w1"], a["L0_ffn_w3"]], axis=2)
    arrays = {"patches": pt, "weights": wts, "vectors": vec, "consts": cst, "bcsel": bcsel.reshape(96, -1),
              "gate_b": a["L0_ffn_gate_b"], "w13": w13, "w2": a["L0_ffn_w2"]}
    arrays = {k: np.ascontiguousarray(q) for k, q in arrays.items()}
    nc = _bacc.Bacc("TRN2", target_bir_lowering=False, num_devices=1)
    args = [nc.dram_tensor(k, q.shape, _mybir.dt.from_np(q.dtype), kind="ExternalInput").ap() for k, q in arrays.items()]
    out = nc.dram_tensor("out", (B, T, D), _mybir.dt.float32, kind="ExternalOutput").ap()
    vit_mamba_moe(nc, *args, out)
    r = _run(nc, [arrays], core_ids=[0])
    return r.results[0]["out"]
```
